# Optimizing a Trainium2 kernel written in Bass

```python
import numpy as np
import jax
import jax.numpy as jnp

def _softmax(x, axis=-1):
    return jax.nn.softmax(x, axis=axis)

def _gelu(x):
    return jax.nn.gelu(x, approximate=True)

def _silu(x):
    return jax.nn.silu(x)

def _sigmoid(x):
    return jax.nn.sigmoid(x)

def _layernorm(x, axis=-1, eps=1e-05):
    m = jnp.mean(x, axis=axis, keepdims=True)
    v = jnp.var(x, axis=axis, keepdims=True)
    return (x - m) / jnp.sqrt(v + eps)

def _scatter_add(tgt, idx, src, axis=0):
    return tgt.at[idx].add(src)

def _segment_sum(src, seg, n):
    return jax.ops.segment_sum(src, seg, n)
kernel_name = 'mk_adaln_d1_jaxref_r4_ecb777'

def setup_inputs(seed: int=0):
    np.random.seed(seed)
    _w = jnp.asarray

    def _L0_attn_setup():
        import jax, jax.numpy as jnp
        import numpy as np
        D = 256
        INNER = 384
        S = 16
        K = 3
        BATCH = 4
        L = 1024
        key = jax.random.key(seed)
        ks = jax.random.split(key, 8)
        x = jax.random.normal(ks[0], (BATCH, L, D), jnp.float32)
        ln_w = jnp.ones((D,), jnp.float32)
        ln_b = jnp.zeros((D,), jnp.float32)
        W_in = (jax.random.normal(ks[1], (D, 2 * INNER), jnp.float32) / np.sqrt(D)).astype(jnp.float32)
        conv_w = (jax.random.normal(ks[2], (INNER, K), jnp.float32) * 0.3).astype(jnp.float32)
        A = (-0.5 * jnp.eye(S) + 0.02 * jax.random.normal(ks[3], (S, S), jnp.float32)).astype(jnp.float32)
        Bm = (jax.random.normal(ks[4], (S, INNER), jnp.float32) / np.sqrt(INNER)).astype(jnp.float32)
        Cm = (jax.random.normal(ks[5], (INNER, S), jnp.float32) / np.sqrt(INNER)).astype(jnp.float32)
        W_out = (jax.random.normal(ks[6], (INNER, D), jnp.float32) / np.sqrt(INNER)).astype(jnp.float32)
        return dict(x=x, ln_w=ln_w, ln_b=ln_b, W_in=W_in, conv_w=conv_w, A=A, Bm=Bm, Cm=Cm, W_out=W_out)
    _L0_attn_in = _L0_attn_setup()

    def _L0_ffn_setup():
        import jax, jax.numpy as jnp
        import numpy as np
        B, T, C, H, E, MIN_E = (4, 512, 256, 128, 16, 2)
        IS_CAUSAL = False

        def _forward(hidden_states, sim_matrix, gates, q_proj, k_proj, v_proj, o_proj):
            b, t, c = hidden_states.shape
            n = b * t
            x = hidden_states.reshape(n, c)
            xn = x / jnp.maximum(jnp.linalg.norm(x, axis=-1, keepdims=True), 1e-12)
            sn = sim_matrix / jnp.maximum(jnp.linalg.norm(sim_matrix, axis=0, keepdims=True), 1e-12)
            logits = xn @ sn - jax.nn.sigmoid(gates)
            gated = jax.nn.relu(logits)
            hard = (gated > 0).astype(gated.dtype)
            mask = gated + jax.lax.stop_gradient(hard - gated)
            inactive = jnp.sum(hard, axis=1) == 0
            _, fb_idx = jax.lax.top_k(logits, MIN_E)
            fb = jnp.zeros((n, logits.shape[1]), gated.dtype).at[jnp.arange(n)[:, None], fb_idx].set(1.0)
            put = jax.lax.stop_gradient(inactive[:, None].astype(gated.dtype) * fb)
            mask = mask * (1.0 - put) + put
            masked = jnp.where(mask > 0, gated, -jnp.inf)
            w = jax.nn.softmax(masked, axis=-1)

            def moe_proj(p):
                y = jnp.einsum('nc,ech->neh', x, p)
                return jnp.einsum('ne,neh->nh', w, y)
            q = moe_proj(q_proj).reshape(b, t, -1)
            k = moe_proj(k_proj).reshape(b, t, -1)
            v = moe_proj(v_proj).reshape(b, t, -1)
            h = q.shape[-1]
            scores = jnp.einsum('bth,bsh->bts', q, k) / jnp.sqrt(jnp.asarray(h, q.dtype))
            if IS_CAUSAL and t > 1:
                causal = jnp.tril(jnp.ones((t, t), bool))
                scores = jnp.where(causal[None], scores, -jnp.inf)
            attn = jax.nn.softmax(scores, axis=-1)
            o = jnp.einsum('bts,bsh->bth', attn, v).reshape(n, h)
            z = jnp.einsum('ne,nh->enh', w, o)
            out = jnp.einsum('enh,ehc->nc', z, o_proj)
            return out.reshape(b, t, c)
        key = jax.random.key(seed)
        ks = jax.random.split(key, 6)
        lim_qkv = float(np.sqrt(6.0 / (C + H)))
        inp = {'hidden_states': jax.random.normal(ks[0], (B, T, C), jnp.float32), 'sim_matrix': jax.random.normal(ks[1], (C, E), jnp.float32), 'gates': jnp.zeros((E,), jnp.float32), 'q_proj': jax.random.uniform(ks[2], (E, C, H), jnp.float32, -lim_qkv, lim_qkv), 'k_proj': jax.random.uniform(ks[3], (E, C, H), jnp.float32, -lim_qkv, lim_qkv), 'v_proj': jax.random.uniform(ks[4], (E, C, H), jnp.float32, -lim_qkv, lim_qkv), 'o_proj': jax.random.uniform(ks[5], (E, H, C), jnp.float32, -lim_qkv, lim_qkv)}
        return inp
    _L0_ffn_in = _L0_ffn_setup()
    _L0_c = _w((lambda *s: np.random.randn(*s).astype(np.float32) * 0.05)(1, 256))
    _L0_wmod = _w((lambda *s: np.random.randn(*s).astype(np.float32) * 0.05)(256, 6 * 256) * 256 ** (-0.5))
    _d = {'L0_attn_x': _L0_attn_in['x'], 'L0_attn_ln_w': _L0_attn_in['ln_w'], 'L0_attn_ln_b': _L0_attn_in['ln_b'], 'L0_attn_W_in': _L0_attn_in['W_in'], 'L0_attn_conv_w': _L0_attn_in['conv_w'], 'L0_attn_A': _L0_attn_in['A'], 'L0_attn_Bm': _L0_attn_in['Bm'], 'L0_attn_Cm': _L0_attn_in['Cm'], 'L0_attn_W_out': _L0_attn_in['W_out'], 'L0_ffn_sim_matrix': _L0_ffn_in['sim_matrix'], 'L0_ffn_gates': _L0_ffn_in['gates'], 'L0_ffn_q_proj': _L0_ffn_in['q_proj'], 'L0_ffn_k_proj': _L0_ffn_in['k_proj'], 'L0_ffn_v_proj': _L0_ffn_in['v_proj'], 'L0_ffn_o_proj': _L0_ffn_in['o_proj'], 'L0_c': _L0_c, 'L0_wmod': _L0_wmod}
    _x0 = _d['L0_attn_x']
    _d['L0_attn_x'] = jax.random.normal(jax.random.fold_in(jax.random.key(seed), 1), (1, 4096, 256), dtype=_x0.dtype)
    del _x0
    return _d

def reference(L0_attn_x, L0_attn_ln_w, L0_attn_ln_b, L0_attn_W_in, L0_attn_conv_w, L0_attn_A, L0_attn_Bm, L0_attn_Cm, L0_attn_W_out, L0_ffn_sim_matrix, L0_ffn_gates, L0_ffn_q_proj, L0_ffn_k_proj, L0_ffn_v_proj, L0_ffn_o_proj, L0_c, L0_wmod):

    def _L0_attn_ref(x, ln_w, ln_b, W_in, conv_w, A, Bm, Cm, W_out):
        import jax, jax.numpy as jnp
        import numpy as np
        D = 256
        INNER = 384
        S = 16
        K = 3
        BATCH = 4
        L = 1024
        seq = x.shape[1]
        mu = x.mean(-1, keepdims=True)
        var = ((x - mu) ** 2).mean(-1, keepdims=True)
        h = (x - mu) * jax.lax.rsqrt(var + 1e-05) * ln_w + ln_b
        proj = h @ W_in
        data, gate = (proj[..., :INNER], proj[..., INNER:])
        xp = jnp.pad(data, ((0, 0), (K - 1, 0), (0, 0)))
        conv = sum((xp[:, j:j + seq, :] * conv_w[:, j] for j in range(K)))
        u = jax.nn.silu(conv)
        M = jnp.eye(S, dtype=x.dtype) + A.T
        Bu = jnp.einsum('bti,si->tbs', u, Bm)

        def step(state, bu_t):
            s = state @ M + bu_t
            return (s, s)
        init = jnp.zeros((x.shape[0], S), x.dtype)
        _, states = jax.lax.scan(step, init, Bu)
        y = jnp.einsum('tbs,is->bti', states, Cm)
        out = jax.nn.sigmoid(gate) * y @ W_out
        return x + out

    def _L0_ffn_ref(hidden_states, sim_matrix, gates, q_proj, k_proj, v_proj, o_proj):
        import jax, jax.numpy as jnp
        import numpy as np
        B, T, C, H, E, MIN_E = (4, 512, 256, 128, 16, 2)
        IS_CAUSAL = False

        def _forward(hidden_states, sim_matrix, gates, q_proj, k_proj, v_proj, o_proj):
            b, t, c = hidden_states.shape
            n = b * t
            x = hidden_states.reshape(n, c)
            xn = x / jnp.maximum(jnp.linalg.norm(x, axis=-1, keepdims=True), 1e-12)
            sn = sim_matrix / jnp.maximum(jnp.linalg.norm(sim_matrix, axis=0, keepdims=True), 1e-12)
            logits = xn @ sn - jax.nn.sigmoid(gates)
            gated = jax.nn.relu(logits)
            hard = (gated > 0).astype(gated.dtype)
            mask = gated + jax.lax.stop_gradient(hard - gated)
            inactive = jnp.sum(hard, axis=1) == 0
            _, fb_idx = jax.lax.top_k(logits, MIN_E)
            fb = jnp.zeros((n, logits.shape[1]), gated.dtype).at[jnp.arange(n)[:, None], fb_idx].set(1.0)
            put = jax.lax.stop_gradient(inactive[:, None].astype(gated.dtype) * fb)
            mask = mask * (1.0 - put) + put
            masked = jnp.where(mask > 0, gated, -jnp.inf)
            w = jax.nn.softmax(masked, axis=-1)

            def moe_proj(p):
                y = jnp.einsum('nc,ech->neh', x, p)
                return jnp.einsum('ne,neh->nh', w, y)
            q = moe_proj(q_proj).reshape(b, t, -1)
            k = moe_proj(k_proj).reshape(b, t, -1)
            v = moe_proj(v_proj).reshape(b, t, -1)
            h = q.shape[-1]
            scores = jnp.einsum('bth,bsh->bts', q, k) / jnp.sqrt(jnp.asarray(h, q.dtype))
            if IS_CAUSAL and t > 1:
                causal = jnp.tril(jnp.ones((t, t), bool))
                scores = jnp.where(causal[None], scores, -jnp.inf)
            attn = jax.nn.softmax(scores, axis=-1)
            o = jnp.einsum('bts,bsh->bth', attn, v).reshape(n, h)
            z = jnp.einsum('ne,nh->enh', w, o)
            out = jnp.einsum('enh,ehc->nc', z, o_proj)
            return out.reshape(b, t, c)
        return _forward(hidden_states, sim_matrix, gates, q_proj, k_proj, v_proj, o_proj)
    x = L0_attn_x
    mod = (_silu(L0_c) @ L0_wmod).reshape(L0_c.shape[0], 6, 1, -1)
    sa, ca, ga, sb, cb, gb = (mod[:, 0], mod[:, 1], mod[:, 2], mod[:, 3], mod[:, 4], mod[:, 5])
    ga = (2 * (ga >= 0) - 1) * jnp.maximum(jnp.abs(ga), 0.25)
    gb = (2 * (gb >= 0) - 1) * jnp.maximum(jnp.abs(gb), 0.25)
    h = _layernorm(x, axis=-1) * (1 + ca) + sa
    x = x + ga * _L0_attn_ref(h, L0_attn_ln_w, L0_attn_ln_b, L0_attn_W_in, L0_attn_conv_w, L0_attn_A, L0_attn_Bm, L0_attn_Cm, L0_attn_W_out)
    h = _layernorm(x, axis=-1) * (1 + cb) + sb
    x = x + gb * _L0_ffn_ref(h, L0_ffn_sim_matrix, L0_ffn_gates, L0_ffn_q_proj, L0_ffn_k_proj, L0_ffn_v_proj, L0_ffn_o_proj)
    return x

_drawn_inputs = setup_inputs


def setup_inputs(seed=0):
    import zlib

    import numpy as np

    out = dict(_drawn_inputs(seed))
    spreads = {'L0_attn_ln_w': (1.0, 0.6), 'L0_attn_ln_b': (0.0, 0.8), 'L0_ffn_gates': (0.0, 0.8)}
    factors = {'L0_attn_W_in': 5.616,
     'L0_attn_conv_w': 5.661,
     'L0_attn_Bm': 4.931,
     'L0_attn_Cm': 4.936,
     'L0_attn_W_out': 4.845,
     'L0_ffn_sim_matrix': 8.0,
     'L0_ffn_q_proj': 8.0,
     'L0_ffn_k_proj': 8.0,
     'L0_ffn_v_proj': 8.0,
     'L0_ffn_o_proj': 8.0}
    for name, (base, spread) in spreads.items():
        noise = np.random.default_rng([zlib.crc32(name.encode()), seed]).standard_normal(out[name].shape)
        drawn = base * np.exp(spread * noise) if base else spread * noise
        out[name] = jnp.asarray(drawn.astype(out[name].dtype))
    for name, factor in factors.items():
        out[name] = (out[name] * factor).astype(out[name].dtype)
    return out
```

```python
from contextlib import ExitStack

import concourse.bass as bass
from concourse import mybir

F32 = mybir.dt.float32
F32R = mybir.dt.float32r
ALU = mybir.AluOpType
ACT = mybir.ActivationFunctionType
AX_X = mybir.AxisListType.X


def adaln_block_kernel(nc, x, ln_w, ln_b, w_in, conv_w, a_mat, a_mat_t, bm_t, cm_t, w_out,
                       sim, gates, q_proj, k_proj, v_proj, o_proj, cond, wmod, out):
    P = 128
    N, C = x.shape
    KC = C // P
    INNER = w_in.shape[1] // 2
    FI = INNER // P
    S = a_mat.shape[0]
    TAPS = conv_w.shape[1]
    E, _, H = q_proj.shape
    BT = 512
    TT = BT // P
    NB = N // BT
    NT = N // P
    KG = N // BT
    H3 = 3 * H
    SCALE = float(H) ** -0.5
    SCAN = N.bit_length() - 1
    assert NB * S == P and NB % 2 == 0 and NB >= 4 and FI == 3 and KC == 2 and TT == 4 and E == 16
    assert H == P

    r_dram = nc.dram_tensor("residual_scratch", (N, C), F32).ap()
    x2_dram = nc.dram_tensor("x2_scratch", (N, C), F32).ap()
    gate_dram = nc.dram_tensor("gate_scratch", (P, FI, N), F32).ap()
    bu_dram = nc.dram_tensor("bu_scratch", (P, BT), F32).ap()
    st_dram = nc.dram_tensor("state_scratch", (P, BT), F32).ap()

    def tok_view(ap):
        return ap.rearrange("(n p) c -> p n c", p=P)

    def upto(i, p, per, k=0):
        return i * (2 * per) + (p * per + k)

    def wait(eng, sem, value):
        if not isinstance(value, int) or value > 0:
            eng.wait_ge(sem, value)

    class Link:

        def __init__(self, eng, sem, per):
            self.eng, self.sem, self.per, self.n, self.base = eng, sem, per, 0, 0

        def block(self, i, p):
            assert self.n in (0, self.per), (self.sem, self.n)
            self.n, self.base = 0, upto(i, p, self.per)

        def done(self, ins):
            ins.then_inc(self.sem, 1)
            self.n += 1

        def wait(self):
            self.eng.wait_ge(self.sem, self.base + self.n)

    def slots(eng, body):
        body(0, 0, False)
        body(0, 1, False)
        with eng.Fori(1, NB // 2 - 1) as i:
            body(i, 0, False)
            body(i, 1, False)
        body(NB // 2 - 1, 0, False)
        body(NB // 2 - 1, 1, True)

    def following(i, p):
        return (i, 1) if p == 0 else (i + 1, 0)

    nc.disable_value_cache = True

    with ExitStack() as whole:
        def alloc(stack):
            def sb(name, shape, dt=F32):
                return stack.enter_context(nc.sbuf_tensor(name, shape, dt))
            return sb

        def sem(name):
            return whole.enter_context(nc.semaphore(name))

        sb = alloc(whole)
        ident = sb("ident", [P, P])
        ones_f = sb("ones_f", [P, P])
        ones_r = sb("ones_r", [1, P], F32R)
        minus_half = sb("minus_half", [P, S])
        eps = sb("eps", [P, TT])
        modv = sb("modv", [P, 6, C])
        w_all = sb("w_all", [P, NT, E])
        q_t = sb("q_t", [P, N])
        k_t = sb("k_t", [P, N])
        v_all = sb("v_all", [P, NT, H])
        ps = whole.enter_context(nc.psum_tensor("ps", [P, 8, 512], F32))

        mid = whole.enter_context(ExitStack())
        sb = alloc(mid)
        sn = sb("sn", [P, KC, E])
        sig_gates = sb("sig_gates", [P, E])
        rank = sb("rank", [P, TT, E])
        w_hi = sb("w_hi", [P, KC, E, 3, H], F32R)
        w_lo = sb("w_lo", [P, KC, E, 3, H], F32R)

        one = mid.enter_context(ExitStack())
        sb = alloc(one)
        c_col = sb("c_col", [P, KC])
        c_sig = sb("c_sig", [P, KC])
        c_bc = sb("c_bc", [P, KC, P])
        lnw = sb("lnw", [P, KC])
        lnb = sb("lnb", [P, KC])
        cw = sb("cw", [P, FI, TAPS])
        simt = sb("simt", [P, KC, E])
        sim_sq = sb("sim_sq", [P, KC, E])
        col_inv = sb("col_inv", [P, E])
        g_tmp = w_all[:].rearrange("p n e -> p (n e)").rearrange("p (g c) -> p g c", g=2)
        win_hi = sb("win_hi", [P, KC, 2 * INNER], F32R)
        win_lo = sb("win_lo", [P, KC, 2 * INNER], F32R)
        bmt = sb("bmt", [P, FI, S])
        pad = 4 * S
        free_q, free_k, free_v = q_t[:], k_t[:], v_all[:].rearrange("p n h -> p (n h)")
        powers = free_k[:, 0:SCAN * (pad + 2 * P)].rearrange("p (k n) -> p k n", k=SCAN)
        gate = free_q[:, 0:FI * BT].rearrange("p (f n) -> p f n", f=FI)
        win = free_q[:, 0:FI * BT].rearrange("p (k n) -> p k n", k=KC)
        n2 = free_q[:, FI * BT:FI * BT + TT * C].rearrange("p (t c) -> p t c", t=TT)
        ht = free_q[:, FI * BT + TT * C:FI * BT + TT * C + KC * BT].rearrange("p (k n) -> p k n", k=KC)
        bu = free_q[0:S, N - BT:N]
        cv = free_v[:, 0:FI * BT].rearrange("p (f n) -> p f n", f=FI)
        sg = free_v[:, FI * BT:2 * FI * BT].rearrange("p (f n) -> p f n", f=FI)
        h_b = free_v[:, 2 * FI * BT:2 * FI * BT + TT * C].rearrange("p (t c) -> p t c", t=TT)
        assert FI * BT == KC * 2 * INNER and FI * BT + TT * C + KC * BT + BT <= N
        wmod_ld = sb("wmod_ld", [P, KC, 6 * C])
        scan_s = [wmod_ld[:, 0, 0:BT], wmod_ld[:, 1, 0:BT]]
        wstage = wmod_ld[:].rearrange("p s (k e t h) -> p s k e t h", k=KC, e=E // NB, t=3)
        xt = sb("xt", [P, 2, TT, C])
        h_a = sb("h_a", [P, TT, C])
        hb = [h_a[:], h_b]
        bst = sb("bst", [P, TT, 6])
        small = sb("small", [P, 2 * TT * 4])
        mv = small[:, 0:2 * TT * 2].rearrange("p (n t v) -> p n t v", n=2, v=2)
        var_eps = small[:, 2 * TT * 2:2 * TT * 3].rearrange("p (n t) -> p n t", n=2)
        rs = small[:, 2 * TT * 3:2 * TT * 4].rearrange("p (n t) -> p n t", n=2)
        ht_hi = sb("ht_hi", [P, KC, BT], F32R)
        ht_lo = sb("ht_lo", [P, KC, BT], F32R)
        data = sb("data", [P, FI, BT + TAPS - 1])

        carriers = sem("carriers")
        params_in = sem("params_in")
        zeroed = sem("zeroed")
        a_in = sem("a_in")
        x_in = [sem("x_in0"), sem("x_in1")]
        r_out = [sem("r_out0"), sem("r_out1")]
        w_in_sem = [sem("w_in0"), sem("w_in1")]
        gate_out = sem("gate_out")
        bu_out = sem("bu_out")
        pool_const = sem("pool_const")
        pre_act = sem("pre_act")
        pre_dve = sem("pre_dve")
        pre_pool = sem("pre_pool")
        mod_mm = sem("mod_mm")
        mod_ready = sem("mod_ready")
        win_split = sem("win_split")
        colnorm_mm = sem("colnorm_mm")
        col_ss = sem("col_ss")
        conv_link = sem("conv_link")
        halo_ready = sem("halo_ready")
        pow_mm = sem("pow_mm")
        pow_ready = sem("pow_ready")
        dve_a = sem("dve_a")
        pool_a = sem("pool_a")
        mv_ready = sem("mv_ready")
        rs_ready = sem("rs_ready")
        h_ready = sem("h_ready")
        n2_ready = sem("n2_ready")
        n2_transposed = sem("n2_transposed")
        ht_ready = sem("ht_ready")
        ht_lo_ready = sem("ht_lo_ready")
        proj_mm = sem("proj_mm")
        proj_evac = sem("proj_evac")
        conv_ready = sem("conv_ready")
        csig_ready = sem("csig_ready")
        u_ready = sem("u_ready")
        r_ready = sem("r_ready")
        bu_mm = sem("bu_mm")
        bu_ready = sem("bu_ready")
        whi_ready = sem("whi_ready")
        wlo_ready = sem("wlo_ready")
        scan_in = sem("scan_in")
        scan_mm = sem("scan_mm")
        scan_add = sem("scan_add")
        st_out = sem("st_out")

        T_BANK, P_BANK, BU_BANK, MISC = 0, 2, 6, 7
        N_PARAMS = 9
        DVE_A, POOL_A = 5, 3
        EB = E // NB

        def apart(eng):
            eng.sem_inc(carriers, 1)

        def pw_m(k, shift=0):
            return powers[:, k, pad - S * shift:pad - S * shift + P]

        with nc.Block() as block:
            @block.sync
            def _(sp):
                xv, rv = tok_view(x), tok_view(r_dram)
                for p in range(2):
                    sp.dma_start(xt[:, p], xv[:, p * TT:(p + 1) * TT, :]).then_inc(x_in[p], 16)
                params = [
                    (c_col[:], cond),
                    (wmod_ld[:], wmod.rearrange("(k p) n -> p k n", p=P)),
                    (lnw[:], ln_w),
                    (lnb[:], ln_b),
                    (win, w_in.rearrange("(k p) n -> p k n", p=P)),
                    (simt[:], sim.rearrange("(k p) e -> p k e", p=P)),
                    (sig_gates[:], gates.rearrange("(a e) -> a e", a=1).to_broadcast([P, E])),
                    (cw[:], conv_w.rearrange("(f p) j -> p f j", p=P)),
                    (bmt[:], bm_t.rearrange("(f p) s -> p f s", p=P)),
                ]
                assert len(params) == N_PARAMS
                for dst, src in params:
                    sp.dma_start(dst, src).then_inc(params_in, 16)
                sp.wait_ge(zeroed, 1)
                for g in range(NB):
                    rows = slice(S * g, S * g + S)
                    sp.dma_start(powers[rows, 0, pad + S * g:pad + S * g + S], a_mat_t).then_inc(a_in, 16)
                    sp.dma_start(powers[rows, 0, pad + P + S * g:pad + P + S * g + S], a_mat).then_inc(a_in, 16)

                def load_w(i, p):
                    for t, proj in enumerate((q_proj, k_proj, v_proj)):
                        e0 = i * (2 * EB) + EB * p
                        for k in range(KC):
                            sp.dma_start(wstage[:, p, k, :, t],
                                         proj[bass.ds(e0, EB), k * P:(k + 1) * P, :].rearrange("e c h -> c e h")
                                         ).then_inc(w_in_sem[p], 16)

                sp.wait_ge(mod_mm, 1)
                load_w(0, 0)
                load_w(0, 1)

                def slot(i, p, last, reload):
                    sp.wait_ge(r_ready, upto(i, p, 1, 1))
                    sp.dma_start(rv[:, bass.ds(i * (2 * TT) + p * TT, TT), :], xt[:, p]).then_inc(r_out[p], 16)
                    if reload:
                        sp.wait_ge(r_out[p], i * 16 + 16)
                        sp.dma_start(xt[:, p], xv[:, bass.ds(i * (2 * TT) + (p + 2) * TT, TT), :]
                                     ).then_inc(x_in[p], 16)
                        sp.wait_ge(whi_ready, upto(i, p, 1, 1))
                        sp.wait_ge(wlo_ready, upto(i, p, 1, 1))
                        load_w(i + 1, p)

                with sp.Fori(0, NB // 2 - 1) as i:
                    slot(i, 0, False, True)
                    slot(i, 1, False, True)
                slot(NB // 2 - 1, 0, False, False)
                slot(NB // 2 - 1, 1, True, False)
                sp.wait_ge(bu_out, 16 * NB)
                sp.wait_ge(wlo_ready, NB)
                sp.wait_ge(whi_ready, NB)
                sp.dma_start(scan_s[0], bu_dram).then_inc(scan_in, 16)
                sp.wait_ge(scan_add, SCAN)
                sp.dma_start(st_dram, scan_s[SCAN % 2]).then_inc(st_out, 16)
                sp.wait_ge(st_out, 16)
                for p in range(2):
                    sp.wait_ge(r_out[p], 16 * (NB // 2))
                sp.wait_ge(gate_out, 16 * NB)

            @block.gpsimd
            def _(pool):
                nc.gpsimd.memset(powers, 0.0).then_inc(zeroed, 1)
                nc.gpsimd.memset(minus_half[:], -0.5)
                nc.gpsimd.memset(eps[:], 1e-5)
                nc.gpsimd.memset(data[:, :, 0:TAPS - 1], 0.0)
                nc.gpsimd.memset(ones_f[:], 1.0).then_inc(pool_const, 1)
                pool.wait_ge(pool_const, 1)
                nc.gpsimd.affine_select(out=ident[:], in_=ones_f[:], compare_op=ALU.is_equal, fill=0.0, base=0,
                                        pattern=[[1, P]], channel_multiplier=-1).then_inc(pool_const, 1)
                for e in range(E):
                    ins = nc.gpsimd.memset(rank[:, :, e], float(E - e))
                ins.then_inc(pool_const, 1)
                pool.wait_ge(col_ss, 1)
                nc.gpsimd.tensor_tensor(col_inv[:], col_inv[:], minus_half[:], ALU.pow).then_inc(pre_pool, 1)
                link = Link(pool, pool_a, POOL_A)

                def inv_std(i, p, n):
                    pool.wait_ge(mv_ready, upto(i, p, 2, n + 1))
                    link.done(nc.gpsimd.tensor_tensor(var_eps[:, n], mv[:, n, :, 1], eps[:], ALU.add))
                    link.wait()
                    nc.gpsimd.tensor_tensor(rs[:, n], var_eps[:, n], minus_half[:, 0:TT], ALU.pow
                                            ).then_inc(rs_ready, 1)

                def norm_help(i, p):
                    link.block(i, p)
                    inv_std(i, p, 0)
                    inv_std(i, p, 1)
                    pool.wait_ge(ht_ready, upto(i, p, 1, 1))
                    nc.gpsimd.tensor_tensor(ht_lo[:], ht, ht_hi[:].bitcast(F32), ALU.subtract
                                            ).then_inc(ht_lo_ready, 1)

                def residual(i, p):
                    pool.wait_ge(n2_ready, upto(i, p, 1, 1))
                    ga = modv[:, 2:3, :].to_broadcast([P, TT, C])
                    link.done(nc.gpsimd.tensor_tensor(hb[p], hb[p], ga, ALU.mult))
                    link.wait()
                    nc.gpsimd.tensor_tensor(xt[:, p], xt[:, p], hb[p], ALU.add).then_inc(r_ready, 1)

                norm_help(0, 0)
                residual(0, 0)

                def slot(i, p, last):
                    if not last:
                        norm_help(*following(i, p))
                    pool.wait_ge(csig_ready, upto(i, p, 1, 1))
                    nc.gpsimd.tensor_tensor(sg, sg, cv, ALU.mult).then_inc(u_ready, 1)
                    pool.wait_ge(whi_ready, upto(i, p, 1, 1))
                    for k in range(KC):
                        e0 = i * (2 * EB) + EB * p
                        ins = nc.gpsimd.tensor_tensor(
                            w_lo[:, k, bass.ds(e0, EB)], wstage[:, p, k],
                            w_hi[:, k, bass.ds(e0, EB)].bitcast(F32), ALU.subtract)
                    ins.then_inc(wlo_ready, 1)
                    if not last:
                        residual(*following(i, p))

                slots(pool, slot)

            @block.scalar
            def _(act):
                act.wait_ge(params_in, 16 * N_PARAMS)
                nc.scalar.activation(c_sig[:], c_col[:], ACT.Sigmoid).then_inc(pre_act, 1)
                nc.scalar.activation(sig_gates[:], sig_gates[:], ACT.Sigmoid)
                nc.scalar.copy(win_hi[:], win).then_inc(pre_act, 1)
                act.wait_ge(pool_const, 1)
                nc.scalar.copy(ones_r[:], ones_f[0:1, :])

                def hidden(i, p):
                    act.wait_ge(n2_transposed, upto(i, p, 1, 1))
                    for k in range(KC):
                        nc.scalar.activation(ht[:, k], ps[:, T_BANK + k, :], ACT.Identity,
                                             bias=lnb[:, k:k + 1], scale=lnw[:, k:k + 1])
                        ins = nc.scalar.activation(ht_hi[:, k], ps[:, T_BANK + k, :], ACT.Identity,
                                                   bias=lnb[:, k:k + 1], scale=lnw[:, k:k + 1])
                    ins.then_inc(ht_ready, 1)

                def project_out(i, p, first=False):
                    wait(act, conv_ready, upto(i, p, 1, 0))
                    if not first:
                        nc.scalar.copy(data[:, :, 0:TAPS - 1], data[:, :, BT:BT + TAPS - 1]).then_inc(halo_ready, 1)
                        act.wait_ge(halo_ready, upto(i, p, 1, 0))
                    for f in range(2 * FI):
                        act.wait_ge(proj_mm, upto(i, p, 2 * FI, f + 1))
                        src = ps[:, P_BANK + (2 * FI * p + f) % 4, :]
                        if f < FI:
                            nc.scalar.copy(data[:, f, TAPS - 1:], src).then_inc(proj_evac, 1)
                        else:
                            if f == FI:
                                wait(act, gate_out, upto(i, p, 16, 0))
                            nc.scalar.activation(gate[:, f - FI], src, ACT.Sigmoid).then_inc(proj_evac, 1)
                    act.wait_ge(proj_evac, upto(i, p, 2 * FI, 2 * FI))
                    act.dma_start(gate_dram[:, :, bass.ds(i * (2 * BT) + p * BT, BT)], gate
                                  ).then_inc(gate_out, 16)

                act.wait_ge(pool_const, 2)
                hidden(0, 0)
                project_out(0, 0, first=True)

                def slot(i, p, last):
                    act.wait_ge(w_in_sem[p], i * (16 * 3 * KC) + 16 * 3 * KC)
                    for k in range(KC):
                        ins = nc.scalar.copy(w_hi[:, k, bass.ds(i * (2 * EB) + EB * p, EB)], wstage[:, p, k])
                    ins.then_inc(whi_ready, 1)
                    if not last:
                        hidden(*following(i, p))
                    act.wait_ge(conv_ready, upto(i, p, 1, 1))
                    wait(act, bu_mm, upto(i, p, 1, 0))
                    nc.scalar.activation(sg, cv, ACT.Sigmoid).then_inc(csig_ready, 1)
                    if not last:
                        project_out(*following(i, p))
                    act.wait_ge(bu_mm, upto(i, p, 1, 1))
                    wait(act, bu_out, upto(i, p, 16, 0))
                    nc.scalar.copy(bu, ps[0:S, BU_BANK, :]).then_inc(bu_ready, 1)
                    act.wait_ge(bu_ready, upto(i, p, 1, 1))
                    act.dma_start(bu_dram[bass.ds(i * (2 * S) + p * S, S), :], bu).then_inc(bu_out, 16)

                slots(act, slot)

            @block.vector
            def _(dve):
                pre = Link(dve, pre_dve, 0)
                dve.wait_ge(params_in, 16 * N_PARAMS)
                dve.wait_ge(pre_act, 1)
                pre.done(nc.vector.tensor_tensor(c_sig[:], c_sig[:], c_col[:], ALU.mult))
                pre.wait()
                for k in range(KC):
                    ins = nc.vector.tensor_copy(c_bc[:, k, :], c_sig[:, k:k + 1].to_broadcast([P, P]))
                pre.done(ins)
                pre.done(nc.vector.tensor_tensor(sim_sq[:], simt[:], simt[:], ALU.mult))
                dve.wait_ge(pre_act, 2)
                nc.vector.tensor_tensor(win_lo[:], win, win_hi[:].bitcast(F32), ALU.subtract
                                        ).then_inc(win_split, 1)
                dve.wait_ge(a_in, 16 * 2 * NB)
                dve.wait_ge(pool_const, 2)
                for n in range(2):
                    blk = powers[:, 0, pad + n * P:pad + (n + 1) * P]
                    ins = nc.vector.tensor_tensor(blk, blk, ident[:], ALU.add)
                ins.then_inc(pow_ready, 1)
                dve.wait_ge(mod_mm, 1)
                mod_ps = ps[:, T_BANK:T_BANK + 3, :].rearrange("p b (h n) -> p (b h) n", h=2)
                nc.vector.tensor_copy(modv[:, 0], mod_ps[:, 0])
                nc.vector.tensor_scalar(modv[:, 1], mod_ps[:, 1], 1.0, None, ALU.add)
                nc.vector.tensor_copy(modv[:, 3], mod_ps[:, 3])
                nc.vector.tensor_scalar(modv[:, 4], mod_ps[:, 4], 1.0, None, ALU.add)
                for n, g in enumerate((2, 5)):
                    nc.vector.tensor_copy(modv[:, g], mod_ps[:, g])
                    ins = nc.vector.tensor_scalar(g_tmp[:, n], mod_ps[:, g], 0.0, 2.0, ALU.is_ge, ALU.mult)
                pre.done(ins)
                pre.wait()
                for n, g in enumerate((2, 5)):
                    nc.vector.scalar_tensor_tensor(out=modv[:, g], in0=modv[:, g], scalar=-1.0,
                                                   in1=modv[:, g], op0=ALU.mult, op1=ALU.max)
                    ins = nc.vector.tensor_scalar(g_tmp[:, n], g_tmp[:, n], -1.0, None, ALU.add)
                pre.done(ins)
                pre.wait()
                for n, g in enumerate((2, 5)):
                    ins = nc.vector.scalar_tensor_tensor(out=modv[:, g], in0=modv[:, g], scalar=0.25,
                                                         in1=g_tmp[:, n], op0=ALU.max, op1=ALU.mult)
                ins.then_inc(mod_ready, 1)
                dve.wait_ge(colnorm_mm, 1)
                nc.vector.tensor_scalar(col_inv[:], ps[:, MISC, 0:E], 1e-24, None, ALU.max).then_inc(col_ss, 1)
                dve.wait_ge(mod_ready, 1)
                link = Link(dve, dve_a, DVE_A)

                def stats(src, n):
                    for t in range(TT):
                        ins = nc.vector.bn_stats(bst[:, t], src[:, t])
                    link.done(ins)
                    link.wait()
                    apart(dve)
                    for t in range(TT):
                        ins = nc.vector.bn_aggr(mv[:, n, t], bst[:, t])
                    ins.then_inc(mv_ready, 1)

                def normalize(dst, src, n):
                    for t in range(TT):
                        ins = nc.vector.tensor_scalar(dst[:, t], src[:, t], mv[:, n, t, 0:1], rs[:, n, t:t + 1],
                                                      ALU.subtract, ALU.mult)
                    return ins

                def norms(i, p):
                    link.block(i, p)
                    dve.wait_ge(x_in[p], i * 16 + 16)
                    stats(xt[:, p], 0)
                    wait(dve, r_ready, upto(i, p, 1, -1))
                    dve.wait_ge(rs_ready, upto(i, p, 2, 1))
                    link.done(normalize(hb[p], xt[:, p], 0))
                    link.wait()
                    link.done(nc.vector.tensor_tensor(hb[p], hb[p],
                                                      modv[:, 1:2, :].to_broadcast([P, TT, C]), ALU.mult))
                    link.wait()
                    link.done(nc.vector.tensor_tensor(hb[p], hb[p],
                                                      modv[:, 0:1, :].to_broadcast([P, TT, C]), ALU.add))
                    link.wait()
                    stats(hb[p], 1)
                    wait(dve, n2_transposed, upto(i, p, 1, 0))
                    dve.wait_ge(rs_ready, upto(i, p, 2, 2))
                    normalize(n2, hb[p], 1).then_inc(n2_ready, 1)

                norms(0, 0)
                dve.wait_ge(pre_pool, 1)
                for k in range(KC):
                    nc.vector.tensor_tensor(sn[:, k], simt[:, k], col_inv[:], ALU.mult)
                for k in range(1, SCAN):
                    dve.wait_ge(pow_mm, k)
                    nc.vector.tensor_copy(powers[:, k, pad:], ps[:, MISC, 0:2 * P]).then_inc(pow_ready, 1)

                taps = Link(dve, conv_link, 2)

                def conv(i, p):
                    taps.block(i, p)
                    dve.wait_ge(proj_evac, upto(i, p, 2 * FI, FI))
                    wait(dve, u_ready, upto(i, p, 1, 0))
                    for f in range(FI):
                        ins = nc.vector.tensor_scalar(cv[:, f], data[:, f, 0:BT], cw[:, f, 0:1], None, ALU.mult)
                    taps.done(ins)
                    for j in range(1, TAPS):
                        taps.wait()
                        for f in range(FI):
                            ins = nc.vector.scalar_tensor_tensor(
                                out=cv[:, f], in0=data[:, f, j:j + BT], scalar=cw[:, f, j:j + 1],
                                in1=cv[:, f], op0=ALU.mult, op1=ALU.add)
                        if j < TAPS - 1:
                            taps.done(ins)
                    ins.then_inc(conv_ready, 1)

                def slot(i, p, last):
                    if not last:
                        norms(*following(i, p))
                    conv(i, p)

                slots(dve, slot)
                for k in range(SCAN):
                    if k == 0:
                        dve.wait_ge(scan_in, 16)
                    dve.wait_ge(scan_mm, k + 1)
                    nc.vector.tensor_tensor(scan_s[(k + 1) % 2], scan_s[k % 2], ps[:, k % 2, :], ALU.add
                                            ).then_inc(scan_add, 1)

            @block.tensor
            def _(pe):
                pe.wait_ge(pre_dve, 3)
                for b in range(3):
                    for k in range(KC):
                        ins = nc.tensor.matmul(ps[:, T_BANK + b, :], c_bc[:, k, :], wmod_ld[:, k, b * BT:(b + 1) * BT],
                                               start=(k == 0), stop=(k == KC - 1))
                ins.then_inc(mod_mm, 1)
                pe.wait_ge(pool_const, 2)
                for k in range(KC):
                    ins = nc.tensor.matmul(ps[:, MISC, 0:E], ones_f[:], sim_sq[:, k, :],
                                           start=(k == 0), stop=(k == KC - 1))
                ins.then_inc(colnorm_mm, 1)

                def transposes(i, p):
                    pe.wait_ge(n2_ready, upto(i, p, 1, 1))
                    wait(pe, ht_ready, upto(i, p, 1, 0))
                    for k in range(KC):
                        for t in range(TT):
                            ins = nc.tensor.transpose(ps[:, T_BANK + k, t * P:(t + 1) * P],
                                                      n2[:, t, k * P:(k + 1) * P], ident[:])
                    ins.then_inc(n2_transposed, 1)

                def project(i, p):
                    pe.wait_ge(ht_lo_ready, upto(i, p, 1, 1))
                    for f in range(2 * FI):
                        bank = P_BANK + (2 * FI * p + f) % 4
                        wait(pe, proj_evac, upto(i, p, 2 * FI, f - 3))
                        cols = slice(f * P, (f + 1) * P)
                        for k in range(KC):
                            for n, (a, b) in enumerate(((win_hi, ht_hi), (win_hi, ht_lo), (win_lo, ht_hi))):
                                ins = nc.tensor.matmul(ps[:, bank, :], a[:, k, cols], b[:, k, :],
                                                       start=(k == 0 and n == 0), stop=(k == KC - 1 and n == 2))
                        ins.then_inc(proj_mm, 1)

                def input_term(i, p):
                    pe.wait_ge(u_ready, upto(i, p, 1, 1))
                    wait(pe, bu_ready, upto(i, p, 1, 0))
                    for f in range(FI):
                        ins = nc.tensor.matmul(ps[0:S, BU_BANK, :], bmt[:, f, :], sg[:, f, :],
                                               start=(f == 0), stop=(f == FI - 1))
                    ins.then_inc(bu_mm, 1)

                pe.wait_ge(mod_ready, 1)
                transposes(0, 0)
                pe.wait_ge(win_split, 1)
                project(0, 0)
                pe.wait_ge(col_ss, 1)
                for k in range(1, SCAN):
                    pe.wait_ge(pow_ready, k)
                    m, mt = powers[:, k - 1, pad:pad + P], powers[:, k - 1, pad + P:]
                    nc.tensor.matmul(ps[:, MISC, 0:P], mt, m, start=True, stop=True)
                    nc.tensor.matmul(ps[:, MISC, P:2 * P], m, mt, start=True, stop=True).then_inc(pow_mm, 1)

                def slot(i, p, last):
                    if not last:
                        transposes(*following(i, p))
                        project(*following(i, p))
                    input_term(i, p)

                slots(pe, slot)
                pe.wait_ge(scan_in, 16)
                pe.wait_ge(pow_ready, SCAN)
                for k in range(SCAN):
                    d = 1 << k
                    if k:
                        pe.wait_ge(scan_add, k)
                    src, dst = scan_s[k % 2], ps[:, k % 2, :]
                    if d < BT:
                        nc.tensor.matmul(dst[:, d:BT], pw_m(k), src[:, 0:BT - d], start=True, stop=True)
                        ins = nc.tensor.matmul(dst[:, 0:d], pw_m(k, 1), src[:, BT - d:BT], start=True, stop=True)
                    else:
                        ins = nc.tensor.matmul(dst, pw_m(k, d // BT), src, start=True, stop=True)
                    ins.then_inc(scan_mm, 1)
        one.close()

        two = mid.enter_context(ExitStack())
        sb = alloc(two)
        wout = sb("wout", [P, FI, C])
        cmt = sb("cmt", [S, INNER])
        stb = sb("stb", [S, BT])
        gy = sb("gy", [P, FI, BT])
        x2 = sb("x2", [P, TT, C])
        h2 = sb("h2", [P, TT, C])
        h2t = sb("h2t", [P, KC, BT])
        xt_hi = sb("xt_hi", [P, 2, KC, BT], F32R)
        xt_lo = sb("xt_lo", [P, 2, KC, BT], F32R)
        acc = sb("acc", [P, 2, H3])
        junk = sb("junk", [P, TT, C])
        bst2 = sb("bst2", [P, TT, 6])
        mv2 = sb("mv2", [P, TT, 2])
        var2 = sb("var2", [P, TT])
        rs2 = sb("rs2", [P, TT])
        sumsq = sb("sumsq", [P, TT])
        inv_norm = sb("inv_norm", [P, TT])
        w_cur = sb("w_cur", [P, 2, TT, E])
        lg = sb("lg", [P, TT, E])
        gated = sb("gated", [P, TT, E])
        hard = sb("hard", [P, TT, E])
        pick = sb("pick", [P, TT, E])
        first_hot = sb("first_hot", [P, TT, E])
        lg_rest = sb("lg_rest", [P, TT, E])
        shifted = sb("shifted", [P, TT, E])
        g_max = sb("g_max", [P, TT, 1])
        top = sb("top", [P, TT, 1])
        inactive = sb("inactive", [P, TT, 1])
        w_sum = sb("w_sum", [P, TT, 1])

        params2_in = sem("params2_in")
        st_in = sem("st_in")
        gate_in = sem("gate_in")
        r_in = sem("r_in")
        x2_out = sem("x2_out")
        y_mm = sem("y_mm")
        gy_ready = sem("gy_ready")
        out_mm = sem("out_mm")
        x2_ready = sem("x2_ready")
        mv2_ready = sem("mv2_ready")
        pool_b = sem("pool_b")
        rs2_ready = sem("rs2_ready")
        h2_ready = sem("h2_ready")
        sumsq_ready = sem("sumsq_ready")
        inv_norm_ready = sem("inv_norm_ready")
        h2_transposed = sem("h2_transposed")
        h2t_ready = sem("h2t_ready")
        xlo_ready = sem("xlo_ready")
        logits_mm = sem("logits_mm")
        dve_b = sem("dve_b")
        shifted_ready = sem("shifted_ready")
        exp_ready = sem("exp_ready")
        w_ready = sem("w_ready")
        moe_mm = sem("moe_mm")
        moe_acc = sem("moe_acc")
        qk_mm = sem("qk_mm")
        qkv_ready = sem("qkv_ready")

        STEPS = TT * E
        MOE_BANKS, C_BANK, QK_BANK = 4, 4, 7
        DVE_B, POOL_B = 25, 2
        AT_Y, AT_GATE, AT_OUT, AT_X2, AT_TRANSPOSE, AT_LOGITS, AT_ROUTE = 1, 4, 8, 12, 32, 38, 42

        def tiles(i, p, t=0, n=1):
            return bass.ds(i * (2 * TT) + p * TT + t, n)

        with nc.Block() as block:
            @block.sync
            def _(sp):
                def prepare(i, p):
                    wait(sp, y_mm, upto(i, p, 1, 0))
                    sp.dma_start(stb[:], st_dram[bass.ds(i * (2 * S) + p * S, S), :]).then_inc(st_in, 16)
                    wait(sp, out_mm, upto(i, p, 1, 0))
                    sp.dma_start(gy[:], gate_dram[:, :, bass.ds(i * (2 * BT) + p * BT, BT)]).then_inc(gate_in, 16)
                    wait(sp, x2_out, upto(i, p, 16, 0))
                    wait(sp, h2_ready, upto(i, p, 1, 0))
                    sp.dma_start(x2[:], tok_view(r_dram)[:, tiles(i, p, 0, TT), :]).then_inc(r_in, 16)
                    sp.wait_ge(x2_ready, upto(i, p, 1, 1))
                    sp.dma_start(tok_view(x2_dram)[:, tiles(i, p, 0, TT), :], x2[:]).then_inc(x2_out, 16)

                sp.dma_start(cmt[:], cm_t).then_inc(params2_in, 16)
                sp.dma_start(wout[:], w_out.rearrange("(f p) n -> p f n", p=P)).then_inc(params2_in, 16)
                prepare(0, 0)
                slots(sp, lambda i, p, last: None if last else prepare(*following(i, p)))
                sp.wait_ge(x2_out, 16 * NB)

            @block.gpsimd
            def _(pool):
                link = Link(pool, pool_b, POOL_B)

                def prepare(i, p):
                    link.block(i, p)
                    pool.wait_ge(mv2_ready, upto(i, p, 1, 1))
                    link.done(nc.gpsimd.tensor_tensor(var2[:], mv2[:, :, 1], eps[:], ALU.add))
                    link.wait()
                    nc.gpsimd.tensor_tensor(rs2[:], var2[:], minus_half[:, 0:TT], ALU.pow).then_inc(rs2_ready, 1)
                    pool.wait_ge(sumsq_ready, upto(i, p, 1, 1))
                    wait(pool, w_ready, upto(i, p, 1, 0))
                    apart(pool)
                    link.done(nc.gpsimd.tensor_scalar(sumsq[:], sumsq[:], 1e-24, None, ALU.max))
                    link.wait()
                    nc.gpsimd.tensor_tensor(inv_norm[:], sumsq[:], minus_half[:, 0:TT], ALU.pow
                                            ).then_inc(inv_norm_ready, 1)
                    pool.wait_ge(h2t_ready, upto(i, p, 1, 1))
                    nc.gpsimd.tensor_tensor(xt_lo[:, p], h2t[:], xt_hi[:, p].bitcast(F32), ALU.subtract
                                            ).then_inc(xlo_ready, 1)

                prepare(0, 0)
                slots(pool, lambda i, p, last: None if last else prepare(*following(i, p)))

            @block.scalar
            def _(act):
                def hidden(i, p):
                    act.wait_ge(h2_ready, upto(i, p, 1, 1))
                    wait(act, inv_norm_ready, upto(i, p, 1, 0))
                    for t in range(TT):
                        ins = nc.scalar.activation(junk[:, t], h2[:, t], ACT.Square, accum_out=sumsq[:, t:t + 1])
                    ins.then_inc(sumsq_ready, 1)
                    act.wait_ge(h2_transposed, upto(i, p, 1, 1))
                    wait(act, logits_mm, upto(i, p, 1, 0))
                    src = ps[:, C_BANK + 1:C_BANK + 3, :]
                    nc.scalar.copy(h2t[:], src)
                    wait(act, moe_mm, upto(i, p, STEPS, -STEPS))
                    nc.scalar.copy(xt_hi[:, p], src).then_inc(h2t_ready, 1)

                def exp(i, p):
                    act.wait_ge(shifted_ready, upto(i, p, 1, 1))
                    nc.scalar.activation(shifted[:], shifted[:], ACT.Exp).then_inc(exp_ready, 1)

                def evacuate(i, p, t):
                    act.wait_ge(qk_mm, upto(i, p, TT, t + 1))
                    cols = bass.ds(i * (2 * BT) + p * BT + t * P, P)
                    nc.scalar.copy(q_t[:, cols], ps[:, QK_BANK, 0:P])
                    nc.scalar.copy(k_t[:, cols], ps[:, QK_BANK, P:2 * P])
                    nc.scalar.copy(v_all[:, tiles(i, p, t), :], acc[:, t % 2:t % 2 + 1, 2 * H:]).then_inc(qkv_ready, 1)

                hidden(0, 0)
                exp(0, 0)

                def slot(i, p, last):
                    evacuate(i, p, 0)
                    if not last:
                        hidden(*following(i, p))
                    evacuate(i, p, 1)
                    if not last:
                        exp(*following(i, p))
                    evacuate(i, p, 2)
                    evacuate(i, p, 3)

                slots(act, slot)

            @block.vector
            def _(dve):
                link = Link(dve, dve_b, DVE_B)

                def gate_times_y(i, p):
                    dve.wait_ge(y_mm, upto(i, p, 1, 1))
                    dve.wait_ge(gate_in, upto(i, p, 16, 16))
                    nc.vector.tensor_tensor(gy[:], gy[:], ps[:, C_BANK:C_BANK + FI, :], ALU.mult).then_inc(gy_ready, 1)

                def op(ins):
                    link.done(ins)

                out_ps = ps[:, C_BANK:C_BANK + 2, :].rearrange("p b (t c) -> p (b t) c", c=C)

                def norm_piece(n, i, p):
                    if n == 0:
                        link.block(i, p)
                        dve.wait_ge(out_mm, upto(i, p, 1, 1))
                        wait(dve, h2_transposed, upto(i, p, 1, 0))
                        wait(dve, sumsq_ready, upto(i, p, 1, 0))
                        op(nc.vector.tensor_tensor(h2[:], out_ps, modv[:, 2:3, :].to_broadcast([P, TT, C]), ALU.mult))
                    elif n == 1:
                        dve.wait_ge(r_in, upto(i, p, 16, 16))
                        link.wait()
                        nc.vector.tensor_tensor(x2[:], x2[:], h2[:], ALU.add).then_inc(x2_ready, 1)
                    elif n == 2:
                        dve.wait_ge(x2_ready, upto(i, p, 1, 1))
                        for t in range(TT):
                            ins = nc.vector.bn_stats(bst2[:, t], x2[:, t])
                        op(ins)
                    elif n == 3:
                        link.wait()
                        apart(dve)
                        for t in range(TT):
                            ins = nc.vector.bn_aggr(mv2[:, t], bst2[:, t])
                        ins.then_inc(mv2_ready, 1)
                    elif n == 4:
                        dve.wait_ge(rs2_ready, upto(i, p, 1, 1))
                        for t in range(TT):
                            ins = nc.vector.tensor_scalar(h2[:, t], x2[:, t], mv2[:, t, 0:1], rs2[:, t:t + 1],
                                                          ALU.subtract, ALU.mult)
                        op(ins)
                    elif n == 5:
                        link.wait()
                        op(nc.vector.tensor_tensor(h2[:], h2[:], modv[:, 4:5, :].to_broadcast([P, TT, C]), ALU.mult))
                    else:
                        link.wait()
                        nc.vector.tensor_tensor(h2[:], h2[:], modv[:, 3:4, :].to_broadcast([P, TT, C]), ALU.add
                                                ).then_inc(h2_ready, 1)

                def wide(a):
                    return a.to_broadcast([P, TT, E])

                def route_piece(n, i, p):
                    tt, tr, ts = nc.vector.tensor_tensor, nc.vector.tensor_reduce, nc.vector.tensor_scalar
                    if n == 0:
                        dve.wait_ge(logits_mm, upto(i, p, 1, 1))
                        dve.wait_ge(inv_norm_ready, upto(i, p, 1, 1))
                        op(tt(lg[:], ps[:, C_BANK, 0:TT * E].rearrange("p (t e) -> p t e", e=E),
                              wide(inv_norm[:].rearrange("p (t a) -> p t a", a=1)), ALU.mult))
                        link.wait()
                        op(tt(lg[:], lg[:], wide(sig_gates[:].rearrange("p (a e) -> p a e", a=1)), ALU.subtract))
                    elif n == 1:
                        link.wait()
                        ts(gated[:], lg[:], 0.0, None, ALU.max)
                        ts(hard[:], lg[:], 0.0, None, ALU.is_gt)
                        op(tr(top[:], lg[:], AX_X, ALU.max))
                        link.wait()
                        op(tr(g_max[:], gated[:], AX_X, ALU.max))
                    elif n == 2:
                        link.wait()
                        tt(shifted[:], gated[:], wide(g_max[:]), ALU.subtract).then_inc(shifted_ready, 1)
                        ts(inactive[:], g_max[:], 0.0, None, ALU.is_le)
                        op(tt(pick[:], lg[:], wide(top[:]), ALU.is_equal))
                        link.wait()
                        op(tt(pick[:], pick[:], rank[:], ALU.mult))
                    elif n == 3:
                        link.wait()
                        op(tr(top[:], pick[:], AX_X, ALU.max))
                        link.wait()
                        op(tt(first_hot[:], rank[:], wide(top[:]), ALU.is_equal))
                    elif n == 4:
                        link.wait()
                        op(nc.vector.scalar_tensor_tensor(out=lg_rest[:], in0=first_hot[:], scalar=-1e30,
                                                          in1=lg[:], op0=ALU.mult, op1=ALU.add))
                        link.wait()
                        op(tr(top[:], lg_rest[:], AX_X, ALU.max))
                    elif n == 5:
                        link.wait()
                        op(tt(pick[:], lg_rest[:], wide(top[:]), ALU.is_equal))
                        link.wait()
                        op(tt(pick[:], pick[:], rank[:], ALU.mult))
                    elif n == 6:
                        link.wait()
                        op(tr(top[:], pick[:], AX_X, ALU.max))
                        link.wait()
                        op(tt(pick[:], rank[:], wide(top[:]), ALU.is_equal))
                    elif n == 7:
                        link.wait()
                        op(tt(pick[:], pick[:], first_hot[:], ALU.add))
                        link.wait()
                        op(tt(pick[:], pick[:], wide(inactive[:]), ALU.mult))
                        link.wait()
                        op(tt(pick[:], pick[:], hard[:], ALU.add))
                    elif n == 8:
                        dve.wait_ge(exp_ready, upto(i, p, 1, 1))
                        link.wait()
                        op(tt(pick[:], pick[:], shifted[:], ALU.mult))
                        link.wait()
                        op(tr(w_sum[:], pick[:], AX_X, ALU.add))
                    elif n == 9:
                        link.wait()
                        op(nc.vector.reciprocal(w_sum[:], w_sum[:]))
                        link.wait()
                        op(tt(w_cur[:, p], pick[:], wide(w_sum[:]), ALU.mult))
                    else:
                        link.wait()
                        nc.vector.tensor_copy(w_all[:, tiles(i, p, 0, TT), :], w_cur[:, p]).then_inc(w_ready, 1)

                NORM_PIECES, ROUTE_PIECES = 7, 11
                gate_times_y(0, 0)
                for n in range(NORM_PIECES):
                    norm_piece(n, 0, 0)
                for n in range(ROUTE_PIECES):
                    route_piece(n, 0, 0)

                def slot(i, p, last):
                    dve.wait_ge(w_ready, upto(i, p, 1, 1))
                    for s in range(STEPS):
                        t, e = divmod(s, E)
                        dve.wait_ge(moe_mm, upto(i, p, STEPS, s + 1))
                        src, w, dst = ps[:, s % MOE_BANKS, 0:H3], w_cur[:, p, t, e:e + 1], acc[:, t % 2]
                        if e == 0:
                            wait(dve, qkv_ready, upto(i, p, TT, t - 1))
                            nc.vector.tensor_scalar(dst, src, w, None, ALU.mult).then_inc(moe_acc, 1)
                        else:
                            dve.wait_ge(moe_acc, upto(i, p, STEPS, s))
                            nc.vector.scalar_tensor_tensor(out=dst, in0=src, scalar=w, in1=dst,
                                                           op0=ALU.mult, op1=ALU.add).then_inc(moe_acc, 1)
                        if not last:
                            ni, np_ = following(i, p)
                            if s == AT_GATE:
                                gate_times_y(ni, np_)
                            for n in range(NORM_PIECES):
                                if s == AT_X2 + 2 * n + (1 if n >= 4 else 0):
                                    norm_piece(n, ni, np_)
                            for n in range(ROUTE_PIECES):
                                if s == AT_ROUTE + n + (2 if n >= 8 else 0):
                                    route_piece(n, ni, np_)

                slots(dve, slot)

            @block.tensor
            def _(pe):
                def y_piece(i, p):
                    pe.wait_ge(st_in, upto(i, p, 16, 16))
                    wait(pe, w_ready, upto(i, p, 1, 0))
                    wait(pe, h2t_ready, upto(i, p, 1, 0))
                    for f in range(FI):
                        ins = nc.tensor.matmul(ps[:, C_BANK + f, :], cmt[:, f * P:(f + 1) * P], stb[:],
                                               start=True, stop=True)
                    ins.then_inc(y_mm, 1)

                def out_piece(i, p):
                    pe.wait_ge(gy_ready, upto(i, p, 1, 1))
                    for t in range(TT):
                        dst = ps[:, C_BANK + t // 2, (t % 2) * C:(t % 2 + 1) * C]
                        for f in range(FI):
                            ins = nc.tensor.matmul(dst, gy[:, f, t * P:(t + 1) * P], wout[:, f, :],
                                                   start=(f == 0), stop=(f == FI - 1))
                    ins.then_inc(out_mm, 1)

                def transpose_piece(i, p):
                    pe.wait_ge(h2_ready, upto(i, p, 1, 1))
                    for k in range(KC):
                        for t in range(TT):
                            ins = nc.tensor.transpose(ps[:, C_BANK + 1 + k, t * P:(t + 1) * P],
                                                      h2[:, t, k * P:(k + 1) * P], ident[:])
                    ins.then_inc(h2_transposed, 1)

                def logits_piece(i, p):
                    pe.wait_ge(h2t_ready, upto(i, p, 1, 1))
                    for t in range(TT):
                        for k in range(KC):
                            ins = nc.tensor.matmul(ps[:, C_BANK, t * E:(t + 1) * E], h2t[:, k, t * P:(t + 1) * P],
                                                   sn[:, k, :], start=(k == 0), stop=(k == KC - 1))
                    ins.then_inc(logits_mm, 1)

                def qk_transposes(i, p, t):
                    pe.wait_ge(moe_acc, upto(i, p, STEPS, (t + 1) * E))
                    wait(pe, qkv_ready, upto(i, p, TT, t))
                    nc.tensor.transpose(ps[:, QK_BANK, 0:P], acc[:, t % 2, 0:H], ident[:])
                    nc.tensor.transpose(ps[:, QK_BANK, P:2 * P], acc[:, t % 2, H:2 * H], ident[:]).then_inc(qk_mm, 1)

                pe.wait_ge(params2_in, 32)
                pieces = {AT_Y: y_piece, AT_OUT: out_piece, AT_TRANSPOSE: transpose_piece, AT_LOGITS: logits_piece}
                for at in sorted(pieces):
                    pieces[at](0, 0)

                def slot(i, p, last):
                    pe.wait_ge(xlo_ready, upto(i, p, 1, 1))
                    for s in range(STEPS):
                        t, e = divmod(s, E)
                        wait(pe, moe_acc, upto(i, p, STEPS, s - MOE_BANKS + 1))
                        rows = slice(t * P, (t + 1) * P)
                        for k in range(KC):
                            for n, (a, b) in enumerate(((xt_hi, w_hi), (xt_hi, w_lo), (xt_lo, w_hi))):
                                ins = nc.tensor.matmul(
                                    ps[:, s % MOE_BANKS, 0:H3], a[:, p, k, rows],
                                    b[:, k, e].rearrange("p t h -> p (t h)"),
                                    start=(k == 0 and n == 0), stop=(k == KC - 1 and n == 2))
                        ins.then_inc(moe_mm, 1)
                        if e == 2 and t:
                            qk_transposes(i, p, t - 1)
                        if not last and s in pieces:
                            pieces[s](*following(i, p))
                    qk_transposes(i, p, TT - 1)

                slots(pe, slot)
        two.close()
        mid.close()

        three = whole.enter_context(ExitStack())
        sb = alloc(three)
        k_hi = sb("k_hi", [P, N], F32R)
        k_lo = sb("k_lo", [P, N], F32R)
        v_hi = sb("v_hi", [P, NT, H], F32R)
        v_lo = sb("v_lo", [P, NT, H], F32R)
        o_hi = sb("o_hi", [P, E, C], F32R)
        o_lo = sb("o_lo", [P, E, C], F32R)
        o_stage = k_t[:].rearrange("p (e c) -> p e c", e=E)
        q_hi = sb("q_hi", [P, 2, BT], F32R)
        q_lo = sb("q_lo", [P, 2, BT], F32R)
        PB = 3
        pf = sb("pf", [P, PB, BT])
        p_hi = sb("p_hi", [P, PB, BT], F32R)
        p_lo = sb("p_lo", [P, PB, BT], F32R)
        p_sum = sb("p_sum", [P, 2, BT])
        ot_hi = sb("ot_hi", [P, 2, BT], F32R)
        ot_lo = sb("ot_lo", [P, 2, BT], F32R)
        mx = sb("mx", [P, TT, KG])
        neg_max = sb("neg_max", [P, TT])
        neg_row = sb("neg_row", [1, 2, BT], F32R)
        inv_sum = sb("inv_sum", [P, TT, 1])
        w_out_s = sb("w_out_s", [P, 2, TT, E])
        y = sb("y", [P, 2, C])
        yo = sb("yo", [P, 2, C])
        x2b = sb("x2b", [P, TT, C])

        o_in = sem("o_in")
        k_hi_ready = sem("k_hi_ready")
        k_lo_ready = sem("k_lo_ready")
        v_hi_ready = sem("v_hi_ready")
        v_lo_ready = sem("v_lo_ready")
        o_hi_ready = sem("o_hi_ready")
        o_lo_ready = sem("o_lo_ready")
        q_hi_ready = sem("q_hi_ready")
        q_lo_ready = sem("q_lo_ready")
        max_mm = sem("max_mm")
        max_red = sem("max_red")
        neg_max_ready = sem("neg_max_ready")
        neg_mm = sem("neg_mm")
        neg_row_ready = sem("neg_row_ready")
        s_mm = sem("s_mm")
        pf_ready = sem("pf_ready")
        p_hi_ready = sem("p_hi_ready")
        p_lo_ready = sem("p_lo_ready")
        p_summed = sem("p_summed")
        pv_mm = sem("pv_mm")
        sum_mm = sem("sum_mm")
        inv_sum_ready = sem("inv_sum_ready")
        w_out_ready = sem("w_out_ready")
        ot_hi_ready = sem("ot_hi_ready")
        ot_lo_ready = sem("ot_lo_ready")
        o_mm = sem("o_mm")
        y_acc = sem("y_acc")
        yo_ready = sem("yo_ready")
        yo_scaled = sem("yo_scaled")
        x2_in = sem("x2_in")
        out_done = [sem("out_done0"), sem("out_done1")]

        S_BANK, MAX_BANK, O_BANK, Y_BANK, NEG_BANK = 0, 2, 3, 5, 7
        LAG = 2
        PAIRS = E // 2
        assert TT * PAIRS == NT and TT * KG == NT

        def before(i, p):
            return (i - 1, 1) if p == 0 else (i, 0)

        def cycle(eng, start, body, finish):
            start()
            body(0, 0, True, False)
            body(0, 1, False, False)
            with eng.Fori(1, NB // 2 - 1) as i:
                body(i, 0, False, False)
                body(i, 1, False, False)
            body(NB // 2 - 1, 0, False, False)
            body(NB // 2 - 1, 1, False, True)
            finish()

        with nc.Block() as block:
            @block.sync
            def _(sp):
                sp.wait_ge(k_lo_ready, 1)
                sp.dma_start(o_stage, o_proj.rearrange("e h c -> h e c")).then_inc(o_in, 16)
                ov = tok_view(out)

                def outputs(i, p):
                    wait(sp, yo_ready, upto(i, p, TT, 0))
                    sp.dma_start(x2b[:], tok_view(x2_dram)[:, tiles(i, p, 0, TT), :]).then_inc(x2_in, 16)
                    for t in range(TT):
                        sp.wait_ge(yo_ready, upto(i, p, TT, t + 1))
                        sp.dma_start(ov[:, tiles(i, p, t), :], yo[:, t % 2:t % 2 + 1, :]).then_inc(out_done[t % 2], 16)

                outputs(0, 0)
                outputs(0, 1)
                with sp.Fori(1, NB // 2) as i:
                    outputs(i, 0)
                    outputs(i, 1)
                for n in range(2):
                    sp.wait_ge(out_done[n], 16 * NB * TT // 2)

            @block.gpsimd
            def _(pool):
                def finish_tile(i, p, t):
                    pool.wait_ge(y_acc, upto(i, p, TT * E, (t + 1) * E))
                    wait(pool, out_done[t % 2], upto(i, p, 16 * TT // 2, 16 * (t // 2)))
                    nc.gpsimd.tensor_tensor(yo[:, t % 2], y[:, t % 2], modv[:, 5], ALU.mult).then_inc(yo_scaled, 1)
                    if t == 0:
                        pool.wait_ge(x2_in, upto(i, p, 16, 16))
                    pool.wait_ge(yo_scaled, upto(i, p, TT, t + 1))
                    nc.gpsimd.tensor_tensor(yo[:, t % 2], yo[:, t % 2], x2b[:, t], ALU.add).then_inc(yo_ready, 1)

                def body(i, p, first, last):
                    for j in range(NT):
                        pool.wait_ge(pf_ready, upto(i, p, NT, j + 1))
                        if j == 0:
                            wait(pool, sum_mm, upto(i, p, 1, -1))
                            apart(pool)
                            nc.gpsimd.tensor_copy(p_sum[:, p], pf[:, 0]).then_inc(p_summed, 1)
                        else:
                            pool.wait_ge(p_summed, upto(i, p, NT, j))
                            nc.gpsimd.tensor_tensor(p_sum[:, p], p_sum[:, p], pf[:, j % PB], ALU.add
                                                    ).then_inc(p_summed, 1)
                        if not first and j % PAIRS == LAG + 1 and j >= PAIRS:
                            finish_tile(*before(i, p), j // PAIRS - 1)
                    if not first:
                        finish_tile(*before(i, p), TT - 1)

                def finish():
                    for t in range(TT):
                        finish_tile(NB // 2 - 1, 1, t)

                cycle(pool, lambda: None, body, finish)

            @block.scalar
            def _(act):
                def split_q(i, p):
                    nc.scalar.copy(q_hi[:, p], q_t[:, bass.ds(i * (2 * BT) + p * BT, BT)]).then_inc(q_hi_ready, 1)

                def max_row(i, p):
                    act.wait_ge(neg_mm, upto(i, p, 1, 1))
                    nc.scalar.copy(neg_row[:, p], ps[0:1, NEG_BANK, :]).then_inc(neg_row_ready, 1)

                def start():
                    split_q(0, 0)
                    nc.scalar.copy(k_hi[:], k_t[:]).then_inc(k_hi_ready, 1)
                    nc.scalar.copy(v_hi[:], v_all[:]).then_inc(v_hi_ready, 1)
                    split_q(0, 1)
                    act.wait_ge(o_in, 16)
                    nc.scalar.copy(o_hi[:], o_stage).then_inc(o_hi_ready, 1)
                    max_row(0, 0)

                def body(i, p, first, last):
                    for j in range(NT):
                        act.wait_ge(s_mm, upto(i, p, NT, j + 1))
                        wait(act, p_summed, upto(i, p, NT, j - PB + 1))
                        wait(act, p_lo_ready, upto(i, p, NT, j - PB + 1))
                        wait(act, pv_mm, upto(i, p, NT, j - PB + 1))
                        buf = j % PB
                        nc.scalar.activation(pf[:, buf], ps[:, S_BANK + j % 2, :], ACT.Exp, scale=SCALE
                                             ).then_inc(pf_ready, 1)
                        nc.scalar.activation(p_hi[:, buf], ps[:, S_BANK + j % 2, :], ACT.Exp, scale=SCALE
                                             ).then_inc(p_hi_ready, 1)
                    if not last:
                        max_row(*following(i, p))
                    act.wait_ge(pv_mm, upto(i, p, NT, NT))
                    wait(act, o_mm, upto(i, p, NT, -NT))
                    nc.scalar.copy(ot_hi[:, p], ps[:, O_BANK + p, :]).then_inc(ot_hi_ready, 1)
                    if not last:
                        if isinstance(i, int) and i == NB // 2 - 1:
                            return
                        split_q(i + 1, p)

                cycle(act, start, body, lambda: None)

            @block.vector
            def _(dve):
                def split_q(i, p):
                    dve.wait_ge(q_hi_ready, upto(i, p, 1, 1))
                    nc.vector.tensor_tensor(q_lo[:, p], q_t[:, bass.ds(i * (2 * BT) + p * BT, BT)],
                                            q_hi[:, p].bitcast(F32), ALU.subtract).then_inc(q_lo_ready, 1)

                def max_piece(i, p, j):
                    dve.wait_ge(max_mm, upto(i, p, NT, j + 1))
                    t, g = divmod(j, KG)
                    nc.vector.tensor_reduce(mx[:, t, g:g + 1], ps[:, MAX_BANK, :], AX_X, ALU.max
                                            ).then_inc(max_red, 1)

                def max_all(i, p):
                    dve.wait_ge(max_red, upto(i, p, NT, NT))
                    wait(dve, neg_mm, upto(i, p, 1, 0))
                    nc.vector.tensor_reduce(neg_max[:], mx[:], AX_X, ALU.max, negate=True).then_inc(neg_max_ready, 1)

                def start():
                    split_q(0, 0)
                    dve.wait_ge(k_hi_ready, 1)
                    for j in range(NT):
                        max_piece(0, 0, j)
                    max_all(0, 0)
                    nc.vector.tensor_tensor(k_lo[:], k_t[:], k_hi[:].bitcast(F32), ALU.subtract).then_inc(k_lo_ready, 1)
                    dve.wait_ge(v_hi_ready, 1)
                    nc.vector.tensor_tensor(v_lo[:], v_all[:], v_hi[:].bitcast(F32), ALU.subtract
                                            ).then_inc(v_lo_ready, 1)
                    split_q(0, 1)

                def low_part(i, p, j):
                    dve.wait_ge(p_hi_ready, upto(i, p, NT, j + 1))
                    wait(dve, pv_mm, upto(i, p, NT, j - PB + 1))
                    nc.vector.tensor_tensor(p_lo[:, j % PB], pf[:, j % PB], p_hi[:, j % PB].bitcast(F32),
                                            ALU.subtract).then_inc(p_lo_ready, 1)

                def accumulate(i, p, j):
                    t, pair = divmod(j, PAIRS)
                    dve.wait_ge(o_mm, upto(i, p, NT, j + 1))
                    for n in range(2):
                        e = 2 * pair + n
                        src, w = ps[:, Y_BANK + j % 2, n * C:(n + 1) * C], w_out_s[:, p, t, e:e + 1]
                        if e == 0:
                            wait(dve, yo_ready, upto(i, p, TT, t - 1))
                            nc.vector.tensor_scalar(y[:, t % 2], src, w, None, ALU.mult).then_inc(y_acc, 1)
                        else:
                            dve.wait_ge(y_acc, upto(i, p, TT * E, t * E + e))
                            nc.vector.scalar_tensor_tensor(out=y[:, t % 2], in0=src, scalar=w, in1=y[:, t % 2],
                                                           op0=ALU.mult, op1=ALU.add).then_inc(y_acc, 1)

                def body(i, p, first, last):
                    for j in range(NT + LAG):
                        if 1 <= j <= NT:
                            low_part(i, p, j - 1)
                        if not last and j < NT:
                            max_piece(*following(i, p), j)
                        if not first and j >= LAG:
                            accumulate(*before(i, p), j - LAG)
                    if not last:
                        max_all(*following(i, p))
                    dve.wait_ge(sum_mm, upto(i, p, 1, 1))
                    nc.vector.reciprocal(inv_sum[:, :, 0], ps[:, MAX_BANK, 0:TT]).then_inc(inv_sum_ready, 1)
                    dve.wait_ge(inv_sum_ready, upto(i, p, 1, 1))
                    nc.vector.tensor_tensor(w_out_s[:, p], w_all[:, tiles(i, p, 0, TT), :],
                                            inv_sum[:].to_broadcast([P, TT, E]), ALU.mult).then_inc(w_out_ready, 1)
                    dve.wait_ge(ot_hi_ready, upto(i, p, 1, 1))
                    nc.vector.tensor_tensor(ot_lo[:, p], ps[:, O_BANK + p, :], ot_hi[:, p].bitcast(F32),
                                            ALU.subtract).then_inc(ot_lo_ready, 1)
                    if first:
                        dve.wait_ge(o_hi_ready, 1)
                        nc.vector.tensor_tensor(o_lo[:], o_stage, o_hi[:].bitcast(F32), ALU.subtract
                                                ).then_inc(o_lo_ready, 1)
                    dve.wait_ge(w_out_ready, upto(i, p, 1, 1))
                    if not last and not (isinstance(i, int) and i == NB // 2 - 1):
                        split_q(i + 1, p)

                def finish():
                    for j in range(NT):
                        accumulate(NB // 2 - 1, 1, j)

                cycle(dve, start, body, finish)

            @block.tensor
            def _(pe):
                def max_piece(i, p, j):
                    t, g = divmod(j, KG)
                    if j == 0:
                        pe.wait_ge(q_hi_ready, upto(i, p, 1, 1))
                        wait(pe, inv_sum_ready, upto(i, p, 1, -1))
                    wait(pe, max_red, upto(i, p, NT, j))
                    nc.tensor.matmul(ps[:, MAX_BANK, :], q_hi[:, p, t * P:(t + 1) * P], k_hi[:, g * BT:(g + 1) * BT],
                                     start=True, stop=True).then_inc(max_mm, 1)

                def max_transposes(i, p):
                    pe.wait_ge(neg_max_ready, upto(i, p, 1, 1))
                    wait(pe, neg_row_ready, upto(i, p, 1, 0))
                    for t in range(TT):
                        ins = nc.tensor.transpose(ps[0:1, NEG_BANK, t * P:(t + 1) * P], neg_max[:, t:t + 1], ident[:])
                    ins.then_inc(neg_mm, 1)

                def scores(i, p, j):
                    if j == 0:
                        pe.wait_ge(q_lo_ready, upto(i, p, 1, 1))
                        pe.wait_ge(neg_row_ready, upto(i, p, 1, 1))
                    wait(pe, p_hi_ready, upto(i, p, NT, j - 1))
                    keys, dst = slice(j * P, (j + 1) * P), ps[:, S_BANK + j % 2, :]
                    nc.tensor.matmul(dst, k_hi[:, keys], q_hi[:, p], start=True, stop=False)
                    nc.tensor.matmul(dst, k_hi[:, keys], q_lo[:, p], start=False, stop=False)
                    nc.tensor.matmul(dst, k_lo[:, keys], q_hi[:, p], start=False, stop=False)
                    nc.tensor.matmul(dst, ones_r[:], neg_row[:, p], start=False, stop=True).then_inc(s_mm, 1)

                def values(i, p, j):
                    if j == 0:
                        wait(pe, ot_lo_ready, upto(i, p, 1, -1))
                    pe.wait_ge(p_lo_ready, upto(i, p, NT, j + 1))
                    dst, buf = ps[:, O_BANK + p, :], j % PB
                    nc.tensor.matmul(dst, v_hi[:, j], p_hi[:, buf], start=(j == 0), stop=False)
                    nc.tensor.matmul(dst, v_lo[:, j], p_hi[:, buf], start=False, stop=False)
                    nc.tensor.matmul(dst, v_hi[:, j], p_lo[:, buf], start=False, stop=(j == NT - 1)).then_inc(pv_mm, 1)

                def project(i, p, j):
                    t, pair = divmod(j, PAIRS)
                    if j == 0:
                        pe.wait_ge(ot_lo_ready, upto(i, p, 1, 1))
                        pe.wait_ge(w_out_ready, upto(i, p, 1, 1))
                    wait(pe, y_acc, upto(i, p, TT * E, 2 * (j - 1)))
                    rows, dst = slice(t * P, (t + 1) * P), ps[:, Y_BANK + j % 2, :]
                    for n, (a, b) in enumerate(((ot_hi, o_hi), (ot_hi, o_lo), (ot_lo, o_hi))):
                        ins = nc.tensor.matmul(dst, a[:, p, rows],
                                               b[:, 2 * pair:2 * pair + 2].rearrange("p e c -> p (e c)"),
                                               start=(n == 0), stop=(n == 2))
                    ins.then_inc(o_mm, 1)

                def start():
                    pe.wait_ge(k_hi_ready, 1)
                    for j in range(NT):
                        max_piece(0, 0, j)
                    max_transposes(0, 0)
                    pe.wait_ge(k_lo_ready, 1)
                    pe.wait_ge(v_lo_ready, 1)

                def body(i, p, first, last):
                    for j in range(NT + LAG):
                        if j < NT:
                            scores(i, p, j)
                        if not last and j < NT:
                            max_piece(*following(i, p), j)
                        if not first and j >= LAG:
                            project(*before(i, p), j - LAG)
                        if j >= LAG:
                            values(i, p, j - LAG)
                    if not last:
                        max_transposes(*following(i, p))
                        pe.wait_ge(max_red, upto(*following(i, p), NT, NT))
                    pe.wait_ge(p_summed, upto(i, p, NT, NT))
                    for t in range(TT):
                        ins = nc.tensor.matmul(ps[:, MAX_BANK, t:t + 1], p_sum[:, p, t * P:(t + 1) * P],
                                               ones_f[:, 0:1], start=True, stop=True)
                    ins.then_inc(sum_mm, 1)
                    if first:
                        pe.wait_ge(o_lo_ready, 1)

                def finish():
                    for j in range(NT):
                        project(NB // 2 - 1, 1, j)

                cycle(pe, start, body, finish)


def kernel(**inputs):
    import numpy as np
    import concourse.bacc as bacc
    from concourse.bass_utils import run_bass_kernel_spmd

    a = {name[3:]: np.asarray(value) for name, value in inputs.items()}
    n, c = a["attn_x"].shape[1:]
    by_column = lambda v: v.reshape(-1, 128).T
    laid = {
        "x": a["attn_x"].reshape(n, c), "ln_w": by_column(a["attn_ln_w"]),
        "ln_b": by_column(a["attn_ln_b"]), "w_in": a["attn_W_in"],
        "conv_w": a["attn_conv_w"], "a_mat": a["attn_A"], "a_mat_t": a["attn_A"].T, "bm_t": a["attn_Bm"].T,
        "cm_t": a["attn_Cm"].T, "w_out": a["attn_W_out"], "sim": a["ffn_sim_matrix"], "gates": a["ffn_gates"],
        "q_proj": a["ffn_q_proj"], "k_proj": a["ffn_k_proj"], "v_proj": a["ffn_v_proj"],
        "o_proj": a["ffn_o_proj"], "cond": by_column(a["c"]), "wmod": a["wmod"],
    }
    nc = bacc.Bacc("TRN2", target_bir_lowering=False, num_devices=1)
    arrays, args = {}, []
    for name, value in laid.items():
        arrays["in_" + name] = np.ascontiguousarray(value)
        args.append(nc.dram_tensor("in_" + name, value.shape, mybir.dt.from_np(value.dtype), kind="ExternalInput").ap())
    out = nc.dram_tensor("out_x", (n, c), F32, kind="ExternalOutput").ap()
    adaln_block_kernel(nc, *args, out)
    r = run_bass_kernel_spmd(nc, [arrays], core_ids=[0])
    return r.results[0]["out_x"].reshape(1, n, c)
```

```python
from contextlib import ExitStack

import concourse.bass as bass
from concourse import mybir

F32 = mybir.dt.float32
F32R = mybir.dt.float32r
ALU = mybir.AluOpType
ACT = mybir.ActivationFunctionType
AX_X = mybir.AxisListType.X


def adaln_block_kernel(nc, x, ln_w, ln_b, w_in, conv_w, a_mat, a_mat_t, bm_t, cm_t, w_out,
                       sim, gates, q_proj, k_proj, v_proj, o_proj, cond, wmod, out):
    P = 128
    N, C = x.shape
    KC = C // P
    INNER = w_in.shape[1] // 2
    FI = INNER // P
    S = a_mat.shape[0]
    TAPS = conv_w.shape[1]
    E, _, H = q_proj.shape
    BT = 512
    TT = BT // P
    NB = N // BT
    NT = N // P
    KG = N // BT
    H3 = 3 * H
    SCALE = float(H) ** -0.5
    assert NB * S == P and NB % 2 == 0 and NB >= 4 and FI == 3 and KC == 2 and TT == 4 and E == 16
    assert H == P

    GT = BT * S // P
    SCAN = BT.bit_length() - 1
    X2_COLS = TT * C

    x2_dram = nc.dram_tensor("x2_scratch", (N, C), F32).ap()
    qk_dram = nc.dram_tensor("qk_scratch", (P, 2, N), F32).ap()
    v_dram = nc.dram_tensor("v_scratch", (N, H), F32).ap()
    bu_dram = nc.dram_tensor("bu_scratch", (NB, P, GT), F32).ap()
    st_dram = nc.dram_tensor("state_scratch", (2, NB, P, GT), F32).ap()

    def tok_view(ap):
        return ap.rearrange("(n p) c -> p n c", p=P)

    def upto(i, p, per, k=0):
        return i * (2 * per) + (p * per + k)

    def wait(eng, sem, value):
        if not isinstance(value, int) or value > 0:
            eng.wait_ge(sem, value)

    class Link:

        def __init__(self, eng, sem, per):
            self.eng, self.sem, self.per, self.n, self.base = eng, sem, per, 0, 0

        def block(self, i, p):
            assert self.n in (0, self.per), (self.sem, self.n)
            self.n, self.base = 0, upto(i, p, self.per)

        def done(self, ins):
            ins.then_inc(self.sem, 1)
            self.n += 1

        def wait(self):
            self.eng.wait_ge(self.sem, self.base + self.n)

    def slots(eng, body):
        body(0, 0, 2)
        body(0, 1, 2)
        with eng.Fori(1, NB // 2 - 1) as i:
            body(i, 0, 2)
            body(i, 1, 2)
        body(NB // 2 - 1, 0, 1)
        body(NB // 2 - 1, 1, 0)

    def following(i, p):
        return (i, 1) if p == 0 else (i + 1, 0)

    nc.disable_value_cache = True

    with ExitStack() as whole:
        def alloc(stack):
            def sb(name, shape, dt=F32):
                return stack.enter_context(nc.sbuf_tensor(name, shape, dt))
            return sb

        def sem(name):
            return whole.enter_context(nc.semaphore(name))

        sb = alloc(whole)
        ident = sb("ident", [P, P])
        ones_f = sb("ones_f", [P, P])
        ones_r = sb("ones_r", [1, P], F32R)
        modv = sb("modv", [P, 6, C])
        w_all = sb("w_all", [P, NT, E])
        inv_sum = sb("inv_sum", [P, TT, 1])
        mx = sb("mx", [P, TT, KG])
        ps = whole.enter_context(nc.psum_tensor("ps", [P, 8, 512], F32))

        memory = sb("memory", [P, 11 * C * TT + 768])
        taken = [0]

        def carve(shape, at=None):
            n = 1
            for d in shape:
                n *= d
            start = taken[0] if at is None else at
            taken[0] = max(taken[0], start + n)
            assert taken[0] <= memory.shape[1]
            flat = memory[:, start:start + n]
            if len(shape) == 1:
                return flat
            if len(shape) == 2:
                return flat.rearrange("p (a b) -> p a b", b=shape[1])
            return flat.rearrange("p (a b c) -> p a b c", b=shape[1], c=shape[2])

        k_t = carve([N])
        v_all = carve([NT, H])
        q_st = carve([2, BT])
        taken[0] = 0
        xt = carve([TT, C])
        hb = carve([TT, C])
        sg = carve([FI, BT])
        n2 = carve([TT, C], at=2 * X2_COLS)
        ht = carve([KC, BT], at=3 * X2_COLS)
        h2 = carve([TT, C])
        x2 = carve([TT, C])
        gy = carve([FI, BT])
        h2t = carve([KC, BT])
        wmod_at = taken[0]
        data = carve([FI, BT + TAPS - 1])
        cv = carve([FI, BT])
        wmod_ld = carve([KC, 6 * C], at=wmod_at)
        win = carve([KC, 2 * INNER], at=5 * X2_COLS)
        cm_ld = carve([INNER], at=4 * X2_COLS)[0:3 * S]
        c_bc = carve([KC, P], at=4 * X2_COLS + INNER)
        simt = carve([KC, E], at=4 * X2_COLS + INNER + KC * P)
        powers_t = carve([2, P], at=4 * X2_COLS + INNER + KC * P + KC * E)
        w_third = carve([KC, 3, H], at=6 * X2_COLS + FI * BT)
        assert 2 * N <= taken[0]

        memory_r = sb("memory_r", [P, 4 * INNER * KC + 4 * KC * BT], F32R)
        WIN_COLS, XT_COLS = KC * 2 * INNER, KC * BT
        win_hi = memory_r[:, 0:WIN_COLS].rearrange("p (k n) -> p k n", k=KC)
        win_lo = memory_r[:, WIN_COLS:2 * WIN_COLS].rearrange("p (k n) -> p k n", k=KC)
        xt_parts = memory_r[:, 2 * WIN_COLS:].rearrange("p (q l k n) -> p q l k n", q=2, l=2, k=KC)
        xt_hi = [xt_parts[:, q, 0] for q in range(2)]
        xt_lo = [xt_parts[:, q, 1] for q in range(2)]
        k_hi = memory_r[:, 0:N]
        q_hi = memory_r[:, N:N + 2 * BT].rearrange("p (q n) -> p q n", q=2)
        q_lo = memory_r[:, N + 2 * BT:N + 4 * BT].rearrange("p (q n) -> p q n", q=2)
        assert N + 2 * BT <= 2 * WIN_COLS + 2 * XT_COLS

        one = whole.enter_context(ExitStack())
        sb = alloc(one)
        w_hi = sb("w_hi", [P, KC, E, 3, H], F32R)
        w_lo = sb("w_lo", [P, KC, E, 3, H], F32R)
        wst = sb("wst", [P, 2, KC, 3, H])
        pad = 4 * S
        powers = sb("powers", [P, SCAN, pad + P])
        wrap = sb("wrap", [P, P])
        minus_half = sb("minus_half", [P, TT])
        eps = sb("eps", [P, TT])
        sn = sb("sn", [P, KC, E])
        sim_sq = sb("sim_sq", [P, KC, E])
        sig_gates = sb("sig_gates", [P, E])
        col_inv = sb("col_inv", [P, E])
        half_e = sb("half_e", [P, E])
        wout = sb("wout", [P, FI, C])
        cm_parts = sb("cm_parts", [3 * S, INNER], F32R)
        rank = sb("rank", [P, TT, E])
        c_col = sb("c_col", [P, KC])
        c_sig = sb("c_sig", [P, KC])
        lnw = sb("lnw", [P, KC])
        lnb = sb("lnb", [P, KC])
        cw = sb("cw", [P, FI, TAPS])
        bmt = sb("bmt", [P, FI, S])
        bst = sb("bst", [P, 3, TT, 6])
        mv = sb("mv", [P, 3, TT, 2])
        var_eps = sb("var_eps", [P, 3, TT])
        rs = sb("rs", [P, 3, TT])
        sumsq = sb("sumsq", [P, TT])
        inv_norm = sb("inv_norm", [P, TT])
        scan_s = [sb("scan_a", [P, GT]), sb("scan_b", [P, GT])]
        carry = sb("carry", [P, 1])
        s_parts = sb("s_parts", [P, 2, GT], F32R)
        st_parts = sb("st_parts", [3 * S, BT], F32R)
        bu = sb("bu", [S, BT])
        w_staged = [wst[:, 0], wst[:, 1], w_third]
        w_stage = wst[:].rearrange("p a k t h -> p (a k t h)")
        acc = w_stage[:, 0:2 * H3].rearrange("p (a n) -> p a n", a=2)
        qk_st = w_stage[:, 2 * H3:2 * H3 + 4 * P].rearrange("p (a b n) -> p a b n", a=2, b=2)
        w_cur = sb("w_cur", [P, 2, TT, E])
        lg = sb("lg", [P, TT, E])
        gated = sb("gated", [P, TT, E])
        hard = sb("hard", [P, TT, E])
        pick = sb("pick", [P, TT, E])
        first_hot = sb("first_hot", [P, TT, E])
        lg_rest = sb("lg_rest", [P, TT, E])
        shifted = sb("shifted", [P, TT, E])
        g_max = sb("g_max", [P, TT, 1])
        top = sb("top", [P, TT, 1])
        inactive = sb("inactive", [P, TT, 1])
        w_sum = sb("w_sum", [P, TT, 1])
        g_tmp = w_all[:].rearrange("p n e -> p (n e)").rearrange("p (g c) -> p g c", g=2)

        carriers = sem("carriers")
        params_in = sem("params_in")
        zeroed = sem("zeroed")
        a_in = sem("a_in")
        x_in = sem("x_in")
        cond_in = sem("cond_in")
        wmod_in = sem("wmod_in")
        w_in_sem = [sem(f"w_in{n}") for n in range(3)]
        w_hi_ready = sem("w_hi_ready")
        w_lo_ready = sem("w_lo_ready")
        pool_const = sem("pool_const")
        sig_ready = sem("sig_ready")
        win_hi_ready = sem("win_hi_ready")
        cm_hi_ready = sem("cm_hi_ready")
        pre_dve = sem("pre_dve")
        sn_ready = sem("sn_ready")
        wout_ready = sem("wout_ready")
        col_inv_ready = sem("col_inv_ready")
        mod_mm = sem("mod_mm")
        mod_copied = sem("mod_copied")
        mod_ready = sem("mod_ready")
        parts_ready = sem("parts_ready")
        colnorm_mm = sem("colnorm_mm")
        col_ss = sem("col_ss")
        pow_mm = sem("pow_mm")
        pow_ready = sem("pow_ready")
        dve_a = sem("dve_a")
        pool_a = sem("pool_a")
        mv_ready = sem("mv_ready")
        rs_ready = sem("rs_ready")
        n2_ready = sem("n2_ready")
        n2_transposed = sem("n2_transposed")
        ht_ready = sem("ht_ready")
        ht_lo_ready = sem("ht_lo_ready")
        proj_mm = sem("proj_mm")
        proj_evac = sem("proj_evac")
        conv_link = sem("conv_link")
        conv_ready = sem("conv_ready")
        halo_ready = sem("halo_ready")
        csig_ready = sem("csig_ready")
        u_ready = sem("u_ready")
        r_ready = sem("r_ready")
        bu_mm = sem("bu_mm")
        bu_ready = sem("bu_ready")
        bu_out = sem("bu_out")
        scan_in = sem("scan_in")
        carry_mm = sem("carry_mm")
        carry_added = sem("carry_added")
        scan_mm = sem("scan_mm")
        scan_add = sem("scan_add")
        s_hi_ready = sem("s_hi_ready")
        s_parts_ready = sem("s_parts_ready")
        st_out = sem("st_out")
        st_in = sem("st_in")
        x2_out = sem("x2_out")
        y_mm = sem("y_mm")
        gy_ready = sem("gy_ready")
        out_mm = sem("out_mm")
        x2_ready = sem("x2_ready")
        h2_ready = sem("h2_ready")
        pool_b = sem("pool_b")
        mv2_ready = sem("mv2_ready")
        rs2_ready = sem("rs2_ready")
        sumsq_ready = sem("sumsq_ready")
        inv_norm_ready = sem("inv_norm_ready")
        h2_transposed = sem("h2_transposed")
        h2t_ready = sem("h2t_ready")
        xlo_ready = sem("xlo_ready")
        logits_mm = sem("logits_mm")
        dve_b = sem("dve_b")
        shifted_ready = sem("shifted_ready")
        exp_ready = sem("exp_ready")
        w_ready = sem("w_ready")
        moe_mm = sem("moe_mm")
        moe_acc = sem("moe_acc")
        qk_mm = sem("qk_mm")
        qk_ready = sem("qk_ready")
        qk_out = [sem("qk_out0"), sem("qk_out1")]
        v_out = [sem("v_out0"), sem("v_out1")]
        kv_in = [sem(f"kv_in{g}") for g in range(NB)]
        q_in = sem("q_in")
        q_hi_ready = sem("q_hi_ready")
        k_hi_ready = sem("k_hi_ready")
        max_mm = sem("max_mm")
        max_red = sem("max_red")
        h_scaled = sem("h_scaled")
        win_free = sem("win_free")

        STEPS = TT * E
        MOE_BANKS, QK_BANK = 4, 7
        X0, X1, X2 = 4, 5, 6
        DVE_A, DVE_B, POOL_A, POOL_B = 4, 23, 2, 2
        DVE_ROUTE = 46
        N_PARAMS = 11
        W_BUFS = len(w_staged)
        MAX_FROM, MAX_EARLY = 6, TT * (KG - 1)
        SCAN_AT = {1 + 2 * k: k for k in range(SCAN)}
        PE_TRANSPOSE_N2, PE_Y, PE_OUT, PE_PROJECT, PE_TRANSPOSE_H2, PE_LOGITS, PE_BU = 19, 24, 27, 31, 40, 44, 49
        DVE_PIECES = {
            0: ("carry", 0), 2: ("norm", 0), 6: ("norm", 1), 9: ("norm", 2), 12: ("norm", 3), 15: ("norm", 4),
            24: ("gate", 0), 29: ("x2", 0), 31: ("x2", 1), 33: ("x2", 2), 34: ("x2", 3), 37: ("x2", 4),
            35: ("conv", 0), 39: ("conv", 1),
        }

        def tiles(i, p, t=0, n=1):
            return bass.ds(i * (2 * TT) + p * TT + t, n)

        def apart(eng):
            eng.sem_inc(carriers, 1)

        def pw_m(k, shift=0):
            return powers[:, k, pad - S * shift:pad - S * shift + P]

        with nc.Block() as block:
            @block.sync
            def _(sp):
                xv = tok_view(x)
                sp.dma_start(c_col[:], cond).then_inc(cond_in, 16)
                sp.dma_start(xt, xv[:, 0:TT, :]).then_inc(x_in, 16)
                sp.dma_start(wmod_ld, wmod.rearrange("(k p) n -> p k n", p=P)).then_inc(wmod_in, 16)
                cm_rows = [(cm_ld[n * S:(n + 1) * S, :], cm_t) for n in range(3)]
                params = [
                    (lnw[:], ln_w),
                    (lnb[:], ln_b),
                    (win, w_in.rearrange("(k p) n -> p k n", p=P)),
                    (simt, sim.rearrange("(k p) e -> p k e", p=P)),
                    (sig_gates[:], gates.rearrange("(a e) -> a e", a=1).to_broadcast([P, E])),
                    (cw[:], conv_w.rearrange("(f p) j -> p f j", p=P)),
                    (bmt[:], bm_t.rearrange("(f p) s -> p f s", p=P)),
                    (wout[:], w_out.rearrange("(f p) n -> p f n", p=P)),
                ] + cm_rows
                assert len(params) == N_PARAMS
                for dst, src in params:
                    sp.dma_start(dst, src).then_inc(params_in, 16)
                sp.wait_ge(zeroed, 1)
                for g in range(NB):
                    rows = slice(S * g, S * g + S)
                    sp.dma_start(powers[rows, 0, pad + S * g:pad + S * g + S], a_mat_t).then_inc(a_in, 16)
                    sp.dma_start(powers_t[rows, 0, S * g:S * g + S], a_mat).then_inc(a_in, 16)

                def load_w(e0, e1):
                    for e in range(e0, e1):
                        if e >= W_BUFS:
                            sp.wait_ge(w_lo_ready, e - W_BUFS + 1)
                        for t, proj in enumerate((q_proj, k_proj, v_proj)):
                            sp.dma_start(w_staged[e % W_BUFS][:, :, t], proj[e].rearrange("(k p) h -> p k h", p=P)
                                         ).then_inc(w_in_sem[e % W_BUFS], 16)

                def scan_load(i, p):
                    sp.wait_ge(bu_out, upto(i, p, 16, 16))
                    wait(sp, s_parts_ready, upto(i, p, 1, 0))
                    sp.dma_start(scan_s[0][:], bu_dram[bass.ds(i * 2 + p, 1)].rearrange("a p t -> p (a t)")
                                 ).then_inc(scan_in, 16)

                def states_round(i, p):
                    sp.wait_ge(s_parts_ready, upto(i, p, 1, 1))
                    for l in range(2):
                        sp.dma_start(st_dram[l, bass.ds(i * 2 + p, 1)].rearrange("a p t -> p (a t)"), s_parts[:, l].bitcast(F32)
                                     ).then_inc(st_out, 16)
                    sp.wait_ge(st_out, upto(i, p, 32, 32))
                    wait(sp, y_mm, upto(i, p, 1, 0))
                    for n, l in enumerate((0, 1, 0)):
                        sp.dma_start(st_parts[n * S:(n + 1) * S, :].bitcast(F32).rearrange("s (g t) -> s g t", g=NB),
                                     st_dram[l, bass.ds(i * 2 + p, 1)].rearrange("a (g s) t -> s (a g) t", s=S)
                                     ).then_inc(st_in, 16)

                def x2_store(i, p):
                    sp.wait_ge(x2_ready, upto(i, p, 1, 1))
                    sp.dma_start(tok_view(x2_dram)[:, tiles(i, p, 0, TT), :], x2).then_inc(x2_out, 16)

                def x_load(i, p):
                    sp.wait_ge(r_ready, upto(i, p, 1, 0))
                    sp.dma_start(xt, xv[:, tiles(i, p, 0, TT), :]).then_inc(x_in, 16)

                load_w(0, 6)
                x_load(0, 1)
                load_w(6, 9)
                scan_load(0, 0)
                load_w(9, 12)
                states_round(0, 0)
                load_w(12, 15)
                x2_store(0, 0)
                load_w(15, E)
                scan_load(0, 1)

                def slot(i, p, ahead):
                    if ahead >= 2:
                        x_load(i + 1, p)
                    if ahead >= 1:
                        states_round(*following(i, p))
                        x2_store(*following(i, p))
                    if ahead >= 2:
                        scan_load(i + 1, p)
                    if ahead == 0:
                        for g in range(NB):
                            if g == 0:
                                sp.wait_ge(h2t_ready, NB)
                                sp.wait_ge(x2_out, 16 * NB)
                                sp.wait_ge(xlo_ready, NB)
                                sp.wait_ge(w_ready, NB)
                                sp.wait_ge(moe_mm, (NB - 1) * STEPS)
                                sp.wait_ge(u_ready, NB)
                                sp.wait_ge(bu_mm, NB)
                            for n in range(2):
                                sp.wait_ge(qk_out[n], 16 * (g + 1) * TT // 2)
                                sp.wait_ge(v_out[n], 16 * (g + 1) * TT // 2)
                            sp.dma_start(k_t[:, g * BT:(g + 1) * BT], qk_dram[:, 1, g * BT:(g + 1) * BT]
                                         ).then_inc(kv_in[g], 16)
                            sp.dma_start(v_all[:, g * TT:(g + 1) * TT, :],
                                         v_dram.rearrange("(n p) h -> p n h", p=P)[:, g * TT:(g + 1) * TT, :]
                                         ).then_inc(kv_in[g], 16)
                            if g == 0:
                                sp.dma_start(q_st[:, 0], qk_dram[:, 0, 0:BT]).then_inc(q_in, 16)
                            if g == NB // 2:
                                sp.wait_ge(q_hi_ready, 1)
                                sp.dma_start(q_st[:, 1], qk_dram[:, 0, BT:2 * BT]).then_inc(q_in, 16)

                slots(sp, slot)

            @block.gpsimd
            def _(pool):
                nc.gpsimd.memset(powers_t, 0.0)
                nc.gpsimd.memset(powers[:], 0.0).then_inc(zeroed, 1)
                nc.gpsimd.memset(minus_half[:], -0.5)
                nc.gpsimd.memset(half_e[:], -0.5)
                nc.gpsimd.memset(eps[:], 1e-5)
                nc.gpsimd.memset(ones_f[:], 1.0).then_inc(pool_const, 1)
                pool.wait_ge(pool_const, 1)
                nc.gpsimd.affine_select(out=ident[:], in_=ones_f[:], compare_op=ALU.is_equal, fill=0.0, base=0,
                                        pattern=[[1, P]], channel_multiplier=-1).then_inc(pool_const, 1)
                for e in range(E):
                    ins = nc.gpsimd.memset(rank[:, :, e], float(E - e))
                ins.then_inc(pool_const, 1)
                pool.wait_ge(col_ss, 1)
                nc.gpsimd.tensor_tensor(col_inv[:], col_inv[:], half_e[:], ALU.pow).then_inc(col_inv_ready, 1)
                link_a, link_b = Link(pool, pool_a, POOL_A), Link(pool, pool_b, POOL_B)

                def inv_std(i, p, n):
                    pool.wait_ge(mv_ready, upto(i, p, 2, n + 1))
                    link_a.done(nc.gpsimd.tensor_tensor(var_eps[:, n], mv[:, n, :, 1], eps[:], ALU.add))
                    link_a.wait()
                    nc.gpsimd.tensor_tensor(rs[:, n], var_eps[:, n], minus_half[:], ALU.pow).then_inc(rs_ready, 1)

                def first_norms(i, p):
                    link_a.block(i, p)
                    inv_std(i, p, 0)
                    inv_std(i, p, 1)

                def low_hidden(i, p):
                    pool.wait_ge(ht_ready, upto(i, p, 1, 1))
                    nc.gpsimd.tensor_tensor(xt_lo[1 - p], ht, xt_hi[1 - p].bitcast(F32), ALU.subtract
                                            ).then_inc(ht_lo_ready, 1)

                def second_norm(i, p):
                    link_b.block(i, p)
                    pool.wait_ge(mv2_ready, upto(i, p, 1, 1))
                    link_b.done(nc.gpsimd.tensor_tensor(var_eps[:, 2], mv[:, 2, :, 1], eps[:], ALU.add))
                    link_b.wait()
                    nc.gpsimd.tensor_tensor(rs[:, 2], var_eps[:, 2], minus_half[:], ALU.pow).then_inc(rs2_ready, 1)

                def residual(i, p):
                    pool.wait_ge(n2_ready, upto(i, p, 1, 1))
                    ga = modv[:, 2:3, :].to_broadcast([P, TT, C])
                    nc.gpsimd.tensor_tensor(hb, hb, ga, ALU.mult).then_inc(h_scaled, 1)
                    wait(pool, x2_out, upto(i, p, 16, 0))
                    wait(pool, h2_ready, upto(i, p, 1, 0))
                    pool.wait_ge(h_scaled, upto(i, p, 1, 1))
                    nc.gpsimd.tensor_tensor(x2, xt, hb, ALU.add).then_inc(r_ready, 1)

                def conv_out(i, p):
                    pool.wait_ge(csig_ready, upto(i, p, 1, 1))
                    nc.gpsimd.tensor_tensor(sg, sg, cv, ALU.mult).then_inc(u_ready, 1)

                def row_norms(i, p):
                    pool.wait_ge(sumsq_ready, upto(i, p, 1, 1))
                    wait(pool, w_ready, upto(i, p, 1, 0))
                    apart(pool)
                    link_b.done(nc.gpsimd.tensor_scalar(sumsq[:], sumsq[:], 1e-24, None, ALU.max))
                    link_b.wait()
                    nc.gpsimd.tensor_tensor(inv_norm[:], sumsq[:], minus_half[:], ALU.pow
                                            ).then_inc(inv_norm_ready, 1)
                    pool.wait_ge(h2t_ready, upto(i, p, 1, 1))
                    nc.gpsimd.tensor_tensor(xt_lo[p], h2t, xt_hi[p].bitcast(F32), ALU.subtract
                                            ).then_inc(xlo_ready, 1)

                first_norms(0, 0)
                pool.wait_ge(win_free, 1)
                pool.wait_ge(mod_ready, 1)
                residual(0, 0)

                def pieces(ahead, c, a):
                    if ahead >= 2:
                        first_norms(*a)
                        low_hidden(*a)
                    second_norm(*c)
                    row_norms(*c)
                    if ahead >= 2:
                        conv_out(*a)
                        residual(*a)

                pieces(2, (0, 0), (0, 1))

                def slot(i, p, ahead):
                    if ahead:
                        pieces(ahead, following(i, p), (i + 1, p))

                slots(pool, slot)

            @block.scalar
            def _(act):
                act.wait_ge(cond_in, 16)
                nc.scalar.activation(c_sig[:], c_col[:], ACT.Sigmoid).then_inc(sig_ready, 1)
                act.wait_ge(pool_const, 2)
                nc.scalar.copy(ones_r[:], ones_f[0:1, :])
                act.wait_ge(params_in, 16 * N_PARAMS)
                nc.scalar.activation(sig_gates[:], sig_gates[:], ACT.Sigmoid)
                nc.scalar.copy(win_hi, win).then_inc(win_hi_ready, 1)
                nc.scalar.copy(cm_parts[:], cm_ld).then_inc(cm_hi_ready, 1)
                act.wait_ge(mod_mm, 1)
                nc.scalar.copy(modv[:, 3], ps[:, X1, C:2 * C])
                nc.scalar.copy(modv[:, 2], ps[:, X1, 0:C]).then_inc(mod_copied, 1)

                def split_w(e0, e1):
                    for e in range(e0, e1):
                        act.wait_ge(w_in_sem[e % W_BUFS], 16 * 3 * (e // W_BUFS + 1))
                        nc.scalar.copy(w_hi[:, :, e], w_staged[e % W_BUFS]).then_inc(w_hi_ready, 1)

                def hidden(i, p):
                    act.wait_ge(n2_transposed, upto(i, p, 1, 1))
                    wait(act, moe_mm, upto(i, p, STEPS, -2 * STEPS))
                    for k in range(KC):
                        nc.scalar.activation(ht[:, k], ps[:, X1 + k, :], ACT.Identity,
                                             bias=lnb[:, k:k + 1], scale=lnw[:, k:k + 1])
                        ins = nc.scalar.activation(xt_hi[1 - p][:, k], ps[:, X1 + k, :], ACT.Identity,
                                                   bias=lnb[:, k:k + 1], scale=lnw[:, k:k + 1])
                    ins.then_inc(ht_ready, 1)

                def project_out(i, p, first=False):
                    wait(act, conv_ready, upto(i, p, 1, 0))
                    wait(act, u_ready, upto(i, p, 1, 0))
                    if first:
                        act.wait_ge(mod_mm, 1)
                        nc.scalar.mul(data[:, :, 0:TAPS - 1], ident[:, 0:FI * (TAPS - 1)].rearrange(
                            "p (f j) -> p f j", f=FI), 0.0)
                    else:
                        nc.scalar.copy(data[:, :, 0:TAPS - 1], data[:, :, BT:BT + TAPS - 1]).then_inc(halo_ready, 1)
                        act.wait_ge(halo_ready, upto(i, p, 1, 0))
                    for f in range(2 * FI):
                        act.wait_ge(proj_mm, upto(i, p, 2 * FI, f + 1))
                        src = ps[:, X0 + (f + 2) % 3, :]
                        if f < FI:
                            nc.scalar.copy(data[:, f, TAPS - 1:], src)
                            nc.scalar.mul(cv[:, f], src, cw[:, f, TAPS - 1:TAPS]).then_inc(proj_evac, 1)
                        else:
                            if f == FI:
                                wait(act, out_mm, upto(i, p, 1, 0))
                            nc.scalar.activation(gy[:, f - FI], src, ACT.Sigmoid).then_inc(proj_evac, 1)

                def conv_sigmoid(i, p):
                    act.wait_ge(conv_ready, upto(i, p, 1, 1))
                    wait(act, bu_mm, upto(i, p, 1, 0))
                    act.wait_ge(ht_lo_ready, upto(i, p, 1, 1))
                    nc.scalar.activation(sg, cv, ACT.Sigmoid).then_inc(csig_ready, 1)

                def bu_store(i, p):
                    act.wait_ge(bu_mm, upto(i, p, 1, 1))
                    wait(act, bu_out, upto(i, p, 16, 0))
                    nc.scalar.copy(bu[:], ps[0:S, X1, :]).then_inc(bu_ready, 1)
                    act.wait_ge(bu_ready, upto(i, p, 1, 1))
                    act.dma_start(bu_dram[bass.ds(i * 2 + p, 1)].rearrange("a (g s) t -> s (a g) t", s=S),
                                  bu[:].rearrange("s (g t) -> s g t", g=NB)).then_inc(bu_out, 16)

                def row_squares(i, p):
                    act.wait_ge(h2_ready, upto(i, p, 1, 1))
                    wait(act, inv_norm_ready, upto(i, p, 1, 0))
                    wait(act, logits_mm, upto(i, p, 1, 0))
                    for t in range(TT):
                        ins = nc.scalar.activation(h2t[:, t // 2, (t % 2) * C:(t % 2 + 1) * C], h2[:, t], ACT.Square,
                                                   accum_out=sumsq[:, t:t + 1])
                    ins.then_inc(sumsq_ready, 1)

                def x_parts(i, p):
                    act.wait_ge(h2_transposed, upto(i, p, 1, 1))
                    act.wait_ge(sumsq_ready, upto(i, p, 1, 1))
                    src = ps[:, X1:X1 + 2, :]
                    nc.scalar.copy(h2t, src)
                    wait(act, moe_mm, upto(i, p, STEPS, -STEPS))
                    if not (isinstance(i, int) and 2 * i + p == NB - 1):
                        act.wait_ge(proj_mm, upto(i, p, 2 * FI, 4 * FI))
                    nc.scalar.copy(xt_hi[p], src).then_inc(h2t_ready, 1)

                def exp(i, p):
                    act.wait_ge(shifted_ready, upto(i, p, 1, 1))
                    nc.scalar.activation(shifted[:], shifted[:], ACT.Exp).then_inc(exp_ready, 1)

                def evacuate(i, p, t):
                    act.wait_ge(qk_mm, upto(i, p, TT, t + 1))
                    wait(act, qk_out[t % 2], upto(i, p, 16 * TT // 2, 16 * (t // 2)))
                    nc.scalar.copy(qk_st[:, t % 2], ps[:, QK_BANK, 0:2 * P].rearrange("p (a n) -> p a n", a=2)
                                   ).then_inc(qk_ready, 1)
                    act.wait_ge(qk_ready, upto(i, p, TT, t + 1))
                    cols = bass.ds(i * (2 * BT) + p * BT + t * P, P)
                    act.dma_start(qk_dram[:, :, cols], qk_st[:, t % 2]).then_inc(qk_out[t % 2], 16)
                    act.dma_start(v_dram[cols, :], acc[:, t % 2, 2 * H:]).then_inc(v_out[t % 2], 16)

                split_w(0, 3)
                hidden(0, 0)
                project_out(0, 0, first=True)
                conv_sigmoid(0, 0)
                split_w(3, 6)
                bu_store(0, 0)
                split_w(6, 9)

                def pieces(ahead, c, a, tile):
                    if ahead >= 2:
                        hidden(*a)
                    tile(0)
                    if ahead >= 2:
                        project_out(*a)
                    tile(1)
                    row_squares(*c)
                    x_parts(*c)
                    if ahead >= 2:
                        conv_sigmoid(*a)
                    exp(*c)
                    if ahead >= 2:
                        bu_store(*a)
                    tile(2)
                    tile(3)

                def more_weights(t):
                    split_w(9 + 3 * t, min(12 + 3 * t, E))
                    if t == 1:
                        act.wait_ge(w_lo_ready, 15)

                pieces(2, (0, 0), (0, 1), more_weights)

                def slot(i, p, ahead):
                    if ahead:
                        pieces(ahead, following(i, p), (i + 1, p), lambda t: evacuate(i, p, t))
                    else:
                        act.wait_ge(q_in, 16)
                        act.wait_ge(moe_mm, (NB - 1) * STEPS)
                        nc.scalar.copy(q_hi[:, 0], q_st[:, 0]).then_inc(q_hi_ready, 1)
                        for t in range(TT):
                            for g in (2 * t, 2 * t + 1):
                                if g < NB - 1:
                                    act.wait_ge(kv_in[g], 32)
                                    nc.scalar.copy(k_hi[:, g * BT:(g + 1) * BT], k_t[:, g * BT:(g + 1) * BT]
                                                   ).then_inc(k_hi_ready, 1)
                            evacuate(i, p, t)
                        for n in range(2):
                            act.wait_ge(qk_out[n], 16 * NB * TT // 2)
                            act.wait_ge(v_out[n], 16 * NB * TT // 2)

                slots(act, slot)

            @block.vector
            def _(dve):
                link, more = Link(dve, dve_a, DVE_A), Link(dve, dve_b, DVE_B)
                taps = Link(dve, conv_link, TAPS - 2)
                tt, tr, ts = nc.vector.tensor_tensor, nc.vector.tensor_reduce, nc.vector.tensor_scalar

                def split_w(e0, e1):
                    for e in range(e0, e1):
                        dve.wait_ge(w_hi_ready, e + 1)
                        tt(w_lo[:, :, e], w_staged[e % W_BUFS], w_hi[:, :, e].bitcast(F32), ALU.subtract
                           ).then_inc(w_lo_ready, 1)

                def stats(src, n, chain):
                    for t in range(TT):
                        ins = nc.vector.bn_stats(bst[:, n, t], src[:, t])
                    chain.done(ins)
                    chain.wait()
                    apart(dve)
                    for t in range(TT):
                        ins = nc.vector.bn_aggr(mv[:, n, t], bst[:, n, t])
                    return ins

                def normalize(dst, src, n):
                    for t in range(TT):
                        ins = ts(dst[:, t], src[:, t], mv[:, n, t, 0:1], rs[:, n, t:t + 1], ALU.subtract, ALU.mult)
                    return ins

                def modulate(dst, src, n, first):
                    for t in range(TT):
                        ins = nc.vector.scalar_tensor_tensor(out=dst[:, t], in0=src[:, t], scalar=mv[:, n, t, 0:1],
                                                             in1=modv[:, first], op0=ALU.subtract, op1=ALU.mult)
                    return ins

                def shift(dst, n, second):
                    for t in range(TT):
                        ins = nc.vector.scalar_tensor_tensor(out=dst[:, t], in0=dst[:, t], scalar=rs[:, n, t:t + 1],
                                                             in1=modv[:, second], op0=ALU.mult, op1=ALU.add)
                    return ins

                def norm_piece(n, i, p):
                    if n == 0:
                        link.block(i, p)
                        dve.wait_ge(x_in, upto(i, p, 16, 16))
                        stats(xt, 0, link).then_inc(mv_ready, 1)
                    elif n == 1:
                        wait(dve, r_ready, upto(i, p, 1, 0))
                        dve.wait_ge(mv_ready, upto(i, p, 2, 1))
                        link.done(modulate(hb, xt, 0, 1))
                    elif n == 2:
                        link.wait()
                        dve.wait_ge(rs_ready, upto(i, p, 2, 1))
                        link.done(shift(hb, 0, 0))
                    elif n == 3:
                        link.wait()
                        stats(hb, 1, link).then_inc(mv_ready, 1)
                    else:
                        wait(dve, bu_mm, upto(i, p, 1, 0))
                        dve.wait_ge(rs_ready, upto(i, p, 2, 2))
                        normalize(n2, hb, 1).then_inc(n2_ready, 1)

                def conv_piece(j, i, p):
                    if j == 0:
                        taps.block(i, p)
                        dve.wait_ge(proj_evac, upto(i, p, 2 * FI, FI))
                    else:
                        taps.wait()
                    for f in range(FI):
                        ins = nc.vector.scalar_tensor_tensor(out=cv[:, f], in0=data[:, f, j:j + BT],
                                                             scalar=cw[:, f, j:j + 1], in1=cv[:, f],
                                                             op0=ALU.mult, op1=ALU.add)
                    if j < TAPS - 2:
                        taps.done(ins)
                    else:
                        ins.then_inc(conv_ready, 1)

                def carry_in(i, p):
                    dve.wait_ge(scan_in, upto(i, p, 16, 16))
                    dve.wait_ge(carry_mm, upto(i, p, 1, 0))
                    tt(scan_s[0][0:S, 0:1], scan_s[0][0:S, 0:1], ps[0:S, X0, P:P + 1], ALU.add
                       ).then_inc(carry_added, 1)

                def scan_step(k, i, p):
                    if k == 0 and isinstance(i, int) and i == 0 and p == 0:
                        dve.wait_ge(scan_in, 16)
                    dve.wait_ge(scan_mm, upto(i, p, SCAN, k + 1))
                    tt(scan_s[(k + 1) % 2][:], scan_s[k % 2][:], ps[:, X0, (k % 2) * GT:(k % 2 + 1) * GT], ALU.add
                       ).then_inc(scan_add, 1)

                def state_parts(i, p):
                    dve.wait_ge(scan_add, upto(i, p, SCAN, SCAN))
                    wait(dve, st_out, upto(i, p, 32, 0))
                    nc.vector.tensor_copy(s_parts[:, 0], scan_s[SCAN % 2][:]).then_inc(s_hi_ready, 1)
                    dve.wait_ge(s_hi_ready, upto(i, p, 1, 1))
                    tt(s_parts[:, 1], scan_s[SCAN % 2][:], s_parts[:, 0].bitcast(F32), ALU.subtract
                       ).then_inc(s_parts_ready, 1)

                def gate_times_y(i, p):
                    dve.wait_ge(y_mm, upto(i, p, 1, 1))
                    dve.wait_ge(proj_evac, upto(i, p, 2 * FI, 2 * FI))
                    tt(gy, gy, ps[:, X0:X0 + FI, :], ALU.mult).then_inc(gy_ready, 1)

                def op(ins):
                    more.done(ins)

                out_ps = ps[:, X0:X0 + 2, :].rearrange("p b (t c) -> p (b t) c", c=C)

                def x2_piece(n, i, p):
                    if n == 0:
                        more.block(i, p)
                        dve.wait_ge(out_mm, upto(i, p, 1, 1))
                        dve.wait_ge(r_ready, upto(i, p, 1, 1))
                        tt(x2, x2, out_ps, ALU.add).then_inc(x2_ready, 1)
                    elif n == 1:
                        dve.wait_ge(x2_ready, upto(i, p, 1, 1))
                        for t in range(TT):
                            ins = nc.vector.bn_stats(bst[:, 2, t], x2[:, t])
                        op(ins)
                    elif n == 2:
                        more.wait()
                        apart(dve)
                        for t in range(TT):
                            ins = nc.vector.bn_aggr(mv[:, 2, t], bst[:, 2, t])
                        ins.then_inc(mv2_ready, 1)
                    elif n == 3:
                        wait(dve, h2_transposed, upto(i, p, 1, 0))
                        wait(dve, sumsq_ready, upto(i, p, 1, 0))
                        dve.wait_ge(mv2_ready, upto(i, p, 1, 1))
                        op(modulate(h2, x2, 2, 4))
                    else:
                        more.wait()
                        dve.wait_ge(rs2_ready, upto(i, p, 1, 1))
                        shift(h2, 2, 3).then_inc(h2_ready, 1)

                def wide(a):
                    return a.to_broadcast([P, TT, E])

                def route_piece(n, i, p):
                    link = more
                    if n == 0:
                        dve.wait_ge(logits_mm, upto(i, p, 1, 1))
                        dve.wait_ge(inv_norm_ready, upto(i, p, 1, 1))
                        op(tt(lg[:], ps[:, X0, 0:TT * E].rearrange("p (t e) -> p t e", e=E),
                              wide(inv_norm[:].rearrange("p (t a) -> p t a", a=1)), ALU.mult))
                        link.wait()
                        op(tt(lg[:], lg[:], wide(sig_gates[:].rearrange("p (a e) -> p a e", a=1)), ALU.subtract))
                    elif n == 1:
                        link.wait()
                        ts(gated[:], lg[:], 0.0, None, ALU.max)
                        ts(hard[:], lg[:], 0.0, None, ALU.is_gt)
                        op(tr(top[:], lg[:], AX_X, ALU.max))
                        link.wait()
                        op(tr(g_max[:], gated[:], AX_X, ALU.max))
                    elif n == 2:
                        link.wait()
                        tt(shifted[:], gated[:], wide(g_max[:]), ALU.subtract).then_inc(shifted_ready, 1)
                        ts(inactive[:], g_max[:], 0.0, None, ALU.is_le)
                        op(tt(pick[:], lg[:], wide(top[:]), ALU.is_equal))
                        link.wait()
                        op(tt(pick[:], pick[:], rank[:], ALU.mult))
                    elif n == 3:
                        link.wait()
                        op(tr(top[:], pick[:], AX_X, ALU.max))
                        link.wait()
                        op(tt(first_hot[:], rank[:], wide(top[:]), ALU.is_equal))
                    elif n == 4:
                        link.wait()
                        op(nc.vector.scalar_tensor_tensor(out=lg_rest[:], in0=first_hot[:], scalar=-1e30,
                                                          in1=lg[:], op0=ALU.mult, op1=ALU.add))
                        link.wait()
                        op(tr(top[:], lg_rest[:], AX_X, ALU.max))
                    elif n == 5:
                        link.wait()
                        op(tt(pick[:], lg_rest[:], wide(top[:]), ALU.is_equal))
                        link.wait()
                        op(tt(pick[:], pick[:], rank[:], ALU.mult))
                    elif n == 6:
                        link.wait()
                        op(tr(top[:], pick[:], AX_X, ALU.max))
                        link.wait()
                        op(tt(pick[:], rank[:], wide(top[:]), ALU.is_equal))
                    elif n == 7:
                        link.wait()
                        op(tt(pick[:], pick[:], first_hot[:], ALU.add))
                        link.wait()
                        op(tt(pick[:], pick[:], wide(inactive[:]), ALU.mult))
                        link.wait()
                        op(tt(pick[:], pick[:], hard[:], ALU.add))
                    elif n == 8:
                        dve.wait_ge(exp_ready, upto(i, p, 1, 1))
                        link.wait()
                        op(tt(pick[:], pick[:], shifted[:], ALU.mult))
                        link.wait()
                        op(tr(w_sum[:], pick[:], AX_X, ALU.add))
                    elif n == 9:
                        link.wait()
                        op(nc.vector.reciprocal(w_sum[:], w_sum[:]))
                        link.wait()
                        op(tt(w_cur[:, p], pick[:], wide(w_sum[:]), ALU.mult))
                    else:
                        link.wait()
                        nc.vector.tensor_copy(w_all[:, tiles(i, p, 0, TT), :], w_cur[:, p]).then_inc(w_ready, 1)

                NORM_PIECES, X2_PIECES, ROUTE_PIECES = 5, 5, 11

                def piece(n, kind, c, a, ahead):
                    if kind == "norm" and ahead >= 2:
                        norm_piece(n, *a)
                    elif kind == "conv" and ahead >= 2:
                        conv_piece(n, *a)
                    elif kind == "carry":
                        carry_in(*c)
                    elif kind == "gate":
                        gate_times_y(*c)
                    elif kind == "x2":
                        x2_piece(n, *c)
                    elif kind == "route":
                        route_piece(n, *c)

                def max_piece(n):
                    g, t = divmod(n, TT)
                    dve.wait_ge(max_mm, n + 1)
                    tr(mx[:, t, g:g + 1], ps[:, X0 + n % 2, :], AX_X, ALU.max).then_inc(max_red, 1)

                def pow_copy(k):
                    dve.wait_ge(pow_mm, k)
                    nc.vector.tensor_copy(powers[:, k, pad:], ps[:, QK_BANK, 0:P])
                    nc.vector.tensor_copy(powers_t[:, k % 2], ps[:, QK_BANK, P:2 * P]).then_inc(pow_ready, 1)

                pre = Link(dve, pre_dve, 0)
                norm_piece(0, 0, 0)
                dve.wait_ge(sig_ready, 1)
                pre.done(tt(c_sig[:], c_sig[:], c_col[:], ALU.mult))
                pre.wait()
                for k in range(KC):
                    ins = nc.vector.tensor_copy(c_bc[:, k, :], c_sig[:, k:k + 1].to_broadcast([P, P]))
                pre.done(ins)
                dve.wait_ge(a_in, 16 * 2 * NB)
                dve.wait_ge(pool_const, 2)
                for blk in (powers[:, 0, pad:], powers_t[:, 0]):
                    ins = tt(blk, blk, ident[:], ALU.add)
                ins.then_inc(pow_ready, 1)
                dve.wait_ge(params_in, 16 * N_PARAMS)
                pre.done(tt(sim_sq[:], simt, simt, ALU.mult))
                dve.wait_ge(mod_mm, 1)
                ts(modv[:, 1], ps[:, X0, C:2 * C], 1.0, None, ALU.add)
                nc.vector.tensor_copy(modv[:, 0], ps[:, X0, 0:C])
                nc.vector.tensor_copy(modv[:, 5], ps[:, X2, C:2 * C])
                pre.done(ts(modv[:, 4], ps[:, X2, 0:C], 1.0, None, ALU.add))
                pre.wait()
                norm_piece(1, 0, 0)
                dve.wait_ge(colnorm_mm, 1)
                ts(col_inv[:], ps[:, QK_BANK, 0:E], 1e-24, None, ALU.max).then_inc(col_ss, 1)
                norm_piece(2, 0, 0)
                pow_copy(1)
                norm_piece(3, 0, 0)
                pow_copy(2)
                dve.wait_ge(win_hi_ready, 1)
                tt(win_lo, win, win_hi.bitcast(F32), ALU.subtract).then_inc(win_free, 1)
                norm_piece(4, 0, 0)
                for k in range(3, 6):
                    pow_copy(k)
                dve.wait_ge(ht_ready, 1)
                tt(xt_lo[1], ht, xt_hi[1].bitcast(F32), ALU.subtract).then_inc(ht_lo_ready, 1)
                dve.wait_ge(mod_copied, 1)
                for n, g in enumerate((2, 5)):
                    ins = ts(g_tmp[:, n], modv[:, g], 0.0, 2.0, ALU.is_ge, ALU.mult)
                pre.done(ins)
                pre.wait()
                for n, g in enumerate((2, 5)):
                    nc.vector.scalar_tensor_tensor(out=modv[:, g], in0=modv[:, g], scalar=-1.0,
                                                   in1=modv[:, g], op0=ALU.mult, op1=ALU.max)
                    ins = ts(g_tmp[:, n], g_tmp[:, n], -1.0, None, ALU.add)
                pre.done(ins)
                pre.wait()
                for n, g in enumerate((2, 5)):
                    ins = nc.vector.scalar_tensor_tensor(out=modv[:, g], in0=modv[:, g], scalar=0.25,
                                                         in1=g_tmp[:, n], op0=ALU.max, op1=ALU.mult)
                ins.then_inc(mod_ready, 1)
                split_w(0, 3)
                for n in range(TAPS - 1):
                    conv_piece(n, 0, 0)
                for k in range(6, SCAN):
                    pow_copy(k)
                dve.wait_ge(csig_ready, 1)
                tt(sg, sg, cv, ALU.mult).then_inc(u_ready, 1)
                dve.wait_ge(cm_hi_ready, 1)
                third = slice(2 * S, 3 * S)
                tt(cm_parts[third, :], cm_ld[third, :], cm_parts[third, :].bitcast(F32), ALU.subtract
                   ).then_inc(parts_ready, 1)
                dve.wait_ge(mod_ready, 1)
                tt(wout[:], wout[:], modv[:, 2:3, :].to_broadcast([P, FI, C]), ALU.mult).then_inc(wout_ready, 1)
                dve.wait_ge(col_inv_ready, 1)
                for k in range(KC):
                    ins = tt(sn[:, k], simt[:, k], col_inv[:], ALU.mult)
                ins.then_inc(sn_ready, 1)
                for n in range(NORM_PIECES):
                    norm_piece(n, 0, 1)
                    if n == 0:
                        split_w(3, 6)
                split_w(6, 9)
                for k in range(SCAN):
                    scan_step(k, 0, 0)
                state_parts(0, 0)
                split_w(9, 12)
                gate_times_y(0, 0)
                for n in range(X2_PIECES):
                    x2_piece(n, 0, 0)
                for n in range(TAPS - 1):
                    conv_piece(n, 0, 1)
                split_w(12, 15)
                for n in range(ROUTE_PIECES):
                    route_piece(n, 0, 0)
                split_w(15, E)

                def slot(i, p, ahead):
                    c, a = following(i, p), (i + 1, p)
                    dve.wait_ge(w_ready, upto(i, p, 1, 1))
                    for s in range(STEPS):
                        t, e = divmod(s, E)
                        dve.wait_ge(moe_mm, upto(i, p, STEPS, s + 1))
                        src, w, dst = ps[:, s % MOE_BANKS, 0:H3], w_cur[:, p, t, e:e + 1], acc[:, t % 2]
                        if e == 0:
                            wait(dve, qk_mm, upto(i, p, TT, t - 1))
                            wait(dve, v_out[t % 2], upto(i, p, 16 * TT // 2, 16 * (t // 2)))
                            ts(dst, src, w, None, ALU.mult).then_inc(moe_acc, 1)
                        else:
                            dve.wait_ge(moe_acc, upto(i, p, STEPS, s))
                            nc.vector.scalar_tensor_tensor(out=dst, in0=src, scalar=w, in1=dst,
                                                           op0=ALU.mult, op1=ALU.add).then_inc(moe_acc, 1)
                        if ahead:
                            if s in DVE_PIECES:
                                kind, n = DVE_PIECES[s]
                                piece(n, kind, c, a, ahead)
                            if s in SCAN_AT:
                                scan_step(SCAN_AT[s], *c)
                                if SCAN_AT[s] == SCAN - 1:
                                    state_parts(*c)
                            if s >= DVE_ROUTE and s - DVE_ROUTE < ROUTE_PIECES:
                                route_piece(s - DVE_ROUTE, *c)
                        elif s >= MAX_FROM and (s - MAX_FROM) % 2 == 1 and (s - MAX_FROM) // 2 < MAX_EARLY:
                            max_piece((s - MAX_FROM) // 2)

                slots(dve, slot)

            @block.tensor
            def _(pe):
                pe.wait_ge(pre_dve, 2)
                pe.wait_ge(wmod_in, 16)
                for b in range(3):
                    for k in range(KC):
                        ins = nc.tensor.matmul(ps[:, X0 + b, :], c_bc[:, k, :], wmod_ld[:, k, b * BT:(b + 1) * BT],
                                               start=(k == 0), stop=(k == KC - 1))
                ins.then_inc(mod_mm, 1)
                pe.wait_ge(pre_dve, 3)
                for k in range(KC):
                    ins = nc.tensor.matmul(ps[:, QK_BANK, 0:E], ones_f[:], sim_sq[:, k, :],
                                           start=(k == 0), stop=(k == KC - 1))
                ins.then_inc(colnorm_mm, 1)

                def next_power(k):
                    pe.wait_ge(pow_ready, k)
                    m, mt = powers[:, k - 1, pad:], powers_t[:, (k - 1) % 2]
                    nc.tensor.matmul(ps[:, QK_BANK, 0:P], mt, m, start=True, stop=True)
                    nc.tensor.matmul(ps[:, QK_BANK, P:2 * P], m, mt, start=True, stop=True).then_inc(pow_mm, 1)

                def n2_transposes(i, p):
                    pe.wait_ge(n2_ready, upto(i, p, 1, 1))
                    for k in range(KC):
                        for t in range(TT):
                            ins = nc.tensor.transpose(ps[:, X1 + k, t * P:(t + 1) * P],
                                                      n2[:, t, k * P:(k + 1) * P], ident[:])
                    ins.then_inc(n2_transposed, 1)

                def project(f, i, p):
                    if f == 0:
                        pe.wait_ge(ht_lo_ready, upto(i, p, 1, 1))
                        wait(pe, x2_ready, upto(i, p, 1, 0))
                    wait(pe, proj_evac, upto(i, p, 2 * FI, f - 2))
                    cols = slice(f * P, (f + 1) * P)
                    for k in range(KC):
                        for n, (a, b) in enumerate(((win_hi, xt_hi), (win_hi, xt_lo), (win_lo, xt_hi))):
                            ins = nc.tensor.matmul(ps[:, X0 + (f + 2) % 3, :], a[:, k, cols], b[1 - p][:, k, :],
                                                   start=(k == 0 and n == 0), stop=(k == KC - 1 and n == 2))
                    ins.then_inc(proj_mm, 1)

                def input_term(i, p):
                    pe.wait_ge(u_ready, upto(i, p, 1, 1))
                    pe.wait_ge(proj_evac, upto(i, p, 2 * FI, 2 * FI))
                    wait(pe, h2t_ready, upto(i, p, 1, 0))
                    for f in range(FI):
                        ins = nc.tensor.matmul(ps[0:S, X1, :], bmt[:, f, :], sg[:, f, :],
                                               start=(f == 0), stop=(f == FI - 1))
                    ins.then_inc(bu_mm, 1)

                def carry_piece(i, p):
                    pe.wait_ge(w_ready, upto(i, p, 1, 0))
                    pe.wait_ge(s_parts_ready, upto(i, p, 1, 0))
                    nc.tensor.matmul(ps[0:S, X0, P:P + 1], powers[:, 0, pad + P - S:pad + P],
                                     scan_s[SCAN % 2][:, GT - 1:GT], start=True, stop=True).then_inc(carry_mm, 1)

                def scan_piece(k, i, p, first=False):
                    d = 1 << k
                    if k:
                        pe.wait_ge(scan_add, upto(i, p, SCAN, k))
                    elif first:
                        pe.wait_ge(scan_in, 16)
                    else:
                        pe.wait_ge(carry_added, upto(i, p, 1, 0))
                    src, dst = scan_s[k % 2], ps[:, X0, (k % 2) * GT:(k % 2 + 1) * GT]
                    if d < GT:
                        nc.tensor.matmul(dst[:, d:GT], pw_m(k), src[:, 0:GT - d], start=True, stop=True)
                        ins = nc.tensor.matmul(dst[:, 0:d], pw_m(k, 1), src[:, GT - d:GT], start=True, stop=True)
                    else:
                        ins = nc.tensor.matmul(dst, pw_m(k, d // GT), src[:], start=True, stop=True)
                    ins.then_inc(scan_mm, 1)

                def y_piece(i, p, ahead):
                    pe.wait_ge(st_in, upto(i, p, 48, 48))
                    pe.wait_ge(bu_ready, upto(i, p, 1, 1))
                    if ahead >= 2:
                        pe.wait_ge(ht_ready, upto(i, p, 1, 2))
                    for f in range(FI):
                        ins = nc.tensor.matmul(ps[:, X0 + f, :], cm_parts[:, f * P:(f + 1) * P], st_parts[:],
                                               start=True, stop=True)
                    ins.then_inc(y_mm, 1)

                def out_piece(i, p):
                    pe.wait_ge(gy_ready, upto(i, p, 1, 1))
                    for t in range(TT):
                        dst = ps[:, X0 + t // 2, (t % 2) * C:(t % 2 + 1) * C]
                        for f in range(FI):
                            ins = nc.tensor.matmul(dst, gy[:, f, t * P:(t + 1) * P], wout[:, f, :],
                                                   start=(f == 0), stop=(f == FI - 1))
                    ins.then_inc(out_mm, 1)

                def h2_transposes(i, p):
                    pe.wait_ge(h2_ready, upto(i, p, 1, 1))
                    if not (isinstance(i, int) and 2 * i + p == NB - 1):
                        pe.wait_ge(proj_evac, upto(i, p, 2 * FI, 4 * FI))
                    for k in range(KC):
                        for t in range(TT):
                            ins = nc.tensor.transpose(ps[:, X1 + k, t * P:(t + 1) * P],
                                                      h2[:, t, k * P:(k + 1) * P], ident[:])
                    ins.then_inc(h2_transposed, 1)

                def logits_piece(i, p):
                    pe.wait_ge(h2t_ready, upto(i, p, 1, 1))
                    for t in range(TT):
                        for k in range(KC):
                            ins = nc.tensor.matmul(ps[:, X0, t * E:(t + 1) * E], h2t[:, k, t * P:(t + 1) * P],
                                                   sn[:, k, :], start=(k == 0), stop=(k == KC - 1))
                    ins.then_inc(logits_mm, 1)

                def qk_transposes(i, p, t):
                    pe.wait_ge(moe_acc, upto(i, p, STEPS, (t + 1) * E))
                    wait(pe, qk_ready, upto(i, p, TT, t))
                    nc.tensor.transpose(ps[:, QK_BANK, 0:P], acc[:, t % 2, 0:H], ident[:])
                    nc.tensor.transpose(ps[:, QK_BANK, P:2 * P], acc[:, t % 2, H:2 * H], ident[:]).then_inc(qk_mm, 1)

                def max_piece(n):
                    g, t = divmod(n, TT)
                    if n == 0:
                        pe.wait_ge(q_hi_ready, 1)
                    pe.wait_ge(k_hi_ready, g + 1)
                    if n >= 2:
                        pe.wait_ge(max_red, n - 1)
                    nc.tensor.matmul(ps[:, X0 + n % 2, :], q_hi[:, 0, t * P:(t + 1) * P], k_hi[:, g * BT:(g + 1) * BT],
                                     start=True, stop=True).then_inc(max_mm, 1)

                pe.wait_ge(col_ss, 1)
                for k in range(1, 3):
                    next_power(k)
                pe.wait_ge(mod_copied, 1)
                n2_transposes(0, 0)
                for k in range(3, 6):
                    next_power(k)
                pe.wait_ge(win_free, 1)
                for f in range(2 * FI):
                    project(f, 0, 0)
                for k in range(6, SCAN):
                    next_power(k)
                input_term(0, 0)
                pe.wait_ge(bu_ready, 1)
                n2_transposes(0, 1)
                pe.wait_ge(pow_ready, SCAN)
                for k in range(SCAN):
                    scan_piece(k, 0, 0, first=True)
                pe.wait_ge(parts_ready, 1)
                pe.wait_ge(wout_ready, 1)
                y_piece(0, 0, 2)
                out_piece(0, 0)
                for f in range(2 * FI):
                    project(f, 0, 1)
                h2_transposes(0, 0)
                pe.wait_ge(sn_ready, 1)
                logits_piece(0, 0)
                input_term(0, 1)
                pe.wait_ge(w_lo_ready, E)

                def slot(i, p, ahead):
                    c, a = following(i, p), (i + 1, p)
                    pe.wait_ge(xlo_ready, upto(i, p, 1, 1))
                    for s in range(STEPS):
                        t, e = divmod(s, E)
                        wait(pe, moe_acc, upto(i, p, STEPS, s - MOE_BANKS + 1))
                        rows = slice(t * P, (t + 1) * P)
                        for k in range(KC):
                            for n, (x_part, w_part) in enumerate(((xt_hi, w_hi), (xt_hi, w_lo), (xt_lo, w_hi))):
                                ins = nc.tensor.matmul(
                                    ps[:, s % MOE_BANKS, 0:H3], x_part[p][:, k, rows],
                                    w_part[:, k, e].rearrange("p t h -> p (t h)"),
                                    start=(k == 0 and n == 0), stop=(k == KC - 1 and n == 2))
                        ins.then_inc(moe_mm, 1)
                        if e == 3 and t:
                            qk_transposes(i, p, t - 1)
                        if ahead:
                            if s == 0:
                                carry_piece(*c)
                            if s in SCAN_AT:
                                scan_piece(SCAN_AT[s], *c)
                            if s == PE_Y:
                                y_piece(*c, ahead)
                            if s == PE_OUT:
                                out_piece(*c)
                            if s == PE_TRANSPOSE_H2:
                                h2_transposes(*c)
                            if s == PE_LOGITS:
                                logits_piece(*c)
                        if ahead >= 2:
                            if s == PE_TRANSPOSE_N2:
                                n2_transposes(*a)
                            if PE_PROJECT <= s < PE_PROJECT + 2 * FI:
                                project(s - PE_PROJECT, *a)
                            if s == PE_BU:
                                input_term(*a)
                        if not ahead and s >= MAX_FROM and (s - MAX_FROM) % 2 == 0 and (s - MAX_FROM) // 2 < MAX_EARLY:
                            max_piece((s - MAX_FROM) // 2)
                    qk_transposes(i, p, TT - 1)

                slots(pe, slot)
        one.close()

        three = whole.enter_context(ExitStack())
        sb = alloc(three)
        k_lo = sb("k_lo", [P, N], F32R)
        v_hi = sb("v_hi", [P, NT, H], F32R)
        v_lo = sb("v_lo", [P, NT, H], F32R)
        o_hi = sb("o_hi", [P, E, C], F32R)
        o_lo = sb("o_lo", [P, E, C], F32R)
        o_stage = k_t.rearrange("p (e c) -> p e c", e=E)
        PB = 3
        pf = sb("pf", [P, PB, BT])
        p_hi = sb("p_hi", [P, PB, BT], F32R)
        p_lo = sb("p_lo", [P, PB, BT], F32R)
        p_sum = carve([2, BT], at=2 * N + 2 * BT)
        ot_hi = sb("ot_hi", [P, 2, BT], F32R)
        ot_lo = sb("ot_lo", [P, 2, BT], F32R)
        neg_max = sb("neg_max", [P, TT])
        neg_row = sb("neg_row", [1, 2, BT], F32R)
        w_out_s = sb("w_out_s", [P, 2, TT, E])
        y = carve([2, C], at=2 * N + 4 * BT)
        yo = carve([2, C], at=2 * N + 4 * BT + 2 * C)
        x2b = sb("x2b", [P, TT, C])

        o_in = sem("o_in")
        k_lo_ready = sem("k_lo_ready")
        v_hi_ready = sem("v_hi_ready")
        v_lo_ready = sem("v_lo_ready")
        o_hi_ready = sem("o_hi_ready")
        o_lo_ready = sem("o_lo_ready")
        q_lo_ready = sem("q_lo_ready")
        neg_max_ready = sem("neg_max_ready")
        neg_mm = sem("neg_mm")
        neg_row_ready = sem("neg_row_ready")
        s_mm = sem("s_mm")
        pf_ready = sem("pf_ready")
        p_hi_ready = sem("p_hi_ready")
        p_lo_ready = sem("p_lo_ready")
        p_summed = sem("p_summed")
        pv_mm = sem("pv_mm")
        sum_mm = sem("sum_mm")
        inv_sum_ready = sem("inv_sum_ready")
        w_out_ready = sem("w_out_ready")
        ot_hi_ready = sem("ot_hi_ready")
        ot_lo_ready = sem("ot_lo_ready")
        o_mm = sem("o_mm")
        y_acc = sem("y_acc")
        yo_ready = sem("yo_ready")
        yo_scaled = sem("yo_scaled")
        x2_in = sem("x2_in")
        out_done = [sem("out_done0"), sem("out_done1")]

        S_BANK, MAX_BANK, O_BANK, Y_BANK, NEG_BANK = 0, 2, 3, 5, 7
        O_FROM = 2 * NB
        LAG = 2
        PAIRS = E // 2
        assert TT * PAIRS == NT and TT * KG == NT

        def before(i, p):
            return (i - 1, 1) if p == 0 else (i, 0)

        def cycle(eng, start, body, finish):
            start()
            body(0, 0, True, False)
            body(0, 1, False, False)
            with eng.Fori(1, NB // 2 - 1) as i:
                body(i, 0, False, False)
                body(i, 1, False, False)
            body(NB // 2 - 1, 0, False, False)
            body(NB // 2 - 1, 1, False, True)
            finish()

        with nc.Block() as block:
            @block.sync
            def _(sp):
                sp.wait_ge(k_lo_ready, NB)
                sp.dma_start(o_stage, o_proj.rearrange("e h c -> h e c")).then_inc(o_in, 16)
                ov = tok_view(out)

                def outputs(i, p):
                    wait(sp, yo_ready, upto(i, p, TT, 0))
                    sp.dma_start(x2b[:], tok_view(x2_dram)[:, tiles(i, p, 0, TT), :]).then_inc(x2_in, 16)
                    for t in range(TT):
                        sp.wait_ge(yo_ready, upto(i, p, TT, t + 1))
                        sp.dma_start(ov[:, tiles(i, p, t), :], yo[:, t % 2:t % 2 + 1, :]).then_inc(out_done[t % 2], 16)

                outputs(0, 0)
                outputs(0, 1)
                with sp.Fori(1, NB // 2) as i:
                    outputs(i, 0)
                    outputs(i, 1)
                for n in range(2):
                    sp.wait_ge(out_done[n], 16 * NB * TT // 2)

            @block.gpsimd
            def _(pool):
                def finish_tile(i, p, t):
                    pool.wait_ge(y_acc, upto(i, p, TT * E, (t + 1) * E))
                    wait(pool, out_done[t % 2], upto(i, p, 16 * TT // 2, 16 * (t // 2)))
                    nc.gpsimd.tensor_tensor(yo[:, t % 2], y[:, t % 2], modv[:, 5], ALU.mult).then_inc(yo_scaled, 1)
                    if t == 0:
                        pool.wait_ge(x2_in, upto(i, p, 16, 16))
                    pool.wait_ge(yo_scaled, upto(i, p, TT, t + 1))
                    nc.gpsimd.tensor_tensor(yo[:, t % 2], yo[:, t % 2], x2b[:, t], ALU.add).then_inc(yo_ready, 1)

                def body(i, p, first, last):
                    for j in range(NT):
                        pool.wait_ge(pf_ready, upto(i, p, NT, j + 1))
                        if j == 0:
                            wait(pool, sum_mm, upto(i, p, 1, -1))
                            apart(pool)
                            nc.gpsimd.tensor_copy(p_sum[:, p], pf[:, 0]).then_inc(p_summed, 1)
                        else:
                            pool.wait_ge(p_summed, upto(i, p, NT, j))
                            nc.gpsimd.tensor_tensor(p_sum[:, p], p_sum[:, p], pf[:, j % PB], ALU.add
                                                    ).then_inc(p_summed, 1)
                        if not first and j % PAIRS == LAG + 1 and j >= PAIRS:
                            finish_tile(*before(i, p), j // PAIRS - 1)
                    if not first:
                        finish_tile(*before(i, p), TT - 1)

                def finish():
                    for t in range(TT):
                        finish_tile(NB // 2 - 1, 1, t)

                cycle(pool, lambda: None, body, finish)

            @block.scalar
            def _(act):
                def load_q(i, p):
                    act.wait_ge(q_lo_ready, upto(i, p, 1, -1))
                    act.dma_start(q_st[:, p], qk_dram[:, 0, bass.ds(i * (2 * BT) + p * BT, BT)]).then_inc(q_in, 16)

                def split_q(i, p):
                    act.wait_ge(q_in, upto(i, p, 16, 16))
                    nc.scalar.copy(q_hi[:, p], q_st[:, p]).then_inc(q_hi_ready, 1)

                def split_v(g):
                    act.wait_ge(kv_in[g], 32)
                    nc.scalar.copy(v_hi[:, g * TT:(g + 1) * TT], v_all[:, g * TT:(g + 1) * TT]).then_inc(v_hi_ready, 1)

                def max_row(i, p):
                    act.wait_ge(neg_mm, upto(i, p, 1, 1))
                    nc.scalar.copy(neg_row[:, p], ps[0:1, NEG_BANK, :]).then_inc(neg_row_ready, 1)

                def start():
                    last_keys = slice(N - BT, N)
                    act.wait_ge(kv_in[NB - 1], 32)
                    nc.scalar.copy(k_hi[:, last_keys], k_t[:, last_keys]).then_inc(k_hi_ready, 1)
                    split_q(0, 1)
                    split_v(0)
                    split_v(1)
                    max_row(0, 0)

                def body(i, p, first, last):
                    more = not last and not (isinstance(i, int) and i == NB // 2 - 1)
                    for j in range(NT):
                        if more and j == PB:
                            load_q(i + 1, p)
                        if first and j % 2 == 1 and j // 2 < NB - 2:
                            split_v(j // 2 + 2)
                        if first and j == O_FROM:
                            act.wait_ge(o_in, 16)
                        if first and O_FROM <= j < O_FROM + E // 2:
                            pair = slice(2 * (j - O_FROM), 2 * (j - O_FROM) + 2)
                            nc.scalar.copy(o_hi[:, pair], o_stage[:, pair]).then_inc(o_hi_ready, 1)
                        act.wait_ge(s_mm, upto(i, p, NT, j + 1))
                        wait(act, p_summed, upto(i, p, NT, j - PB + 1))
                        wait(act, p_lo_ready, upto(i, p, NT, j - PB + 1))
                        wait(act, pv_mm, upto(i, p, NT, j - PB + 1))
                        buf = j % PB
                        nc.scalar.activation(pf[:, buf], ps[:, S_BANK + j % 2, :], ACT.Exp, scale=SCALE
                                             ).then_inc(pf_ready, 1)
                        nc.scalar.activation(p_hi[:, buf], ps[:, S_BANK + j % 2, :], ACT.Exp, scale=SCALE
                                             ).then_inc(p_hi_ready, 1)
                    if not last:
                        max_row(*following(i, p))
                    act.wait_ge(pv_mm, upto(i, p, NT, NT))
                    wait(act, o_mm, upto(i, p, NT, -NT))
                    nc.scalar.copy(ot_hi[:, p], ps[:, O_BANK + p, :]).then_inc(ot_hi_ready, 1)
                    if more:
                        split_q(i + 1, p)

                cycle(act, start, body, lambda: None)

            @block.vector
            def _(dve):
                def split_q(i, p):
                    dve.wait_ge(q_hi_ready, upto(i, p, 1, 1))
                    nc.vector.tensor_tensor(q_lo[:, p], q_st[:, p], q_hi[:, p].bitcast(F32), ALU.subtract
                                            ).then_inc(q_lo_ready, 1)

                def low_k(g):
                    dve.wait_ge(k_hi_ready, g + 1)
                    keys = slice(g * BT, (g + 1) * BT)
                    nc.vector.tensor_tensor(k_lo[:, keys], k_t[:, keys], k_hi[:, keys].bitcast(F32), ALU.subtract
                                            ).then_inc(k_lo_ready, 1)

                def low_v(g):
                    dve.wait_ge(v_hi_ready, g + 1)
                    keys = slice(g * TT, (g + 1) * TT)
                    nc.vector.tensor_tensor(v_lo[:, keys], v_all[:, keys], v_hi[:, keys].bitcast(F32), ALU.subtract
                                            ).then_inc(v_lo_ready, 1)

                def low_o(n):
                    dve.wait_ge(o_hi_ready, n + 1)
                    pair = slice(2 * n, 2 * n + 2)
                    nc.vector.tensor_tensor(o_lo[:, pair], o_stage[:, pair], o_hi[:, pair].bitcast(F32), ALU.subtract
                                            ).then_inc(o_lo_ready, 1)

                def max_piece(i, p, j):
                    dve.wait_ge(max_mm, upto(i, p, NT, j + 1))
                    t, g = divmod(j, KG)
                    nc.vector.tensor_reduce(mx[:, t, g:g + 1], ps[:, MAX_BANK, :], AX_X, ALU.max
                                            ).then_inc(max_red, 1)

                def max_all(i, p):
                    dve.wait_ge(max_red, upto(i, p, NT, NT))
                    wait(dve, neg_mm, upto(i, p, 1, 0))
                    nc.vector.tensor_reduce(neg_max[:], mx[:], AX_X, ALU.max, negate=True).then_inc(neg_max_ready, 1)

                def start():
                    split_q(0, 0)
                    low_k(0)
                    for t in range(TT):
                        dve.wait_ge(max_mm, NT - TT + t + 1)
                        nc.vector.tensor_reduce(mx[:, t, KG - 1:KG], ps[:, MAX_BANK + t, :], AX_X, ALU.max
                                                ).then_inc(max_red, 1)
                    max_all(0, 0)
                    split_q(0, 1)
                    low_v(0)

                def low_part(i, p, j):
                    dve.wait_ge(p_hi_ready, upto(i, p, NT, j + 1))
                    wait(dve, pv_mm, upto(i, p, NT, j - PB + 1))
                    nc.vector.tensor_tensor(p_lo[:, j % PB], pf[:, j % PB], p_hi[:, j % PB].bitcast(F32),
                                            ALU.subtract).then_inc(p_lo_ready, 1)

                def accumulate(i, p, j):
                    t, pair = divmod(j, PAIRS)
                    dve.wait_ge(o_mm, upto(i, p, NT, j + 1))
                    for n in range(2):
                        e = 2 * pair + n
                        src, w = ps[:, Y_BANK + j % 2, n * C:(n + 1) * C], w_out_s[:, p, t, e:e + 1]
                        if e == 0:
                            wait(dve, yo_ready, upto(i, p, TT, t - 1))
                            nc.vector.tensor_scalar(y[:, t % 2], src, w, None, ALU.mult).then_inc(y_acc, 1)
                        else:
                            dve.wait_ge(y_acc, upto(i, p, TT * E, t * E + e))
                            nc.vector.scalar_tensor_tensor(out=y[:, t % 2], in0=src, scalar=w, in1=y[:, t % 2],
                                                           op0=ALU.mult, op1=ALU.add).then_inc(y_acc, 1)

                def body(i, p, first, last):
                    for j in range(NT + LAG):
                        if first and j // 2 < NB - 1:
                            (low_v if j % 2 else low_k)(j // 2 + 1)
                        if first and O_FROM < j <= O_FROM + E // 2:
                            low_o(j - O_FROM - 1)
                        if 1 <= j <= NT:
                            low_part(i, p, j - 1)
                        if not last and j < NT:
                            max_piece(*following(i, p), j)
                        if not first and j >= LAG:
                            accumulate(*before(i, p), j - LAG)
                    if not last:
                        max_all(*following(i, p))
                    dve.wait_ge(sum_mm, upto(i, p, 1, 1))
                    nc.vector.reciprocal(inv_sum[:, :, 0], ps[:, MAX_BANK, 0:TT]).then_inc(inv_sum_ready, 1)
                    dve.wait_ge(inv_sum_ready, upto(i, p, 1, 1))
                    nc.vector.tensor_tensor(w_out_s[:, p], w_all[:, tiles(i, p, 0, TT), :],
                                            inv_sum[:].to_broadcast([P, TT, E]), ALU.mult).then_inc(w_out_ready, 1)
                    dve.wait_ge(ot_hi_ready, upto(i, p, 1, 1))
                    nc.vector.tensor_tensor(ot_lo[:, p], ps[:, O_BANK + p, :], ot_hi[:, p].bitcast(F32),
                                            ALU.subtract).then_inc(ot_lo_ready, 1)
                    dve.wait_ge(w_out_ready, upto(i, p, 1, 1))
                    if not last and not (isinstance(i, int) and i == NB // 2 - 1):
                        split_q(i + 1, p)

                def finish():
                    for j in range(NT):
                        accumulate(NB // 2 - 1, 1, j)

                cycle(dve, start, body, finish)

            @block.tensor
            def _(pe):
                def max_piece(i, p, j):
                    t, g = divmod(j, KG)
                    if j == 0:
                        pe.wait_ge(q_hi_ready, upto(i, p, 1, 1))
                        wait(pe, inv_sum_ready, upto(i, p, 1, -1))
                    wait(pe, max_red, upto(i, p, NT, j))
                    nc.tensor.matmul(ps[:, MAX_BANK, :], q_hi[:, p, t * P:(t + 1) * P], k_hi[:, g * BT:(g + 1) * BT],
                                     start=True, stop=True).then_inc(max_mm, 1)

                def max_transposes(i, p):
                    pe.wait_ge(neg_max_ready, upto(i, p, 1, 1))
                    wait(pe, neg_row_ready, upto(i, p, 1, 0))
                    for t in range(TT):
                        ins = nc.tensor.transpose(ps[0:1, NEG_BANK, t * P:(t + 1) * P], neg_max[:, t:t + 1], ident[:])
                    ins.then_inc(neg_mm, 1)

                def scores(i, p, j):
                    if j == 0:
                        pe.wait_ge(q_lo_ready, upto(i, p, 1, 1))
                        pe.wait_ge(neg_row_ready, upto(i, p, 1, 1))
                    wait(pe, p_hi_ready, upto(i, p, NT, j - 1))
                    keys, dst = slice(j * P, (j + 1) * P), ps[:, S_BANK + j % 2, :]
                    nc.tensor.matmul(dst, k_hi[:, keys], q_hi[:, p], start=True, stop=False)
                    nc.tensor.matmul(dst, k_hi[:, keys], q_lo[:, p], start=False, stop=False)
                    nc.tensor.matmul(dst, k_lo[:, keys], q_hi[:, p], start=False, stop=False)
                    nc.tensor.matmul(dst, ones_r[:], neg_row[:, p], start=False, stop=True).then_inc(s_mm, 1)

                def values(i, p, j):
                    if j == 0:
                        wait(pe, ot_lo_ready, upto(i, p, 1, -1))
                    pe.wait_ge(p_lo_ready, upto(i, p, NT, j + 1))
                    dst, buf = ps[:, O_BANK + p, :], j % PB
                    nc.tensor.matmul(dst, v_hi[:, j], p_hi[:, buf], start=(j == 0), stop=False)
                    nc.tensor.matmul(dst, v_lo[:, j], p_hi[:, buf], start=False, stop=False)
                    nc.tensor.matmul(dst, v_hi[:, j], p_lo[:, buf], start=False, stop=(j == NT - 1)).then_inc(pv_mm, 1)

                def project(i, p, j):
                    t, pair = divmod(j, PAIRS)
                    if j == 0:
                        pe.wait_ge(ot_lo_ready, upto(i, p, 1, 1))
                        pe.wait_ge(w_out_ready, upto(i, p, 1, 1))
                    wait(pe, y_acc, upto(i, p, TT * E, 2 * (j - 1)))
                    rows, dst = slice(t * P, (t + 1) * P), ps[:, Y_BANK + j % 2, :]
                    for n, (a, b) in enumerate(((ot_hi, o_hi), (ot_hi, o_lo), (ot_lo, o_hi))):
                        ins = nc.tensor.matmul(dst, a[:, p, rows],
                                               b[:, 2 * pair:2 * pair + 2].rearrange("p e c -> p (e c)"),
                                               start=(n == 0), stop=(n == 2))
                    ins.then_inc(o_mm, 1)

                def start():
                    pe.wait_ge(k_hi_ready, NB)
                    for t in range(TT):
                        nc.tensor.matmul(ps[:, MAX_BANK + t, :], q_hi[:, 0, t * P:(t + 1) * P], k_hi[:, N - BT:],
                                         start=True, stop=True).then_inc(max_mm, 1)
                    max_transposes(0, 0)

                def body(i, p, first, last):
                    for j in range(NT + LAG):
                        if first and j % TT == 0 and j < NT:
                            pe.wait_ge(k_lo_ready, j // TT + 1)
                        if first and j % TT == LAG:
                            pe.wait_ge(v_lo_ready, j // TT + 1)
                        if j < NT:
                            scores(i, p, j)
                        if not last and j < NT:
                            max_piece(*following(i, p), j)
                        if not first and j >= LAG:
                            project(*before(i, p), j - LAG)
                        if j >= LAG:
                            values(i, p, j - LAG)
                    if not last:
                        max_transposes(*following(i, p))
                        pe.wait_ge(max_red, upto(*following(i, p), NT, NT))
                    pe.wait_ge(p_summed, upto(i, p, NT, NT))
                    for t in range(TT):
                        ins = nc.tensor.matmul(ps[:, MAX_BANK, t:t + 1], p_sum[:, p, t * P:(t + 1) * P],
                                               ones_f[:, 0:1], start=True, stop=True)
                    ins.then_inc(sum_mm, 1)
                    if first:
                        pe.wait_ge(o_lo_ready, E // 2)

                def finish():
                    for j in range(NT):
                        project(NB // 2 - 1, 1, j)

                cycle(pe, start, body, finish)


def kernel(**inputs):
    import numpy as np
    import concourse.bacc as bacc
    from concourse.bass_utils import run_bass_kernel_spmd

    a = {name[3:]: np.asarray(value) for name, value in inputs.items()}
    n, c = a["attn_x"].shape[1:]
    by_column = lambda v: v.reshape(-1, 128).T
    laid = {
        "x": a["attn_x"].reshape(n, c), "ln_w": by_column(a["attn_ln_w"]),
        "ln_b": by_column(a["attn_ln_b"]), "w_in": a["attn_W_in"],
        "conv_w": a["attn_conv_w"], "a_mat": a["attn_A"], "a_mat_t": a["attn_A"].T, "bm_t": a["attn_Bm"].T,
        "cm_t": a["attn_Cm"].T, "w_out": a["attn_W_out"], "sim": a["ffn_sim_matrix"], "gates": a["ffn_gates"],
        "q_proj": a["ffn_q_proj"], "k_proj": a["ffn_k_proj"], "v_proj": a["ffn_v_proj"],
        "o_proj": a["ffn_o_proj"], "cond": by_column(a["c"]), "wmod": a["wmod"],
    }
    nc = bacc.Bacc("TRN2", target_bir_lowering=False, num_devices=1)
    arrays, args = {}, []
    for name, value in laid.items():
        arrays["in_" + name] = np.ascontiguousarray(value)
        args.append(nc.dram_tensor("in_" + name, value.shape, mybir.dt.from_np(value.dtype), kind="ExternalInput").ap())
    out = nc.dram_tensor("out_x", (n, c), F32, kind="ExternalOutput").ap()
    adaln_block_kernel(nc, *args, out)
    r = run_bass_kernel_spmd(nc, [arrays], core_ids=[0])
    return r.results[0]["out_x"].reshape(1, n, c)
```

```python
from contextlib import ExitStack

import concourse.bass as bass
from concourse import mybir

F32 = mybir.dt.float32
F32R = mybir.dt.float32r
ALU = mybir.AluOpType
ACT = mybir.ActivationFunctionType
AX_X = mybir.AxisListType.X


def adaln_block_kernel(nc, x, ln_w, ln_b, w_in, conv_w, a_mat, a_mat_t, bm_t, cm_t, w_out,
                       sim, gates, q_proj, k_proj, v_proj, o_proj, cond, wmod, out):
    P = 128
    N, C = x.shape
    KC = C // P
    INNER = w_in.shape[1] // 2
    FI = INNER // P
    S = a_mat.shape[0]
    TAPS = conv_w.shape[1]
    E, _, H = q_proj.shape
    BT = 512
    TT = BT // P
    NB = N // BT
    NT = N // P
    KG = N // BT
    H3 = 3 * H
    SCALE = float(H) ** -0.5
    assert NB * S == P and NB % 2 == 0 and NB >= 4 and FI == 3 and KC == 2 and TT == 4 and E == 16
    assert H == P

    GT = BT * S // P
    SCAN = BT.bit_length() - 1
    X2_COLS = TT * C

    x2_dram = nc.dram_tensor("x2_scratch", (N, C), F32).ap()
    qk_dram = nc.dram_tensor("qk_scratch", (P, 2, N), F32).ap()
    v_dram = nc.dram_tensor("v_scratch", (N, H), F32).ap()
    bu_dram = nc.dram_tensor("bu_scratch", (NB, P, GT), F32).ap()
    st_dram = nc.dram_tensor("state_scratch", (2, NB, P, GT), F32).ap()

    def tok_view(ap):
        return ap.rearrange("(n p) c -> p n c", p=P)

    def upto(i, p, per, k=0):
        return i * (2 * per) + (p * per + k)

    def wait(eng, sem, value):
        if not isinstance(value, int) or value > 0:
            eng.wait_ge(sem, value)

    class Link:

        def __init__(self, eng, sem, per):
            self.eng, self.sem, self.per, self.n, self.base = eng, sem, per, 0, 0

        def block(self, i, p):
            assert self.n in (0, self.per), (self.sem, self.n)
            self.n, self.base = 0, upto(i, p, self.per)

        def done(self, ins):
            ins.then_inc(self.sem, 1)
            self.n += 1

        def wait(self):
            self.eng.wait_ge(self.sem, self.base + self.n)

    def slots(eng, body):
        body(0, 0, 2)
        body(0, 1, 2)
        with eng.Fori(1, NB // 2 - 1) as i:
            body(i, 0, 2)
            body(i, 1, 2)
        body(NB // 2 - 1, 0, 1)
        body(NB // 2 - 1, 1, 0)

    def following(i, p):
        return (i, 1) if p == 0 else (i + 1, 0)

    def before(i, p):
        return (i - 1, 1) if p == 0 else (i, 0)

    nc.disable_value_cache = True

    with ExitStack() as whole:
        def alloc(stack):
            def sb(name, shape, dt=F32):
                return stack.enter_context(nc.sbuf_tensor(name, shape, dt))
            return sb

        def sem(name):
            return whole.enter_context(nc.semaphore(name))

        sb = alloc(whole)
        ident = sb("ident", [P, P])
        ones_f = sb("ones_f", [P, P])
        ones_r = sb("ones_r", [1, P], F32R)
        modv = sb("modv", [P, 6, C])
        w_all = sb("w_all", [P, NT, E])
        inv_sum = sb("inv_sum", [P, TT, 1])
        mx = sb("mx", [P, TT, KG])
        ps = whole.enter_context(nc.psum_tensor("ps", [P, 8, 512], F32))

        memory = sb("memory", [P, 11 * C * TT + 768])
        taken = [0]

        def carve(shape, at=None):
            n = 1
            for d in shape:
                n *= d
            start = taken[0] if at is None else at
            taken[0] = max(taken[0], start + n)
            assert taken[0] <= memory.shape[1]
            flat = memory[:, start:start + n]
            if len(shape) == 1:
                return flat
            if len(shape) == 2:
                return flat.rearrange("p (a b) -> p a b", b=shape[1])
            return flat.rearrange("p (a b c) -> p a b c", b=shape[1], c=shape[2])

        k_t = carve([N])
        v_all = carve([NT, H])
        q_st = carve([2, BT])
        taken[0] = 0
        xt = carve([TT, C])
        hb = carve([TT, C])
        sg = carve([FI, BT])
        n2 = carve([TT, C], at=2 * X2_COLS)
        ht = carve([KC, BT], at=3 * X2_COLS)
        h2 = carve([TT, C])
        x2 = carve([TT, C])
        gy = carve([FI, BT])
        h2t = carve([KC, BT])
        wmod_at = taken[0]
        data = carve([FI, BT + TAPS - 1])
        cv = carve([FI, BT])
        wmod_ld = carve([KC, 6 * C], at=wmod_at)
        win = carve([KC, 2 * INNER], at=5 * X2_COLS)
        cm_ld = carve([INNER], at=4 * X2_COLS)[0:3 * S]
        c_bc = carve([KC, P], at=4 * X2_COLS + INNER)
        simt = carve([KC, E], at=4 * X2_COLS + INNER + KC * P)
        powers_t = carve([2, P], at=4 * X2_COLS + INNER + KC * P + KC * E)
        w_third = carve([KC, 3, H], at=6 * X2_COLS + FI * BT)
        assert 2 * N <= taken[0]

        memory_r = sb("memory_r", [P, 4 * INNER * KC + 4 * KC * BT], F32R)
        WIN_COLS, XT_COLS = KC * 2 * INNER, KC * BT
        win_hi = memory_r[:, 0:WIN_COLS].rearrange("p (k n) -> p k n", k=KC)
        win_lo = memory_r[:, WIN_COLS:2 * WIN_COLS].rearrange("p (k n) -> p k n", k=KC)
        xt_parts = memory_r[:, 2 * WIN_COLS:].rearrange("p (q l k n) -> p q l k n", q=2, l=2, k=KC)
        xt_hi = [xt_parts[:, q, 0] for q in range(2)]
        xt_lo = [xt_parts[:, q, 1] for q in range(2)]
        k_hi = memory_r[:, 0:N]
        q_hi = memory_r[:, N:N + 2 * BT].rearrange("p (q n) -> p q n", q=2)
        q_lo = memory_r[:, N + 2 * BT:N + 4 * BT].rearrange("p (q n) -> p q n", q=2)
        assert N + 2 * BT <= 2 * WIN_COLS + 2 * XT_COLS

        one = whole.enter_context(ExitStack())
        sb = alloc(one)
        w_hi = sb("w_hi", [P, KC, E, 3, H], F32R)
        w_lo = sb("w_lo", [P, KC, E, 3, H], F32R)
        wst = sb("wst", [P, 2, KC, 3, H])
        pad = 4 * S
        powers = sb("powers", [P, SCAN, pad + P])
        wrap = sb("wrap", [P, P])
        minus_half = sb("minus_half", [P, TT])
        eps = sb("eps", [P, TT])
        sn = sb("sn", [P, KC, E])
        sim_sq = sb("sim_sq", [P, KC, E])
        sig_gates = sb("sig_gates", [P, E])
        col_inv = sb("col_inv", [P, E])
        half_e = sb("half_e", [P, E])
        wout = sb("wout", [P, FI, C])
        cm_parts = sb("cm_parts", [3 * S, INNER], F32R)
        rank = sb("rank", [P, TT, E])
        c_col = sb("c_col", [P, KC])
        c_sig = sb("c_sig", [P, KC])
        lnw = sb("lnw", [P, KC])
        lnb = sb("lnb", [P, KC])
        cw = sb("cw", [P, FI, TAPS])
        bmt = sb("bmt", [P, FI, S])
        bst = sb("bst", [P, 3, TT, 6])
        mv = sb("mv", [P, 3, TT, 2])
        var_eps = sb("var_eps", [P, 3, TT])
        rs = sb("rs", [P, 3, TT])
        sumsq = sb("sumsq", [P, TT])
        inv_norm = sb("inv_norm", [P, TT])
        scan_s = [sb("scan_a", [P, GT]), sb("scan_b", [P, GT])]
        carry = sb("carry", [P, 1])
        s_parts = sb("s_parts", [P, 2, GT], F32R)
        st_parts = sb("st_parts", [3 * S, BT], F32R)
        bu = sb("bu", [S, BT])
        w_staged = [wst[:, 0], wst[:, 1], w_third]
        w_stage = wst[:].rearrange("p a k t h -> p (a k t h)")
        acc = w_stage[:, 0:2 * H3].rearrange("p (a n) -> p a n", a=2)
        qk_st = w_stage[:, 2 * H3:2 * H3 + 4 * P].rearrange("p (a b n) -> p a b n", a=2, b=2)
        w_cur = sb("w_cur", [P, 2, TT, E])
        lg = sb("lg", [P, TT, E])
        gated = sb("gated", [P, TT, E])
        hard = sb("hard", [P, TT, E])
        pick = sb("pick", [P, TT, E])
        first_hot = sb("first_hot", [P, TT, E])
        lg_rest = sb("lg_rest", [P, TT, E])
        shifted = sb("shifted", [P, TT, E])
        g_max = sb("g_max", [P, TT, 1])
        top = sb("top", [P, TT, 1])
        inactive = sb("inactive", [P, TT, 1])
        w_sum = sb("w_sum", [P, TT, 1])
        g_tmp = w_all[:].rearrange("p n e -> p (n e)").rearrange("p (g c) -> p g c", g=2)

        carriers = sem("carriers")
        params_in = sem("params_in")
        zeroed = sem("zeroed")
        a_in = sem("a_in")
        x_in = sem("x_in")
        cond_in = sem("cond_in")
        wmod_in = sem("wmod_in")
        w_in_sem = [sem(f"w_in{n}") for n in range(3)]
        w_hi_ready = sem("w_hi_ready")
        w_lo_ready = sem("w_lo_ready")
        pool_const = sem("pool_const")
        sig_ready = sem("sig_ready")
        win_hi_ready = sem("win_hi_ready")
        cm_hi_ready = sem("cm_hi_ready")
        pre_dve = sem("pre_dve")
        sn_ready = sem("sn_ready")
        wout_ready = sem("wout_ready")
        col_inv_ready = sem("col_inv_ready")
        mod_mm = sem("mod_mm")
        mod_copied = sem("mod_copied")
        mod_ready = sem("mod_ready")
        parts_ready = sem("parts_ready")
        colnorm_mm = sem("colnorm_mm")
        col_ss = sem("col_ss")
        pow_mm = sem("pow_mm")
        pow_ready = sem("pow_ready")
        dve_a = sem("dve_a")
        pool_a = sem("pool_a")
        mv_ready = sem("mv_ready")
        rs_ready = sem("rs_ready")
        n2_ready = sem("n2_ready")
        n2_transposed = sem("n2_transposed")
        ht_ready = sem("ht_ready")
        ht_lo_ready = sem("ht_lo_ready")
        proj_mm = sem("proj_mm")
        proj_evac = sem("proj_evac")
        conv_link = sem("conv_link")
        conv_ready = sem("conv_ready")
        halo_ready = sem("halo_ready")
        csig_ready = sem("csig_ready")
        u_ready = sem("u_ready")
        r_ready = sem("r_ready")
        bu_mm = sem("bu_mm")
        bu_ready = sem("bu_ready")
        bu_out = sem("bu_out")
        scan_in = sem("scan_in")
        carry_mm = sem("carry_mm")
        carry_added = sem("carry_added")
        scan_mm = sem("scan_mm")
        scan_add = sem("scan_add")
        s_hi_ready = sem("s_hi_ready")
        s_parts_ready = sem("s_parts_ready")
        st_out = sem("st_out")
        st_in = sem("st_in")
        x2_out = sem("x2_out")
        y_mm = sem("y_mm")
        gy_ready = sem("gy_ready")
        out_mm = sem("out_mm")
        x2_ready = sem("x2_ready")
        h2_ready = sem("h2_ready")
        pool_b = sem("pool_b")
        mv2_ready = sem("mv2_ready")
        rs2_ready = sem("rs2_ready")
        sumsq_ready = sem("sumsq_ready")
        inv_norm_ready = sem("inv_norm_ready")
        h2_transposed = sem("h2_transposed")
        h2t_ready = sem("h2t_ready")
        xlo_ready = sem("xlo_ready")
        logits_mm = sem("logits_mm")
        dve_b = sem("dve_b")
        shifted_ready = sem("shifted_ready")
        exp_ready = sem("exp_ready")
        w_ready = sem("w_ready")
        moe_mm = sem("moe_mm")
        moe_acc = sem("moe_acc")
        qk_mm = sem("qk_mm")
        qk_ready = sem("qk_ready")
        qk_out = [sem("qk_out0"), sem("qk_out1")]
        v_out = [sem("v_out0"), sem("v_out1")]
        kv_in = [sem(f"kv_in{g}") for g in range(NB)]
        q_in = sem("q_in")
        q_hi_ready = sem("q_hi_ready")
        k_hi_ready = sem("k_hi_ready")
        max_mm = sem("max_mm")
        max_red = sem("max_red")
        h_scaled = sem("h_scaled")
        win_free = sem("win_free")

        STEPS = TT * E
        MOE_BANKS, QK_BANK = 4, 7
        X0, X1, X2 = 4, 5, 6
        DVE_A, DVE_B, POOL_A, POOL_B = 4, 23, 2, 2
        DVE_ROUTE = 46
        N_PARAMS = 11
        W_STAGE = [e % 3 if e < E - 4 else e % 2 for e in range(E)]

        def w_user(e):
            return max([n for n in range(e) if W_STAGE[n] == W_STAGE[e]] + [-1])

        def w_arrived(eng, e):
            eng.wait_ge(w_in_sem[W_STAGE[e]], 16 * 3 * (W_STAGE[:e].count(W_STAGE[e]) + 1))
        MAX_FROM, MAX_EARLY = 6, TT * (KG - 1)
        SCAN_AT = {1 + 2 * k: k for k in range(SCAN)}
        PE_TRANSPOSE_N2, PE_Y, PE_OUT, PE_PROJECT, PE_TRANSPOSE_H2, PE_LOGITS, PE_BU = 19, 24, 27, 31, 40, 44, 49
        DVE_PIECES = {
            0: ("carry", 0), 2: ("norm", 0), 6: ("norm", 1), 9: ("norm", 2), 12: ("norm", 3), 15: ("norm", 4),
            24: ("gate", 0), 29: ("x2", 0), 31: ("x2", 1), 33: ("x2", 2), 34: ("x2", 3), 37: ("x2", 4),
            35: ("conv", 0), 39: ("conv", 1),
        }

        def tiles(i, p, t=0, n=1):
            return bass.ds(i * (2 * TT) + p * TT + t, n)

        def apart(eng):
            eng.sem_inc(carriers, 1)

        def pw_m(k, shift=0):
            return powers[:, k, pad - S * shift:pad - S * shift + P]

        with nc.Block() as block:
            @block.sync
            def _(sp):
                xv = tok_view(x)
                sp.dma_start(c_col[:], cond).then_inc(cond_in, 16)
                sp.dma_start(xt, xv[:, 0:TT, :]).then_inc(x_in, 16)
                sp.dma_start(wmod_ld, wmod.rearrange("(k p) n -> p k n", p=P)).then_inc(wmod_in, 16)
                cm_rows = [(cm_ld[n * S:(n + 1) * S, :], cm_t) for n in range(3)]
                params = [
                    (lnw[:], ln_w),
                    (lnb[:], ln_b),
                    (win, w_in.rearrange("(k p) n -> p k n", p=P)),
                    (simt, sim.rearrange("(k p) e -> p k e", p=P)),
                    (sig_gates[:], gates.rearrange("(a e) -> a e", a=1).to_broadcast([P, E])),
                    (cw[:], conv_w.rearrange("(f p) j -> p f j", p=P)),
                    (bmt[:], bm_t.rearrange("(f p) s -> p f s", p=P)),
                    (wout[:], w_out.rearrange("(f p) n -> p f n", p=P)),
                ] + cm_rows
                assert len(params) == N_PARAMS
                for dst, src in params:
                    sp.dma_start(dst, src).then_inc(params_in, 16)
                sp.wait_ge(zeroed, 1)
                for g in range(NB):
                    rows = slice(S * g, S * g + S)
                    sp.dma_start(powers[rows, 0, pad + S * g:pad + S * g + S], a_mat_t).then_inc(a_in, 16)
                    sp.dma_start(powers_t[rows, 0, S * g:S * g + S], a_mat).then_inc(a_in, 16)

                def load_w(e0, e1):
                    for e in range(e0, e1):
                        wait(sp, w_lo_ready, w_user(e) + 1)
                        for t, proj in enumerate((q_proj, k_proj, v_proj)):
                            sp.dma_start(w_staged[W_STAGE[e]][:, :, t], proj[e].rearrange("(k p) h -> p k h", p=P)
                                         ).then_inc(w_in_sem[W_STAGE[e]], 16)

                def scan_load(i, p):
                    sp.wait_ge(bu_out, upto(i, p, 16, 16))
                    wait(sp, s_parts_ready, upto(i, p, 1, 0))
                    sp.dma_start(scan_s[0][:], bu_dram[bass.ds(i * 2 + p, 1)].rearrange("a p t -> p (a t)")
                                 ).then_inc(scan_in, 16)

                def states_round(i, p):
                    sp.wait_ge(s_parts_ready, upto(i, p, 1, 1))
                    for l in range(2):
                        sp.dma_start(st_dram[l, bass.ds(i * 2 + p, 1)].rearrange("a p t -> p (a t)"), s_parts[:, l].bitcast(F32)
                                     ).then_inc(st_out, 16)
                    sp.wait_ge(st_out, upto(i, p, 32, 32))
                    wait(sp, y_mm, upto(i, p, 1, 0))
                    for n, l in enumerate((0, 1, 0)):
                        sp.dma_start(st_parts[n * S:(n + 1) * S, :].bitcast(F32).rearrange("s (g t) -> s g t", g=NB),
                                     st_dram[l, bass.ds(i * 2 + p, 1)].rearrange("a (g s) t -> s (a g) t", s=S)
                                     ).then_inc(st_in, 16)

                def x2_store(i, p):
                    sp.wait_ge(x2_ready, upto(i, p, 1, 1))
                    sp.dma_start(tok_view(x2_dram)[:, tiles(i, p, 0, TT), :], x2).then_inc(x2_out, 16)

                def x_load(i, p):
                    sp.wait_ge(r_ready, upto(i, p, 1, 0))
                    sp.dma_start(xt, xv[:, tiles(i, p, 0, TT), :]).then_inc(x_in, 16)

                load_w(0, 6)
                x_load(0, 1)
                scan_load(0, 0)
                load_w(6, 9)
                states_round(0, 0)
                load_w(9, E)
                x2_store(0, 0)
                scan_load(0, 1)

                def slot(i, p, ahead):
                    if ahead >= 2:
                        x_load(i + 1, p)
                    if ahead >= 1:
                        states_round(*following(i, p))
                        x2_store(*following(i, p))
                    if ahead >= 2:
                        scan_load(i + 1, p)
                    if ahead == 0:
                        for g in range(NB - 1):
                            if g == 0:
                                sp.wait_ge(h2t_ready, NB)
                                sp.wait_ge(x2_out, 16 * NB)
                                sp.wait_ge(xlo_ready, NB)
                                sp.wait_ge(w_ready, NB)
                                sp.wait_ge(moe_mm, (NB - 1) * STEPS)
                                sp.wait_ge(u_ready, NB)
                                sp.wait_ge(bu_mm, NB)
                            for n in range(2):
                                sp.wait_ge(qk_out[n], 16 * (g + 1) * TT // 2)
                                sp.wait_ge(v_out[n], 16 * (g + 1) * TT // 2)
                            sp.dma_start(k_t[:, g * BT:(g + 1) * BT], qk_dram[:, 1, g * BT:(g + 1) * BT]
                                         ).then_inc(kv_in[g], 16)
                            sp.dma_start(v_all[:, g * TT:(g + 1) * TT, :],
                                         v_dram.rearrange("(n p) h -> p n h", p=P)[:, g * TT:(g + 1) * TT, :]
                                         ).then_inc(kv_in[g], 16)
                            if g == 0:
                                sp.dma_start(q_st[:, 0], qk_dram[:, 0, 0:BT]).then_inc(q_in, 16)
                            if g == NB // 2:
                                sp.wait_ge(q_hi_ready, 1)
                                sp.dma_start(q_st[:, 1], qk_dram[:, 0, BT:2 * BT]).then_inc(q_in, 16)

                slots(sp, slot)

            @block.gpsimd
            def _(pool):
                nc.gpsimd.memset(powers_t, 0.0)
                nc.gpsimd.memset(powers[:], 0.0).then_inc(zeroed, 1)
                nc.gpsimd.memset(minus_half[:], -0.5)
                nc.gpsimd.memset(half_e[:], -0.5)
                nc.gpsimd.memset(eps[:], 1e-5)
                nc.gpsimd.memset(ones_f[:], 1.0).then_inc(pool_const, 1)
                pool.wait_ge(pool_const, 1)
                nc.gpsimd.affine_select(out=ident[:], in_=ones_f[:], compare_op=ALU.is_equal, fill=0.0, base=0,
                                        pattern=[[1, P]], channel_multiplier=-1).then_inc(pool_const, 1)
                for e in range(E):
                    ins = nc.gpsimd.memset(rank[:, :, e], float(E - e))
                ins.then_inc(pool_const, 1)
                link_a, link_b = Link(pool, pool_a, POOL_A), Link(pool, pool_b, POOL_B)

                def inv_std(i, p, n):
                    pool.wait_ge(mv_ready, upto(i, p, 2, n + 1))
                    link_a.done(nc.gpsimd.tensor_tensor(var_eps[:, n], mv[:, n, :, 1], eps[:], ALU.add))
                    link_a.wait()
                    nc.gpsimd.tensor_tensor(rs[:, n], var_eps[:, n], minus_half[:], ALU.pow).then_inc(rs_ready, 1)

                def first_norms(i, p):
                    link_a.block(i, p)
                    inv_std(i, p, 0)
                    inv_std(i, p, 1)

                def low_hidden(i, p):
                    pool.wait_ge(ht_ready, upto(i, p, 1, 1))
                    nc.gpsimd.tensor_tensor(xt_lo[1 - p], ht, xt_hi[1 - p].bitcast(F32), ALU.subtract
                                            ).then_inc(ht_lo_ready, 1)

                def second_norm(i, p):
                    link_b.block(i, p)
                    pool.wait_ge(mv2_ready, upto(i, p, 1, 1))
                    link_b.done(nc.gpsimd.tensor_tensor(var_eps[:, 2], mv[:, 2, :, 1], eps[:], ALU.add))
                    link_b.wait()
                    nc.gpsimd.tensor_tensor(rs[:, 2], var_eps[:, 2], minus_half[:], ALU.pow).then_inc(rs2_ready, 1)

                def residual(i, p):
                    pool.wait_ge(n2_ready, upto(i, p, 1, 1))
                    ga = modv[:, 2:3, :].to_broadcast([P, TT, C])
                    nc.gpsimd.tensor_tensor(hb, hb, ga, ALU.mult).then_inc(h_scaled, 1)
                    wait(pool, x2_out, upto(i, p, 16, 0))
                    wait(pool, h2_ready, upto(i, p, 1, 0))
                    pool.wait_ge(h_scaled, upto(i, p, 1, 1))
                    nc.gpsimd.tensor_tensor(x2, xt, hb, ALU.add).then_inc(r_ready, 1)

                def conv_out(i, p):
                    pool.wait_ge(csig_ready, upto(i, p, 1, 1))
                    nc.gpsimd.tensor_tensor(sg, sg, cv, ALU.mult).then_inc(u_ready, 1)

                def row_norms(i, p):
                    pool.wait_ge(sumsq_ready, upto(i, p, 1, 1))
                    wait(pool, w_ready, upto(i, p, 1, 0))
                    apart(pool)
                    link_b.done(nc.gpsimd.tensor_scalar(sumsq[:], sumsq[:], 1e-24, None, ALU.max))
                    link_b.wait()
                    nc.gpsimd.tensor_tensor(inv_norm[:], sumsq[:], minus_half[:], ALU.pow
                                            ).then_inc(inv_norm_ready, 1)
                    pool.wait_ge(h2t_ready, upto(i, p, 1, 1))
                    nc.gpsimd.tensor_tensor(xt_lo[p], h2t, xt_hi[p].bitcast(F32), ALU.subtract
                                            ).then_inc(xlo_ready, 1)

                first_norms(0, 0)
                pool.wait_ge(col_ss, 1)
                nc.gpsimd.tensor_tensor(col_inv[:], col_inv[:], half_e[:], ALU.pow).then_inc(col_inv_ready, 1)
                pool.wait_ge(win_free, 1)
                pool.wait_ge(mod_ready, 1)
                residual(0, 0)

                def pieces(ahead, c, a):
                    if ahead >= 2:
                        first_norms(*a)
                        low_hidden(*a)
                    second_norm(*c)
                    row_norms(*c)
                    if ahead >= 2:
                        conv_out(*a)
                        residual(*a)

                first_norms(0, 1)
                low_hidden(0, 1)
                conv_out(0, 1)
                second_norm(0, 0)
                row_norms(0, 0)
                residual(0, 1)

                def slot(i, p, ahead):
                    if ahead:
                        pieces(ahead, following(i, p), (i + 1, p))

                slots(pool, slot)

            @block.scalar
            def _(act):
                act.wait_ge(cond_in, 16)
                nc.scalar.activation(c_sig[:], c_col[:], ACT.Sigmoid).then_inc(sig_ready, 1)
                act.wait_ge(pool_const, 2)
                nc.scalar.copy(ones_r[:], ones_f[0:1, :])
                act.wait_ge(params_in, 16 * N_PARAMS)
                nc.scalar.activation(sig_gates[:], sig_gates[:], ACT.Sigmoid)
                nc.scalar.copy(win_hi, win).then_inc(win_hi_ready, 1)
                nc.scalar.copy(cm_parts[:], cm_ld).then_inc(cm_hi_ready, 1)
                act.wait_ge(mod_mm, 1)
                nc.scalar.copy(modv[:, 3], ps[:, X1, C:2 * C])
                nc.scalar.copy(modv[:, 2], ps[:, X1, 0:C]).then_inc(mod_copied, 1)

                def split_w(e0, e1):
                    for e in range(e0, e1):
                        w_arrived(act, e)
                        nc.scalar.copy(w_hi[:, :, e], w_staged[W_STAGE[e]]).then_inc(w_hi_ready, 1)

                def hidden(i, p):
                    act.wait_ge(n2_transposed, upto(i, p, 1, 1))
                    wait(act, moe_mm, upto(i, p, STEPS, -2 * STEPS))
                    for k in range(KC):
                        nc.scalar.activation(ht[:, k], ps[:, X1 + k, :], ACT.Identity,
                                             bias=lnb[:, k:k + 1], scale=lnw[:, k:k + 1])
                        ins = nc.scalar.activation(xt_hi[1 - p][:, k], ps[:, X1 + k, :], ACT.Identity,
                                                   bias=lnb[:, k:k + 1], scale=lnw[:, k:k + 1])
                    ins.then_inc(ht_ready, 1)

                def data_out(i, p, first=False):
                    wait(act, conv_ready, upto(i, p, 1, 0))
                    wait(act, u_ready, upto(i, p, 1, 0))
                    if first:
                        act.wait_ge(mod_mm, 1)
                        nc.scalar.mul(data[:, :, 0:TAPS - 1], ident[:, 0:FI * (TAPS - 1)].rearrange(
                            "p (f j) -> p f j", f=FI), 0.0)
                    else:
                        nc.scalar.copy(data[:, :, 0:TAPS - 1], data[:, :, BT:BT + TAPS - 1]).then_inc(halo_ready, 1)
                        act.wait_ge(halo_ready, upto(i, p, 1, 0))
                    evacuate_projection(0, FI, i, p)

                def gates_out(i, p):
                    wait(act, out_mm, upto(i, p, 1, 0))
                    evacuate_projection(FI, 2 * FI, i, p)

                def evacuate_projection(f0, f1, i, p):
                    for f in range(f0, f1):
                        act.wait_ge(proj_mm, upto(i, p, 2 * FI, f + 1))
                        src = ps[:, X0 + (f + 2) % 3, :]
                        if f < FI:
                            nc.scalar.copy(data[:, f, TAPS - 1:], src)
                            nc.scalar.mul(cv[:, f], src, cw[:, f, TAPS - 1:TAPS]).then_inc(proj_evac, 1)
                        else:
                            nc.scalar.activation(gy[:, f - FI], src, ACT.Sigmoid).then_inc(proj_evac, 1)

                def conv_sigmoid(i, p):
                    act.wait_ge(conv_ready, upto(i, p, 1, 1))
                    wait(act, bu_mm, upto(i, p, 1, 0))
                    act.wait_ge(ht_lo_ready, upto(i, p, 1, 1))
                    nc.scalar.activation(sg, cv, ACT.Sigmoid).then_inc(csig_ready, 1)

                def bu_store(i, p):
                    act.wait_ge(bu_mm, upto(i, p, 1, 1))
                    wait(act, bu_out, upto(i, p, 16, 0))
                    nc.scalar.copy(bu[:], ps[0:S, X1, :]).then_inc(bu_ready, 1)
                    act.wait_ge(bu_ready, upto(i, p, 1, 1))
                    act.dma_start(bu_dram[bass.ds(i * 2 + p, 1)].rearrange("a (g s) t -> s (a g) t", s=S),
                                  bu[:].rearrange("s (g t) -> s g t", g=NB)).then_inc(bu_out, 16)

                def row_squares(i, p):
                    act.wait_ge(h2_ready, upto(i, p, 1, 1))
                    wait(act, inv_norm_ready, upto(i, p, 1, 0))
                    wait(act, logits_mm, upto(i, p, 1, 0))
                    for t in range(TT):
                        ins = nc.scalar.activation(h2t[:, t // 2, (t % 2) * C:(t % 2 + 1) * C], h2[:, t], ACT.Square,
                                                   accum_out=sumsq[:, t:t + 1])
                    ins.then_inc(sumsq_ready, 1)

                def x_parts(i, p):
                    act.wait_ge(h2_transposed, upto(i, p, 1, 1))
                    act.wait_ge(sumsq_ready, upto(i, p, 1, 1))
                    src = ps[:, X1:X1 + 2, :]
                    nc.scalar.copy(h2t, src)
                    wait(act, moe_mm, upto(i, p, STEPS, -STEPS))
                    if not (isinstance(i, int) and 2 * i + p == NB - 1):
                        act.wait_ge(proj_mm, upto(i, p, 2 * FI, 4 * FI))
                    nc.scalar.copy(xt_hi[p], src).then_inc(h2t_ready, 1)

                def exp(i, p):
                    act.wait_ge(shifted_ready, upto(i, p, 1, 1))
                    nc.scalar.activation(shifted[:], shifted[:], ACT.Exp).then_inc(exp_ready, 1)

                def evacuate(i, p, t):
                    act.wait_ge(qk_mm, upto(i, p, TT, t + 1))
                    wait(act, qk_out[t % 2], upto(i, p, 16 * TT // 2, 16 * (t // 2)))
                    nc.scalar.copy(qk_st[:, t % 2], ps[:, QK_BANK, 0:2 * P].rearrange("p (a n) -> p a n", a=2)
                                   ).then_inc(qk_ready, 1)
                    act.wait_ge(qk_ready, upto(i, p, TT, t + 1))
                    cols = bass.ds(i * (2 * BT) + p * BT + t * P, P)
                    act.dma_start(qk_dram[:, :, cols], qk_st[:, t % 2]).then_inc(qk_out[t % 2], 16)
                    act.dma_start(v_dram[cols, :], acc[:, t % 2, 2 * H:]).then_inc(v_out[t % 2], 16)

                def last_tile(t):
                    tile, cols = NT - TT + t, slice(N - BT + t * P, N - BT + (t + 1) * P)
                    act.wait_ge(qk_mm, tile + 1)
                    act.wait_ge(qk_out[t % 2], 16 * (tile // 2))
                    nc.scalar.copy(v_all[:, tile], acc[:, t % 2, 2 * H:])
                    nc.scalar.copy(k_t[:, cols], ps[:, QK_BANK, P:2 * P])
                    ins = nc.scalar.copy(k_hi[:, cols], ps[:, QK_BANK, P:2 * P])
                    if t == TT - 1:
                        ins.then_inc(k_hi_ready, 1)
                    nc.scalar.copy(qk_st[:, t % 2, 0], ps[:, QK_BANK, 0:P]).then_inc(qk_ready, 1)
                    act.wait_ge(qk_ready, tile + 1)
                    act.dma_start(qk_dram[:, 0, cols], qk_st[:, t % 2, 0]).then_inc(qk_out[t % 2], 16)

                split_w(0, 3)
                hidden(0, 0)
                data_out(0, 0, first=True)
                gates_out(0, 0)
                conv_sigmoid(0, 0)
                split_w(3, 6)
                bu_store(0, 0)

                def pieces(ahead, c, a, tile):
                    if ahead >= 2:
                        hidden(*a)
                    tile(0)
                    if ahead >= 2:
                        data_out(*a)
                        gates_out(*a)
                    tile(1)
                    row_squares(*c)
                    x_parts(*c)
                    if ahead >= 2:
                        conv_sigmoid(*a)
                    exp(*c)
                    if ahead >= 2:
                        bu_store(*a)
                    tile(2)
                    tile(3)

                hidden(0, 1)
                split_w(6, 9)
                data_out(0, 1)
                split_w(9, 12)
                conv_sigmoid(0, 1)
                gates_out(0, 1)
                split_w(12, 14)
                bu_store(0, 1)
                act.wait_ge(w_lo_ready, E - 4)
                row_squares(0, 0)
                x_parts(0, 0)
                split_w(14, E)
                exp(0, 0)

                def slot(i, p, ahead):
                    if ahead:
                        pieces(ahead, following(i, p), (i + 1, p), lambda t: evacuate(i, p, t))
                    else:
                        act.wait_ge(q_in, 16)
                        act.wait_ge(moe_mm, (NB - 1) * STEPS)
                        nc.scalar.copy(q_hi[:, 0], q_st[:, 0]).then_inc(q_hi_ready, 1)
                        for t in range(TT):
                            for g in (2 * t, 2 * t + 1):
                                if g < NB - 1:
                                    act.wait_ge(kv_in[g], 32)
                                    nc.scalar.copy(k_hi[:, g * BT:(g + 1) * BT], k_t[:, g * BT:(g + 1) * BT]
                                                   ).then_inc(k_hi_ready, 1)
                            if t == 0:
                                act.wait_ge(x2_out, 16 * NB)
                                act.wait_ge(xlo_ready, NB)
                                act.wait_ge(w_ready, NB)
                                act.wait_ge(u_ready, NB)
                                act.wait_ge(bu_mm, NB)
                            last_tile(t)

                slots(act, slot)

            @block.vector
            def _(dve):
                link, more = Link(dve, dve_a, DVE_A), Link(dve, dve_b, DVE_B)
                taps = Link(dve, conv_link, TAPS - 2)
                tt, tr, ts = nc.vector.tensor_tensor, nc.vector.tensor_reduce, nc.vector.tensor_scalar

                def split_w(e0, e1):
                    for e in range(e0, e1):
                        dve.wait_ge(w_hi_ready, e + 1)
                        tt(w_lo[:, :, e], w_staged[W_STAGE[e]], w_hi[:, :, e].bitcast(F32), ALU.subtract
                           ).then_inc(w_lo_ready, 1)

                def stats(src, n, chain):
                    for t in range(TT):
                        ins = nc.vector.bn_stats(bst[:, n, t], src[:, t])
                    chain.done(ins)
                    chain.wait()
                    apart(dve)
                    for t in range(TT):
                        ins = nc.vector.bn_aggr(mv[:, n, t], bst[:, n, t])
                    return ins

                def normalize(dst, src, n):
                    for t in range(TT):
                        ins = ts(dst[:, t], src[:, t], mv[:, n, t, 0:1], rs[:, n, t:t + 1], ALU.subtract, ALU.mult)
                    return ins

                def modulate(dst, src, n, first):
                    for t in range(TT):
                        ins = nc.vector.scalar_tensor_tensor(out=dst[:, t], in0=src[:, t], scalar=mv[:, n, t, 0:1],
                                                             in1=modv[:, first], op0=ALU.subtract, op1=ALU.mult)
                    return ins

                def shift(dst, n, second):
                    for t in range(TT):
                        ins = nc.vector.scalar_tensor_tensor(out=dst[:, t], in0=dst[:, t], scalar=rs[:, n, t:t + 1],
                                                             in1=modv[:, second], op0=ALU.mult, op1=ALU.add)
                    return ins

                def norm_piece(n, i, p):
                    if n == 0:
                        link.block(i, p)
                        dve.wait_ge(x_in, upto(i, p, 16, 16))
                        stats(xt, 0, link).then_inc(mv_ready, 1)
                    elif n == 1:
                        wait(dve, r_ready, upto(i, p, 1, 0))
                        dve.wait_ge(mv_ready, upto(i, p, 2, 1))
                        link.done(modulate(hb, xt, 0, 1))
                    elif n == 2:
                        link.wait()
                        dve.wait_ge(rs_ready, upto(i, p, 2, 1))
                        link.done(shift(hb, 0, 0))
                    elif n == 3:
                        link.wait()
                        stats(hb, 1, link).then_inc(mv_ready, 1)
                    else:
                        wait(dve, bu_mm, upto(i, p, 1, 0))
                        dve.wait_ge(rs_ready, upto(i, p, 2, 2))
                        normalize(n2, hb, 1).then_inc(n2_ready, 1)

                def conv_piece(j, i, p):
                    if j == 0:
                        taps.block(i, p)
                        dve.wait_ge(proj_evac, upto(i, p, 2 * FI, FI))
                    else:
                        taps.wait()
                    for f in range(FI):
                        ins = nc.vector.scalar_tensor_tensor(out=cv[:, f], in0=data[:, f, j:j + BT],
                                                             scalar=cw[:, f, j:j + 1], in1=cv[:, f],
                                                             op0=ALU.mult, op1=ALU.add)
                    if j < TAPS - 2:
                        taps.done(ins)
                    else:
                        ins.then_inc(conv_ready, 1)

                def carry_in(i, p):
                    dve.wait_ge(scan_in, upto(i, p, 16, 16))
                    dve.wait_ge(carry_mm, upto(i, p, 1, 0))
                    tt(scan_s[0][0:S, 0:1], scan_s[0][0:S, 0:1], ps[0:S, X0, P:P + 1], ALU.add
                       ).then_inc(carry_added, 1)

                def scan_step(k, i, p):
                    if k == 0 and isinstance(i, int) and i == 0 and p == 0:
                        dve.wait_ge(scan_in, 16)
                    dve.wait_ge(scan_mm, upto(i, p, SCAN, k + 1))
                    tt(scan_s[(k + 1) % 2][:], scan_s[k % 2][:], ps[:, X0, (k % 2) * GT:(k % 2 + 1) * GT], ALU.add
                       ).then_inc(scan_add, 1)

                def state_parts(i, p):
                    dve.wait_ge(scan_add, upto(i, p, SCAN, SCAN))
                    wait(dve, st_out, upto(i, p, 32, 0))
                    nc.vector.tensor_copy(s_parts[:, 0], scan_s[SCAN % 2][:]).then_inc(s_hi_ready, 1)
                    dve.wait_ge(s_hi_ready, upto(i, p, 1, 1))
                    tt(s_parts[:, 1], scan_s[SCAN % 2][:], s_parts[:, 0].bitcast(F32), ALU.subtract
                       ).then_inc(s_parts_ready, 1)

                def gate_times_y(i, p):
                    dve.wait_ge(y_mm, upto(i, p, 1, 1))
                    dve.wait_ge(proj_evac, upto(i, p, 2 * FI, 2 * FI))
                    tt(gy, gy, ps[:, X0:X0 + FI, :], ALU.mult).then_inc(gy_ready, 1)

                def op(ins):
                    more.done(ins)

                out_ps = ps[:, X0:X0 + 2, :].rearrange("p b (t c) -> p (b t) c", c=C)

                def x2_piece(n, i, p):
                    if n == 0:
                        more.block(i, p)
                        dve.wait_ge(out_mm, upto(i, p, 1, 1))
                        dve.wait_ge(r_ready, upto(i, p, 1, 1))
                        tt(x2, x2, out_ps, ALU.add).then_inc(x2_ready, 1)
                    elif n == 1:
                        dve.wait_ge(x2_ready, upto(i, p, 1, 1))
                        for t in range(TT):
                            ins = nc.vector.bn_stats(bst[:, 2, t], x2[:, t])
                        op(ins)
                    elif n == 2:
                        more.wait()
                        apart(dve)
                        for t in range(TT):
                            ins = nc.vector.bn_aggr(mv[:, 2, t], bst[:, 2, t])
                        ins.then_inc(mv2_ready, 1)
                    elif n == 3:
                        wait(dve, h2_transposed, upto(i, p, 1, 0))
                        wait(dve, sumsq_ready, upto(i, p, 1, 0))
                        dve.wait_ge(mv2_ready, upto(i, p, 1, 1))
                        op(modulate(h2, x2, 2, 4))
                    else:
                        more.wait()
                        dve.wait_ge(rs2_ready, upto(i, p, 1, 1))
                        shift(h2, 2, 3).then_inc(h2_ready, 1)

                def wide(a):
                    return a.to_broadcast([P, TT, E])

                def route_piece(n, i, p):
                    link = more
                    if n == 0:
                        dve.wait_ge(logits_mm, upto(i, p, 1, 1))
                        dve.wait_ge(inv_norm_ready, upto(i, p, 1, 1))
                        op(tt(lg[:], ps[:, X0, 0:TT * E].rearrange("p (t e) -> p t e", e=E),
                              wide(inv_norm[:].rearrange("p (t a) -> p t a", a=1)), ALU.mult))
                        link.wait()
                        op(tt(lg[:], lg[:], wide(sig_gates[:].rearrange("p (a e) -> p a e", a=1)), ALU.subtract))
                    elif n == 1:
                        link.wait()
                        ts(gated[:], lg[:], 0.0, None, ALU.max)
                        ts(hard[:], lg[:], 0.0, None, ALU.is_gt)
                        op(tr(top[:], lg[:], AX_X, ALU.max))
                        link.wait()
                        op(tr(g_max[:], gated[:], AX_X, ALU.max))
                    elif n == 2:
                        link.wait()
                        tt(shifted[:], gated[:], wide(g_max[:]), ALU.subtract).then_inc(shifted_ready, 1)
                        ts(inactive[:], g_max[:], 0.0, None, ALU.is_le)
                        op(tt(pick[:], lg[:], wide(top[:]), ALU.is_equal))
                        link.wait()
                        op(tt(pick[:], pick[:], rank[:], ALU.mult))
                    elif n == 3:
                        link.wait()
                        op(tr(top[:], pick[:], AX_X, ALU.max))
                        link.wait()
                        op(tt(first_hot[:], rank[:], wide(top[:]), ALU.is_equal))
                    elif n == 4:
                        link.wait()
                        op(nc.vector.scalar_tensor_tensor(out=lg_rest[:], in0=first_hot[:], scalar=-1e30,
                                                          in1=lg[:], op0=ALU.mult, op1=ALU.add))
                        link.wait()
                        op(tr(top[:], lg_rest[:], AX_X, ALU.max))
                    elif n == 5:
                        link.wait()
                        op(tt(pick[:], lg_rest[:], wide(top[:]), ALU.is_equal))
                        link.wait()
                        op(tt(pick[:], pick[:], rank[:], ALU.mult))
                    elif n == 6:
                        link.wait()
                        op(tr(top[:], pick[:], AX_X, ALU.max))
                        link.wait()
                        op(tt(pick[:], rank[:], wide(top[:]), ALU.is_equal))
                    elif n == 7:
                        link.wait()
                        op(tt(pick[:], pick[:], first_hot[:], ALU.add))
                        link.wait()
                        op(tt(pick[:], pick[:], wide(inactive[:]), ALU.mult))
                        link.wait()
                        op(tt(pick[:], pick[:], hard[:], ALU.add))
                    elif n == 8:
                        dve.wait_ge(exp_ready, upto(i, p, 1, 1))
                        link.wait()
                        op(tt(pick[:], pick[:], shifted[:], ALU.mult))
                        link.wait()
                        op(tr(w_sum[:], pick[:], AX_X, ALU.add))
                    elif n == 9:
                        link.wait()
                        op(nc.vector.reciprocal(w_sum[:], w_sum[:]))
                        link.wait()
                        op(tt(w_cur[:, p], pick[:], wide(w_sum[:]), ALU.mult))
                    else:
                        link.wait()
                        nc.vector.tensor_copy(w_all[:, tiles(i, p, 0, TT), :], w_cur[:, p]).then_inc(w_ready, 1)

                NORM_PIECES, X2_PIECES, ROUTE_PIECES = 5, 5, 11

                def piece(n, kind, c, a, ahead):
                    if kind == "norm" and ahead >= 2:
                        norm_piece(n, *a)
                    elif kind == "conv" and ahead >= 2:
                        conv_piece(n, *a)
                    elif kind == "carry":
                        carry_in(*c)
                    elif kind == "gate":
                        gate_times_y(*c)
                    elif kind == "x2":
                        x2_piece(n, *c)
                    elif kind == "route":
                        route_piece(n, *c)

                def max_piece(n):
                    g, t = divmod(n, TT)
                    dve.wait_ge(max_mm, n + 1)
                    tr(mx[:, t, g:g + 1], ps[:, X0 + n % 2, :], AX_X, ALU.max).then_inc(max_red, 1)

                def pow_copy(k):
                    dve.wait_ge(pow_mm, k)
                    nc.vector.tensor_copy(powers[:, k, pad:], ps[:, QK_BANK, 0:P])
                    nc.vector.tensor_copy(powers_t[:, k % 2], ps[:, QK_BANK, P:2 * P]).then_inc(pow_ready, 1)

                pre = Link(dve, pre_dve, 0)
                norm_piece(0, 0, 0)
                dve.wait_ge(sig_ready, 1)
                pre.done(tt(c_sig[:], c_sig[:], c_col[:], ALU.mult))
                pre.wait()
                for k in range(KC):
                    ins = nc.vector.tensor_copy(c_bc[:, k, :], c_sig[:, k:k + 1].to_broadcast([P, P]))
                pre.done(ins)
                dve.wait_ge(a_in, 16 * 2 * NB)
                dve.wait_ge(pool_const, 2)
                for blk in (powers[:, 0, pad:], powers_t[:, 0]):
                    ins = tt(blk, blk, ident[:], ALU.add)
                ins.then_inc(pow_ready, 1)
                dve.wait_ge(params_in, 16 * N_PARAMS)
                pre.done(tt(sim_sq[:], simt, simt, ALU.mult))
                dve.wait_ge(mod_mm, 1)
                ts(modv[:, 1], ps[:, X0, C:2 * C], 1.0, None, ALU.add)
                nc.vector.tensor_copy(modv[:, 0], ps[:, X0, 0:C])
                nc.vector.tensor_copy(modv[:, 5], ps[:, X2, C:2 * C])
                pre.done(ts(modv[:, 4], ps[:, X2, 0:C], 1.0, None, ALU.add))
                pre.wait()
                norm_piece(1, 0, 0)
                dve.wait_ge(colnorm_mm, 1)
                ts(col_inv[:], ps[:, QK_BANK, 0:E], 1e-24, None, ALU.max).then_inc(col_ss, 1)
                norm_piece(2, 0, 0)
                pow_copy(1)
                norm_piece(3, 0, 0)
                pow_copy(2)
                dve.wait_ge(win_hi_ready, 1)
                tt(win_lo, win, win_hi.bitcast(F32), ALU.subtract).then_inc(win_free, 1)
                norm_piece(4, 0, 0)
                for k in range(3, 5):
                    pow_copy(k)
                dve.wait_ge(ht_ready, 1)
                tt(xt_lo[1], ht, xt_hi[1].bitcast(F32), ALU.subtract).then_inc(ht_lo_ready, 1)
                dve.wait_ge(mod_copied, 1)
                for n, g in enumerate((2, 5)):
                    ins = ts(g_tmp[:, n], modv[:, g], 0.0, 2.0, ALU.is_ge, ALU.mult)
                pre.done(ins)
                pre.wait()
                for n, g in enumerate((2, 5)):
                    nc.vector.scalar_tensor_tensor(out=modv[:, g], in0=modv[:, g], scalar=-1.0,
                                                   in1=modv[:, g], op0=ALU.mult, op1=ALU.max)
                    ins = ts(g_tmp[:, n], g_tmp[:, n], -1.0, None, ALU.add)
                pre.done(ins)
                pre.wait()
                for n, g in enumerate((2, 5)):
                    ins = nc.vector.scalar_tensor_tensor(out=modv[:, g], in0=modv[:, g], scalar=0.25,
                                                         in1=g_tmp[:, n], op0=ALU.max, op1=ALU.mult)
                ins.then_inc(mod_ready, 1)
                split_w(0, 3)
                for n in range(TAPS - 1):
                    conv_piece(n, 0, 0)
                pow_copy(5)
                norm_piece(0, 0, 1)
                dve.wait_ge(csig_ready, 1)
                tt(sg, sg, cv, ALU.mult).then_inc(u_ready, 1)
                for n in range(1, 4):
                    norm_piece(n, 0, 1)
                pow_copy(6)
                dve.wait_ge(cm_hi_ready, 1)
                third = slice(2 * S, 3 * S)
                tt(cm_parts[third, :], cm_ld[third, :], cm_parts[third, :].bitcast(F32), ALU.subtract
                   ).then_inc(parts_ready, 1)
                dve.wait_ge(mod_ready, 1)
                tt(wout[:], wout[:], modv[:, 2:3, :].to_broadcast([P, FI, C]), ALU.mult).then_inc(wout_ready, 1)
                norm_piece(4, 0, 1)
                pow_copy(7)
                pow_copy(8)
                dve.wait_ge(col_inv_ready, 1)
                for k in range(KC):
                    ins = tt(sn[:, k], simt[:, k], col_inv[:], ALU.mult)
                ins.then_inc(sn_ready, 1)
                for k in range(SCAN):
                    scan_step(k, 0, 0)
                    if k < 3:
                        split_w(3 + k, 4 + k)
                    elif SCAN - 4 <= k < SCAN - 1:
                        split_w(6 + k - (SCAN - 4), 7 + k - (SCAN - 4))
                state_parts(0, 0)
                gate_times_y(0, 0)
                for n in range(TAPS - 1):
                    conv_piece(n, 0, 1)
                split_w(9, 12)
                for n in range(X2_PIECES):
                    x2_piece(n, 0, 0)
                split_w(12, E)
                for n in range(ROUTE_PIECES):
                    route_piece(n, 0, 0)

                def slot(i, p, ahead):
                    c, a = following(i, p), (i + 1, p)
                    dve.wait_ge(w_ready, upto(i, p, 1, 1))
                    for s in range(STEPS):
                        t, e = divmod(s, E)
                        dve.wait_ge(moe_mm, upto(i, p, STEPS, s + 1))
                        src, w, dst = ps[:, s % MOE_BANKS, 0:H3], w_cur[:, p, t, e:e + 1], acc[:, t % 2]
                        if e == 0:
                            wait(dve, qk_mm, upto(i, p, TT, t - 1))
                            if ahead or t < 2:
                                wait(dve, v_out[t % 2], upto(i, p, 16 * TT // 2, 16 * (t // 2)))
                            else:
                                dve.wait_ge(qk_ready, NT - TT + t - 1)
                            ts(dst, src, w, None, ALU.mult).then_inc(moe_acc, 1)
                        else:
                            dve.wait_ge(moe_acc, upto(i, p, STEPS, s))
                            nc.vector.scalar_tensor_tensor(out=dst, in0=src, scalar=w, in1=dst,
                                                           op0=ALU.mult, op1=ALU.add).then_inc(moe_acc, 1)
                        if ahead:
                            if s in DVE_PIECES:
                                kind, n = DVE_PIECES[s]
                                piece(n, kind, c, a, ahead)
                            if s in SCAN_AT:
                                scan_step(SCAN_AT[s], *c)
                                if SCAN_AT[s] == SCAN - 1:
                                    state_parts(*c)
                            if s >= DVE_ROUTE and s - DVE_ROUTE < ROUTE_PIECES:
                                route_piece(s - DVE_ROUTE, *c)
                        elif s >= MAX_FROM and (s - MAX_FROM) % 2 == 1 and (s - MAX_FROM) // 2 < MAX_EARLY:
                            max_piece((s - MAX_FROM) // 2)

                slots(dve, slot)

            @block.tensor
            def _(pe):
                pe.wait_ge(pre_dve, 2)
                pe.wait_ge(wmod_in, 16)
                for b in range(3):
                    for k in range(KC):
                        ins = nc.tensor.matmul(ps[:, X0 + b, :], c_bc[:, k, :], wmod_ld[:, k, b * BT:(b + 1) * BT],
                                               start=(k == 0), stop=(k == KC - 1))
                ins.then_inc(mod_mm, 1)
                pe.wait_ge(pre_dve, 3)
                for k in range(KC):
                    ins = nc.tensor.matmul(ps[:, QK_BANK, 0:E], ones_f[:], sim_sq[:, k, :],
                                           start=(k == 0), stop=(k == KC - 1))
                ins.then_inc(colnorm_mm, 1)

                def next_power(k):
                    pe.wait_ge(pow_ready, k)
                    m, mt = powers[:, k - 1, pad:], powers_t[:, (k - 1) % 2]
                    nc.tensor.matmul(ps[:, QK_BANK, 0:P], mt, m, start=True, stop=True)
                    nc.tensor.matmul(ps[:, QK_BANK, P:2 * P], m, mt, start=True, stop=True).then_inc(pow_mm, 1)

                def n2_transposes(i, p):
                    pe.wait_ge(n2_ready, upto(i, p, 1, 1))
                    for k in range(KC):
                        for t in range(TT):
                            ins = nc.tensor.transpose(ps[:, X1 + k, t * P:(t + 1) * P],
                                                      n2[:, t, k * P:(k + 1) * P], ident[:])
                    ins.then_inc(n2_transposed, 1)

                def project(f, i, p, early=False):
                    if f == 0:
                        pe.wait_ge(ht_lo_ready, upto(i, p, 1, 1))
                        if early:
                            pe.wait_ge(scan_add, upto(i, p, SCAN, 0))
                    if f == (FI if early else 0):
                        wait(pe, x2_ready, upto(i, p, 1, 0))
                    wait(pe, proj_evac, upto(i, p, 2 * FI, f - 2))
                    cols = slice(f * P, (f + 1) * P)
                    for k in range(KC):
                        for n, (a, b) in enumerate(((win_hi, xt_hi), (win_hi, xt_lo), (win_lo, xt_hi))):
                            ins = nc.tensor.matmul(ps[:, X0 + (f + 2) % 3, :], a[:, k, cols], b[1 - p][:, k, :],
                                                   start=(k == 0 and n == 0), stop=(k == KC - 1 and n == 2))
                    ins.then_inc(proj_mm, 1)

                def input_term(i, p, first=False):
                    pe.wait_ge(u_ready, upto(i, p, 1, 1))
                    pe.wait_ge(proj_evac, upto(i, p, 2 * FI, 2 * FI))
                    if not first:
                        wait(pe, h2t_ready, upto(i, p, 1, 0))
                    for f in range(FI):
                        ins = nc.tensor.matmul(ps[0:S, X1, :], bmt[:, f, :], sg[:, f, :],
                                               start=(f == 0), stop=(f == FI - 1))
                    ins.then_inc(bu_mm, 1)

                def carry_piece(i, p):
                    pe.wait_ge(w_ready, upto(i, p, 1, 0))
                    pe.wait_ge(s_parts_ready, upto(i, p, 1, 0))
                    nc.tensor.matmul(ps[0:S, X0, P:P + 1], powers[:, 0, pad + P - S:pad + P],
                                     scan_s[SCAN % 2][:, GT - 1:GT], start=True, stop=True).then_inc(carry_mm, 1)

                def scan_piece(k, i, p, first=False):
                    d = 1 << k
                    if k:
                        pe.wait_ge(scan_add, upto(i, p, SCAN, k))
                    elif first:
                        pe.wait_ge(scan_in, 16)
                    else:
                        pe.wait_ge(carry_added, upto(i, p, 1, 0))
                    src, dst = scan_s[k % 2], ps[:, X0, (k % 2) * GT:(k % 2 + 1) * GT]
                    if d < GT:
                        nc.tensor.matmul(dst[:, d:GT], pw_m(k), src[:, 0:GT - d], start=True, stop=True)
                        ins = nc.tensor.matmul(dst[:, 0:d], pw_m(k, 1), src[:, GT - d:GT], start=True, stop=True)
                    else:
                        ins = nc.tensor.matmul(dst, pw_m(k, d // GT), src[:], start=True, stop=True)
                    ins.then_inc(scan_mm, 1)

                def y_piece(i, p, ahead):
                    pe.wait_ge(st_in, upto(i, p, 48, 48))
                    pe.wait_ge(bu_ready, upto(i, p, 1, 1))
                    if ahead >= 2:
                        pe.wait_ge(ht_ready, upto(i, p, 1, 2))
                    for f in range(FI):
                        ins = nc.tensor.matmul(ps[:, X0 + f, :], cm_parts[:, f * P:(f + 1) * P], st_parts[:],
                                               start=True, stop=True)
                    ins.then_inc(y_mm, 1)

                def out_piece(i, p):
                    pe.wait_ge(gy_ready, upto(i, p, 1, 1))
                    for t in range(TT):
                        dst = ps[:, X0 + t // 2, (t % 2) * C:(t % 2 + 1) * C]
                        for f in range(FI):
                            ins = nc.tensor.matmul(dst, gy[:, f, t * P:(t + 1) * P], wout[:, f, :],
                                                   start=(f == 0), stop=(f == FI - 1))
                    ins.then_inc(out_mm, 1)

                def h2_transposes(i, p):
                    pe.wait_ge(h2_ready, upto(i, p, 1, 1))
                    if not (isinstance(i, int) and 2 * i + p == NB - 1):
                        pe.wait_ge(proj_evac, upto(i, p, 2 * FI, 4 * FI))
                    for k in range(KC):
                        for t in range(TT):
                            ins = nc.tensor.transpose(ps[:, X1 + k, t * P:(t + 1) * P],
                                                      h2[:, t, k * P:(k + 1) * P], ident[:])
                    ins.then_inc(h2_transposed, 1)

                def logits_piece(i, p):
                    pe.wait_ge(h2t_ready, upto(i, p, 1, 1))
                    for t in range(TT):
                        for k in range(KC):
                            ins = nc.tensor.matmul(ps[:, X0, t * E:(t + 1) * E], h2t[:, k, t * P:(t + 1) * P],
                                                   sn[:, k, :], start=(k == 0), stop=(k == KC - 1))
                    ins.then_inc(logits_mm, 1)

                def qk_transposes(i, p, t):
                    pe.wait_ge(moe_acc, upto(i, p, STEPS, (t + 1) * E))
                    wait(pe, qk_ready, upto(i, p, TT, t))
                    nc.tensor.transpose(ps[:, QK_BANK, 0:P], acc[:, t % 2, 0:H], ident[:])
                    nc.tensor.transpose(ps[:, QK_BANK, P:2 * P], acc[:, t % 2, H:2 * H], ident[:]).then_inc(qk_mm, 1)

                def max_piece(n):
                    g, t = divmod(n, TT)
                    if n == 0:
                        pe.wait_ge(q_hi_ready, 1)
                    pe.wait_ge(k_hi_ready, g + 1)
                    if n >= 2:
                        pe.wait_ge(max_red, n - 1)
                    nc.tensor.matmul(ps[:, X0 + n % 2, :], q_hi[:, 0, t * P:(t + 1) * P], k_hi[:, g * BT:(g + 1) * BT],
                                     start=True, stop=True).then_inc(max_mm, 1)

                pe.wait_ge(col_ss, 1)
                for k in range(1, 3):
                    next_power(k)
                pe.wait_ge(mod_copied, 1)
                n2_transposes(0, 0)
                for k in range(3, 5):
                    next_power(k)
                pe.wait_ge(win_free, 1)
                for f in range(2 * FI):
                    project(f, 0, 0)
                next_power(5)
                input_term(0, 0)
                next_power(6)
                next_power(7)
                pe.wait_ge(bu_ready, 1)
                n2_transposes(0, 1)
                next_power(8)
                pe.wait_ge(pow_ready, SCAN)
                for k in range(SCAN):
                    scan_piece(k, 0, 0, first=True)
                for f in range(FI):
                    project(f, 0, 1, early=True)
                pe.wait_ge(parts_ready, 1)
                pe.wait_ge(wout_ready, 1)
                pe.wait_ge(proj_evac, 3 * FI)
                y_piece(0, 0, 2)
                out_piece(0, 0)
                for f in range(FI, 2 * FI):
                    project(f, 0, 1, early=True)
                input_term(0, 1, first=True)
                pe.wait_ge(bu_ready, 2)
                h2_transposes(0, 0)
                pe.wait_ge(sn_ready, 1)
                logits_piece(0, 0)
                pe.wait_ge(w_lo_ready, E)

                def slot(i, p, ahead):
                    c, a = following(i, p), (i + 1, p)
                    pe.wait_ge(xlo_ready, upto(i, p, 1, 1))
                    for s in range(STEPS):
                        t, e = divmod(s, E)
                        wait(pe, moe_acc, upto(i, p, STEPS, s - MOE_BANKS + 1))
                        rows = slice(t * P, (t + 1) * P)
                        for k in range(KC):
                            for n, (x_part, w_part) in enumerate(((xt_hi, w_hi), (xt_hi, w_lo), (xt_lo, w_hi))):
                                ins = nc.tensor.matmul(
                                    ps[:, s % MOE_BANKS, 0:H3], x_part[p][:, k, rows],
                                    w_part[:, k, e].rearrange("p t h -> p (t h)"),
                                    start=(k == 0 and n == 0), stop=(k == KC - 1 and n == 2))
                        ins.then_inc(moe_mm, 1)
                        if s == 4 and not (isinstance(i, int) and 2 * i + p == 0):
                            qk_transposes(*before(i, p), TT - 1)
                        if e == 4 and t:
                            qk_transposes(i, p, t - 1)
                        if ahead:
                            if s == 0:
                                carry_piece(*c)
                            if s in SCAN_AT:
                                scan_piece(SCAN_AT[s], *c)
                            if s == PE_Y:
                                y_piece(*c, ahead)
                            if s == PE_OUT:
                                out_piece(*c)
                            if s == PE_TRANSPOSE_H2:
                                h2_transposes(*c)
                            if s == PE_LOGITS:
                                logits_piece(*c)
                        if ahead >= 2:
                            if s == PE_TRANSPOSE_N2:
                                n2_transposes(*a)
                            if PE_PROJECT <= s < PE_PROJECT + 2 * FI:
                                project(s - PE_PROJECT, *a)
                            if s == PE_BU:
                                input_term(*a)
                        if not ahead and s >= MAX_FROM and (s - MAX_FROM) % 2 == 0 and (s - MAX_FROM) // 2 < MAX_EARLY:
                            max_piece((s - MAX_FROM) // 2)
                    if ahead == 0:
                        qk_transposes(i, p, TT - 1)

                slots(pe, slot)
        one.close()

        three = whole.enter_context(ExitStack())
        sb = alloc(three)
        k_lo = sb("k_lo", [P, N], F32R)
        v_hi = sb("v_hi", [P, NT, H], F32R)
        v_lo = sb("v_lo", [P, NT, H], F32R)
        o_hi = sb("o_hi", [P, E, C], F32R)
        o_lo = sb("o_lo", [P, E, C], F32R)
        o_stage = k_t.rearrange("p (e c) -> p e c", e=E)
        PB = 3
        pf = sb("pf", [P, PB, BT])
        p_hi = sb("p_hi", [P, PB, BT], F32R)
        p_lo = sb("p_lo", [P, PB, BT], F32R)
        p_sum = carve([2, BT], at=2 * N + 2 * BT)
        ot_hi = sb("ot_hi", [P, 2, BT], F32R)
        ot_lo = sb("ot_lo", [P, 2, BT], F32R)
        neg_max = sb("neg_max", [P, TT])
        neg_row = sb("neg_row", [1, 2, BT], F32R)
        w_out_s = sb("w_out_s", [P, 2, TT, E])
        y = carve([2, C], at=2 * N + 4 * BT)
        yo = carve([2, C], at=2 * N + 4 * BT + 2 * C)
        x2b = sb("x2b", [P, TT, C])

        o_in = sem("o_in")
        k_lo_ready = sem("k_lo_ready")
        v_hi_ready = sem("v_hi_ready")
        v_lo_ready = sem("v_lo_ready")
        o_hi_ready = sem("o_hi_ready")
        o_lo_ready = sem("o_lo_ready")
        q_lo_ready = sem("q_lo_ready")
        neg_max_ready = sem("neg_max_ready")
        neg_mm = sem("neg_mm")
        neg_row_ready = sem("neg_row_ready")
        s_mm = sem("s_mm")
        pf_ready = sem("pf_ready")
        p_hi_ready = sem("p_hi_ready")
        p_lo_ready = sem("p_lo_ready")
        p_summed = sem("p_summed")
        pv_mm = sem("pv_mm")
        sum_mm = sem("sum_mm")
        inv_sum_ready = sem("inv_sum_ready")
        w_out_ready = sem("w_out_ready")
        ot_hi_ready = sem("ot_hi_ready")
        ot_lo_ready = sem("ot_lo_ready")
        o_mm = sem("o_mm")
        y_acc = sem("y_acc")
        yo_ready = sem("yo_ready")
        yo_scaled = sem("yo_scaled")
        x2_in = sem("x2_in")
        tail_scaled = sem("tail_scaled")
        tail_summed = sem("tail_summed")
        tail_acc = sem("tail_acc")
        tail_joined = sem("tail_joined")
        out_done = [sem("out_done0"), sem("out_done1")]

        S_BANK, MAX_BANK, O_BANK, Y_BANK, NEG_BANK = 0, 2, 3, 5, 7
        MAX_BANKS = (MAX_BANK, NEG_BANK)
        SUM_BANK = Y_BANK
        MAX_AT, n = {}, 0
        for j in range(NT):
            MAX_AT[j] = [n + m for m in range(2 if j % 5 == 4 else 1) if n + m < NT]
            n += len(MAX_AT[j])
        MAX_DONE = max(j for j in range(NT) if MAX_AT[j]) + 1
        O_FROM = 2 * NB
        LAG = 2
        PAIRS = E // 2
        assert TT * PAIRS == NT and TT * KG == NT

        ACT_PAIRS = (1, 3, 5)
        TAIL_BANKS = (5, 6, 0, 1, 2, 7)
        act_part = p_sum[:, 0].rearrange("p (a c) -> p a c", a=2)

        def by_act(j):
            return j % PAIRS in ACT_PAIRS

        def n_act(j):
            return sum(by_act(m) for m in range(j))

        def n_dve(j):
            return j - n_act(j)

        ADDS = 2 * len(ACT_PAIRS) - 1

        def last_user(j):
            return j - PB + 1 if j >= PB else max(m for m in range(NT) if m % PB == j) + 1 - NT

        def cycle(eng, start, body, finish):
            start()
            body(0, 0, True, False)
            body(0, 1, False, False)
            with eng.Fori(1, NB // 2 - 1) as i:
                body(i, 0, False, False)
                body(i, 1, False, False)
            body(NB // 2 - 1, 0, False, False)
            body(NB // 2 - 1, 1, False, True)
            finish()

        with nc.Block() as block:
            @block.sync
            def _(sp):
                sp.wait_ge(k_lo_ready, NB)
                sp.dma_start(o_stage, o_proj.rearrange("e h c -> h e c")).then_inc(o_in, 16)
                ov = tok_view(out)

                def outputs(i, p):
                    wait(sp, yo_ready, upto(i, p, TT, 0))
                    sp.dma_start(x2b[:], tok_view(x2_dram)[:, tiles(i, p, 0, TT), :]).then_inc(x2_in, 16)
                    for t in range(TT):
                        sp.wait_ge(yo_ready, upto(i, p, TT, t + 1))
                        sp.dma_start(ov[:, tiles(i, p, t), :], yo[:, t % 2:t % 2 + 1, :]).then_inc(out_done[t % 2], 16)

                outputs(0, 0)
                outputs(0, 1)
                with sp.Fori(1, NB // 2) as i:
                    outputs(i, 0)
                    outputs(i, 1)
                for n in range(2):
                    sp.wait_ge(out_done[n], 16 * NB * TT // 2)

            @block.gpsimd
            def _(pool):
                def finish_tile(i, p, t):
                    pool.wait_ge(y_acc, upto(i, p, TT * E, (t + 1) * E))
                    wait(pool, out_done[t % 2], upto(i, p, 16 * TT // 2, 16 * (t // 2)))
                    nc.gpsimd.tensor_tensor(yo[:, t % 2], y[:, t % 2], modv[:, 5], ALU.mult).then_inc(yo_scaled, 1)
                    if t == 0:
                        pool.wait_ge(x2_in, upto(i, p, 16, 16))
                    pool.wait_ge(yo_scaled, upto(i, p, TT, t + 1))
                    nc.gpsimd.tensor_tensor(yo[:, t % 2], yo[:, t % 2], x2b[:, t], ALU.add).then_inc(yo_ready, 1)

                def body(i, p, first, last):
                    for j in range(NT):
                        pool.wait_ge(pf_ready, upto(i, p, NT, j + 1))
                        if j == 0:
                            wait(pool, sum_mm, upto(i, p, 1, -1))
                            apart(pool)
                            nc.gpsimd.tensor_copy(p_sum[:, p], pf[:, 0]).then_inc(p_summed, 1)
                        else:
                            pool.wait_ge(p_summed, upto(i, p, NT, j))
                            nc.gpsimd.tensor_tensor(p_sum[:, p], p_sum[:, p], pf[:, j % PB], ALU.add
                                                    ).then_inc(p_summed, 1)
                        if not first and j % PAIRS == LAG + 1 and j >= PAIRS:
                            finish_tile(*before(i, p), j // PAIRS - 1)
                    if not first:
                        finish_tile(*before(i, p), TT - 1)

                def finish():
                    done = 0
                    for j in range(NT):
                        if not by_act(j):
                            continue
                        t, a = j // PAIRS, n_act(j)
                        halves = [pf[:, a % PB, n * C:(n + 1) * C] for n in range(2)]
                        total = act_part[:, t % 2]
                        pool.wait_ge(tail_scaled, a + 1)
                        if j % PAIRS == ACT_PAIRS[0]:
                            wait(pool, tail_joined, t - 1)
                            nc.gpsimd.tensor_tensor(total, halves[0], halves[1], ALU.add).then_inc(tail_summed, 1)
                            done += 1
                        else:
                            for n in range(2):
                                pool.wait_ge(tail_summed, done)
                                nc.gpsimd.tensor_tensor(total, total, halves[n], ALU.add).then_inc(tail_summed, 1)
                                done += 1

                cycle(pool, lambda: None, body, finish)

            @block.scalar
            def _(act):
                def load_q(i, p):
                    act.wait_ge(q_lo_ready, upto(i, p, 1, -1))
                    act.dma_start(q_st[:, p], qk_dram[:, 0, bass.ds(i * (2 * BT) + p * BT, BT)]).then_inc(q_in, 16)

                def split_q(i, p):
                    act.wait_ge(q_in, upto(i, p, 16, 16))
                    nc.scalar.copy(q_hi[:, p], q_st[:, p]).then_inc(q_hi_ready, 1)

                def split_v(g):
                    if g < NB - 1:
                        act.wait_ge(kv_in[g], 32)
                    nc.scalar.copy(v_hi[:, g * TT:(g + 1) * TT], v_all[:, g * TT:(g + 1) * TT]).then_inc(v_hi_ready, 1)

                def max_row(i, p):
                    act.wait_ge(neg_mm, upto(i, p, 1, 1))
                    nc.scalar.copy(neg_row[:, p], ps[0:1, NEG_BANK, :]).then_inc(neg_row_ready, 1)

                def start():
                    split_q(0, 1)
                    split_v(0)
                    split_v(1)
                    max_row(0, 0)
                    for n in range(2):
                        act.wait_ge(qk_out[n], 16 * NB * TT // 2)
                        act.wait_ge(v_out[n], 16 * (NB - 1) * TT // 2)

                def body(i, p, first, last):
                    more = not last and not (isinstance(i, int) and i == NB // 2 - 1)
                    for j in range(NT):
                        if more and j == PB:
                            load_q(i + 1, p)
                        if first and j % 2 == 1 and j // 2 < NB - 2:
                            split_v(j // 2 + 2)
                        if first and j == O_FROM:
                            act.wait_ge(o_in, 16)
                        if first and O_FROM <= j < O_FROM + E // 2:
                            pair = slice(2 * (j - O_FROM), 2 * (j - O_FROM) + 2)
                            nc.scalar.copy(o_hi[:, pair], o_stage[:, pair]).then_inc(o_hi_ready, 1)
                        if not last and j == MAX_DONE + 2:
                            max_row(*following(i, p))
                        act.wait_ge(s_mm, upto(i, p, NT, j + 1))
                        wait(act, p_summed, upto(i, p, NT, last_user(j)))
                        wait(act, p_lo_ready, upto(i, p, NT, last_user(j)))
                        wait(act, pv_mm, upto(i, p, NT, last_user(j)))
                        buf = j % PB
                        nc.scalar.activation(pf[:, buf], ps[:, S_BANK + j % 2, :], ACT.Exp, scale=SCALE
                                             ).then_inc(pf_ready, 1)
                        nc.scalar.activation(p_hi[:, buf], ps[:, S_BANK + j % 2, :], ACT.Exp, scale=SCALE
                                             ).then_inc(p_hi_ready, 1)
                    if more:
                        split_q(i + 1, p)
                    act.wait_ge(pv_mm, upto(i, p, NT, NT))
                    wait(act, o_mm, upto(i, p, NT, -NT))
                    nc.scalar.copy(ot_hi[:, p], ps[:, O_BANK + p, :]).then_inc(ot_hi_ready, 1)

                def finish():
                    act.wait_ge(w_out_ready, NB)
                    act.wait_ge(p_summed, NB * NT)
                    act.wait_ge(p_lo_ready, NB * NT)
                    for j in range(NT):
                        if not by_act(j):
                            continue
                        t, a = j // PAIRS, n_act(j)
                        act.wait_ge(o_mm, (NB - 1) * NT + j + 1)
                        if a >= PB:
                            before_it = a - PB + 1
                            act.wait_ge(tail_summed, 2 * before_it - (before_it + len(ACT_PAIRS) - 1) // len(ACT_PAIRS))
                        for n in range(2):
                            e = 2 * (j % PAIRS) + n
                            ins = nc.scalar.mul(pf[:, a % PB, n * C:(n + 1) * C],
                                                ps[:, TAIL_BANKS[j % len(TAIL_BANKS)], n * C:(n + 1) * C],
                                                w_out_s[:, 1, t, e:e + 1])
                        ins.then_inc(tail_scaled, 1)

                cycle(act, start, body, finish)

            @block.vector
            def _(dve):
                def split_q(i, p):
                    dve.wait_ge(q_hi_ready, upto(i, p, 1, 1))
                    nc.vector.tensor_tensor(q_lo[:, p], q_st[:, p], q_hi[:, p].bitcast(F32), ALU.subtract
                                            ).then_inc(q_lo_ready, 1)

                def low_k(g):
                    dve.wait_ge(k_hi_ready, g + 1)
                    keys = slice(g * BT, (g + 1) * BT)
                    nc.vector.tensor_tensor(k_lo[:, keys], k_t[:, keys], k_hi[:, keys].bitcast(F32), ALU.subtract
                                            ).then_inc(k_lo_ready, 1)

                def low_v(g):
                    dve.wait_ge(v_hi_ready, g + 1)
                    keys = slice(g * TT, (g + 1) * TT)
                    nc.vector.tensor_tensor(v_lo[:, keys], v_all[:, keys], v_hi[:, keys].bitcast(F32), ALU.subtract
                                            ).then_inc(v_lo_ready, 1)

                def low_o(n):
                    dve.wait_ge(o_hi_ready, n + 1)
                    pair = slice(2 * n, 2 * n + 2)
                    nc.vector.tensor_tensor(o_lo[:, pair], o_stage[:, pair], o_hi[:, pair].bitcast(F32), ALU.subtract
                                            ).then_inc(o_lo_ready, 1)

                def max_piece(i, p, j):
                    dve.wait_ge(max_mm, upto(i, p, NT, j + 1))
                    t, g = divmod(j, KG)
                    nc.vector.tensor_reduce(mx[:, t, g:g + 1], ps[:, MAX_BANKS[j % 2], :], AX_X, ALU.max
                                            ).then_inc(max_red, 1)

                def max_all(i, p):
                    dve.wait_ge(max_red, upto(i, p, NT, NT))
                    wait(dve, neg_mm, upto(i, p, 1, 0))
                    nc.vector.tensor_reduce(neg_max[:], mx[:], AX_X, ALU.max, negate=True).then_inc(neg_max_ready, 1)

                def start():
                    split_q(0, 0)
                    low_k(0)
                    for t in range(TT):
                        dve.wait_ge(max_mm, NT - TT + t + 1)
                        nc.vector.tensor_reduce(mx[:, t, KG - 1:KG], ps[:, MAX_BANK + t, :], AX_X, ALU.max
                                                ).then_inc(max_red, 1)
                    max_all(0, 0)
                    low_v(0)

                def low_part(i, p, j):
                    dve.wait_ge(p_hi_ready, upto(i, p, NT, j + 1))
                    wait(dve, pv_mm, upto(i, p, NT, last_user(j)))
                    nc.vector.tensor_tensor(p_lo[:, j % PB], pf[:, j % PB], p_hi[:, j % PB].bitcast(F32),
                                            ALU.subtract).then_inc(p_lo_ready, 1)

                def accumulate(i, p, j):
                    t, pair = divmod(j, PAIRS)
                    dve.wait_ge(o_mm, upto(i, p, NT, j + 1))
                    for n in range(2):
                        e = 2 * pair + n
                        src, w = ps[:, Y_BANK + j % 2, n * C:(n + 1) * C], w_out_s[:, p, t, e:e + 1]
                        if e == 0:
                            wait(dve, yo_ready, upto(i, p, TT, t - 1))
                            nc.vector.tensor_scalar(y[:, t % 2], src, w, None, ALU.mult).then_inc(y_acc, 1)
                        else:
                            dve.wait_ge(y_acc, upto(i, p, TT * E, t * E + e))
                            nc.vector.scalar_tensor_tensor(out=y[:, t % 2], in0=src, scalar=w, in1=y[:, t % 2],
                                                           op0=ALU.mult, op1=ALU.add).then_inc(y_acc, 1)

                def low_output(i, p):
                    dve.wait_ge(ot_hi_ready, upto(i, p, 1, 1))
                    nc.vector.tensor_tensor(ot_lo[:, p], ps[:, O_BANK + p, :], ot_hi[:, p].bitcast(F32),
                                            ALU.subtract).then_inc(ot_lo_ready, 1)

                def softmax_sums(i, p):
                    dve.wait_ge(sum_mm, upto(i, p, 1, 1))
                    nc.vector.reciprocal(inv_sum[:, :, 0], ps[:, SUM_BANK, 0:TT]).then_inc(inv_sum_ready, 1)
                    dve.wait_ge(inv_sum_ready, upto(i, p, 1, 1))
                    nc.vector.tensor_tensor(w_out_s[:, p], w_all[:, tiles(i, p, 0, TT), :],
                                            inv_sum[:].to_broadcast([P, TT, E]), ALU.mult).then_inc(w_out_ready, 1)
                    dve.wait_ge(w_out_ready, upto(i, p, 1, 1))

                def body(i, p, first, last):
                    for j in range(NT + LAG):
                        if first and j // 2 < NB - 1:
                            (low_v if j % 2 else low_k)(j // 2 + 1)
                        if first and O_FROM < j <= O_FROM + E // 2:
                            low_o(j - O_FROM - 1)
                        if 1 <= j <= NT:
                            low_part(i, p, j - 1)
                        if not last and j < NT:
                            for n in MAX_AT[j]:
                                max_piece(*following(i, p), n)
                            if j == MAX_DONE:
                                max_all(*following(i, p))
                            if j == MAX_DONE + 1:
                                split_q(*following(i, p))
                        if not first:
                            if j == 0:
                                low_output(*before(i, p))
                            if j == 1:
                                softmax_sums(*before(i, p))
                            if j >= LAG:
                                accumulate(*before(i, p), j - LAG)

                def finish():
                    i, p = NB // 2 - 1, 1
                    low_output(i, p)
                    softmax_sums(i, p)
                    chain = 0

                    def join(t, chain):
                        dve.wait_ge(tail_summed, (t + 1) * ADDS)
                        dve.wait_ge(tail_acc, chain)
                        nc.vector.tensor_tensor(y[:, t % 2], y[:, t % 2], act_part[:, t % 2], ALU.add
                                                ).then_inc(tail_joined, 1)
                        dve.wait_ge(tail_joined, t + 1)
                        dve.wait_ge(out_done[t % 2], 16 * ((NT - TT + t) // 2))
                        nc.vector.tensor_tensor(yo[:, t % 2], y[:, t % 2], modv[:, 5], ALU.mult).then_inc(yo_scaled, 1)
                        if t == 0:
                            dve.wait_ge(x2_in, 16 * NB)
                        dve.wait_ge(yo_scaled, NT - TT + t + 1)
                        nc.vector.tensor_tensor(yo[:, t % 2], yo[:, t % 2], x2b[:, t], ALU.add).then_inc(yo_ready, 1)

                    for j in range(NT):
                        if by_act(j):
                            continue
                        t, pair = divmod(j, PAIRS)
                        dve.wait_ge(o_mm, (NB - 1) * NT + j + 1)
                        for n in range(2):
                            e = 2 * pair + n
                            src = ps[:, TAIL_BANKS[j % len(TAIL_BANKS)], n * C:(n + 1) * C]
                            w = w_out_s[:, 1, t, e:e + 1]
                            if e == 0:
                                if t < 2:
                                    dve.wait_ge(yo_ready, NT - TT)
                                else:
                                    dve.wait_ge(yo_scaled, NT - TT + t - 1)
                                nc.vector.tensor_scalar(y[:, t % 2], src, w, None, ALU.mult).then_inc(tail_acc, 1)
                            else:
                                dve.wait_ge(tail_acc, chain)
                                nc.vector.scalar_tensor_tensor(out=y[:, t % 2], in0=src, scalar=w, in1=y[:, t % 2],
                                                               op0=ALU.mult, op1=ALU.add).then_inc(tail_acc, 1)
                            chain += 1
                        if pair == 2 and t:
                            join(t - 1, chain)
                    join(TT - 1, chain)

                cycle(dve, start, body, finish)

            @block.tensor
            def _(pe):
                def max_piece(i, p, j):
                    t, g = divmod(j, KG)
                    if j == 0:
                        pe.wait_ge(q_hi_ready, upto(i, p, 1, 1))
                    wait(pe, max_red, upto(i, p, NT, j - 1))
                    nc.tensor.matmul(ps[:, MAX_BANKS[j % 2], :], q_hi[:, p, t * P:(t + 1) * P], k_hi[:, g * BT:(g + 1) * BT],
                                     start=True, stop=True).then_inc(max_mm, 1)

                def max_transposes(i, p):
                    pe.wait_ge(neg_max_ready, upto(i, p, 1, 1))
                    wait(pe, neg_row_ready, upto(i, p, 1, 0))
                    for t in range(TT):
                        ins = nc.tensor.transpose(ps[0:1, NEG_BANK, t * P:(t + 1) * P], neg_max[:, t:t + 1], ident[:])
                    ins.then_inc(neg_mm, 1)

                def scores(i, p, j):
                    if j == 0:
                        pe.wait_ge(q_lo_ready, upto(i, p, 1, 1))
                        pe.wait_ge(neg_row_ready, upto(i, p, 1, 1))
                    wait(pe, p_hi_ready, upto(i, p, NT, j - 1))
                    keys, dst = slice(j * P, (j + 1) * P), ps[:, S_BANK + j % 2, :]
                    nc.tensor.matmul(dst, k_hi[:, keys], q_hi[:, p], start=True, stop=False)
                    nc.tensor.matmul(dst, k_hi[:, keys], q_lo[:, p], start=False, stop=False)
                    nc.tensor.matmul(dst, k_lo[:, keys], q_hi[:, p], start=False, stop=False)
                    nc.tensor.matmul(dst, ones_r[:], neg_row[:, p], start=False, stop=True).then_inc(s_mm, 1)

                def values(i, p, j):
                    if j == 0:
                        wait(pe, ot_lo_ready, upto(i, p, 1, -1))
                    pe.wait_ge(p_lo_ready, upto(i, p, NT, j + 1))
                    dst, buf = ps[:, O_BANK + p, :], j % PB
                    nc.tensor.matmul(dst, v_hi[:, j], p_hi[:, buf], start=(j == 0), stop=False)
                    nc.tensor.matmul(dst, v_lo[:, j], p_hi[:, buf], start=False, stop=False)
                    nc.tensor.matmul(dst, v_hi[:, j], p_lo[:, buf], start=False, stop=(j == NT - 1)).then_inc(pv_mm, 1)

                def sums(i, p):
                    pe.wait_ge(p_summed, upto(i, p, NT, NT))
                    wait(pe, y_acc, upto(i, p, TT * E, 0))
                    for t in range(TT):
                        ins = nc.tensor.matmul(ps[:, SUM_BANK, t:t + 1], p_sum[:, p, t * P:(t + 1) * P],
                                               ones_f[:, 0:1], start=True, stop=True)
                    ins.then_inc(sum_mm, 1)

                def project(i, p, j, tail=False):
                    t, pair = divmod(j, PAIRS)
                    if j == 0:
                        pe.wait_ge(ot_lo_ready, upto(i, p, 1, 1))
                        pe.wait_ge(inv_sum_ready, upto(i, p, 1, 1))
                    if tail:
                        held = j - len(TAIL_BANKS) + 1
                        if held > 0:
                            wait(pe, tail_acc, 2 * n_dve(held))
                            wait(pe, tail_scaled, n_act(held))
                        elif j < 2:
                            pe.wait_ge(y_acc, (NB - 1) * TT * E)
                    else:
                        wait(pe, y_acc, upto(i, p, TT * E, 2 * (j - 1)))
                    rows = slice(t * P, (t + 1) * P)
                    dst = ps[:, TAIL_BANKS[j % len(TAIL_BANKS)] if tail else Y_BANK + j % 2, :]
                    for n, (a, b) in enumerate(((ot_hi, o_hi), (ot_hi, o_lo), (ot_lo, o_hi))):
                        ins = nc.tensor.matmul(dst, a[:, p, rows],
                                               b[:, 2 * pair:2 * pair + 2].rearrange("p e c -> p (e c)"),
                                               start=(n == 0), stop=(n == 2))
                    ins.then_inc(o_mm, 1)

                def start():
                    pe.wait_ge(k_hi_ready, NB)
                    for t in range(TT):
                        nc.tensor.matmul(ps[:, MAX_BANK + t, :], q_hi[:, 0, t * P:(t + 1) * P], k_hi[:, N - BT:],
                                         start=True, stop=True).then_inc(max_mm, 1)
                    max_transposes(0, 0)

                def body(i, p, first, last):
                    for j in range(NT + LAG):
                        if first and j % TT == 0 and j < NT:
                            pe.wait_ge(k_lo_ready, j // TT + 1)
                        if first and j % TT == LAG:
                            pe.wait_ge(v_lo_ready, j // TT + 1)
                        if j < NT:
                            scores(i, p, j)
                        if not last and j < NT:
                            for n in MAX_AT[j]:
                                max_piece(*following(i, p), n)
                            if j == MAX_DONE + 1:
                                max_transposes(*following(i, p))
                        if not first and j == 1:
                            sums(*before(i, p))
                        if not first and j >= LAG:
                            project(*before(i, p), j - LAG)
                        if j >= LAG:
                            values(i, p, j - LAG)
                    if first:
                        pe.wait_ge(o_lo_ready, E // 2)

                def finish():
                    sums(NB // 2 - 1, 1)
                    for j in range(NT):
                        project(NB // 2 - 1, 1, j, tail=True)

                cycle(pe, start, body, finish)


def kernel(**inputs):
    import numpy as np
    import concourse.bacc as bacc
    from concourse.bass_utils import run_bass_kernel_spmd

    a = {name[3:]: np.asarray(value) for name, value in inputs.items()}
    n, c = a["attn_x"].shape[1:]
    by_column = lambda v: v.reshape(-1, 128).T
    laid = {
        "x": a["attn_x"].reshape(n, c), "ln_w": by_column(a["attn_ln_w"]),
        "ln_b": by_column(a["attn_ln_b"]), "w_in": a["attn_W_in"],
        "conv_w": a["attn_conv_w"], "a_mat": a["attn_A"], "a_mat_t": a["attn_A"].T, "bm_t": a["attn_Bm"].T,
        "cm_t": a["attn_Cm"].T, "w_out": a["attn_W_out"], "sim": a["ffn_sim_matrix"], "gates": a["ffn_gates"],
        "q_proj": a["ffn_q_proj"], "k_proj": a["ffn_k_proj"], "v_proj": a["ffn_v_proj"],
        "o_proj": a["ffn_o_proj"], "cond": by_column(a["c"]), "wmod": a["wmod"],
    }
    nc = bacc.Bacc("TRN2", target_bir_lowering=False, num_devices=1)
    arrays, args = {}, []
    for name, value in laid.items():
        arrays["in_" + name] = np.ascontiguousarray(value)
        args.append(nc.dram_tensor("in_" + name, value.shape, mybir.dt.from_np(value.dtype), kind="ExternalInput").ap())
    out = nc.dram_tensor("out_x", (n, c), F32, kind="ExternalOutput").ap()
    adaln_block_kernel(nc, *args, out)
    r = run_bass_kernel_spmd(nc, [arrays], core_ids=[0])
    return r.results[0]["out_x"].reshape(1, n, c)
```
